# Optimizing a Trainium2 kernel written in Bass

```python
import numpy as np
import jax
import jax.numpy as jnp

def _softmax(x, axis=-1):
    return jax.nn.softmax(x, axis=axis)

def _gelu(x):
    return jax.nn.gelu(x, approximate=True)

def _silu(x):
    return jax.nn.silu(x)

def _sigmoid(x):
    return jax.nn.sigmoid(x)

def _layernorm(x, axis=-1, eps=1e-05):
    m = jnp.mean(x, axis=axis, keepdims=True)
    v = jnp.var(x, axis=axis, keepdims=True)
    return (x - m) / jnp.sqrt(v + eps)

def _scatter_add(tgt, idx, src, axis=0):
    return tgt.at[idx].add(src)

def _segment_sum(src, seg, n):
    return jax.ops.segment_sum(src, seg, n)
kernel_name = 'mk_gnn_ffn_d2_gnn_r8_30ad30'

def setup_inputs(seed: int=0):
    np.random.seed(seed)
    _w = jnp.asarray

    def _rec_inputs():
        import jax
        import jax.numpy as jnp
        _gk = jax.random.key(seed)
        x = -0.0003713 + 1 * jax.random.normal(jax.random.fold_in(_gk, 1), (6250, 256), jnp.float32)
        src = jax.random.randint(jax.random.fold_in(_gk, 2), (100000,), 0, 6250, jnp.int32)
        dst = jax.random.randint(jax.random.fold_in(_gk, 3), (100000,), 0, 6250, jnp.int32)
        _o = jnp.argsort(dst, stable=True)
        src = src[_o]
        dst = dst[_o]
        return (x, src, dst)
    x, src, dst = _rec_inputs()

    def _L0_gnn_setup():
        import jax, jax.numpy as jnp
        import numpy as np
        N = 6250
        E = 100000
        IN_F = 256
        OUT_F = 64
        NHEAD = 4
        ALPHA = 0.2

        def _gat_forward(x, W, a_l, a_r, edge):
            n = x.shape[0]
            row, col = (edge[0], edge[1])
            h = (x @ W).reshape(n, NHEAD, OUT_F)
            hl = jnp.sum(a_l * h, axis=-1)
            hr = jnp.sum(a_r * h, axis=-1)
            e = jax.nn.leaky_relu(hl[row] + hr[col], negative_slope=ALPHA)
            e_max = jax.ops.segment_max(e, row, num_segments=n)
            e_max = jnp.where(jnp.isfinite(e_max), e_max, 0.0)
            ee = jnp.exp(e - e_max[row])
            denom = jax.ops.segment_sum(ee, row, num_segments=n)
            att = ee / denom[row]
            msg = att[:, :, None] * h[col]
            out_h = jax.ops.segment_sum(msg, row, num_segments=n)
            return out_h.reshape(n, NHEAD * OUT_F)
        key = jax.random.key(seed)
        k1, k2, k3, k4, k5 = jax.random.split(key, 5)
        x = jax.random.normal(k1, (N, IN_F), dtype=jnp.float32)
        edge = jax.random.randint(k2, (2, E), 0, N, dtype=jnp.int32)
        stdv_W = float(np.sqrt(6.0 / (IN_F + OUT_F * NHEAD)))
        W = jax.random.uniform(k3, (IN_F, OUT_F * NHEAD), jnp.float32, -stdv_W, stdv_W)
        stdv_a = float(np.sqrt(6.0 / (NHEAD + OUT_F)))
        a_l = jax.random.uniform(k4, (1, NHEAD, OUT_F), jnp.float32, -stdv_a, stdv_a)
        a_r = jax.random.uniform(k5, (1, NHEAD, OUT_F), jnp.float32, -stdv_a, stdv_a)
        return {'x': x, 'edge': edge, 'W': W, 'a_l': a_l, 'a_r': a_r}
    _L0_gnn_all = _L0_gnn_setup()
    _L0_gnn_in = {k: v for k, v in _L0_gnn_all.items() if k in ('W', 'a_l', 'a_r')}
    del _L0_gnn_all

    def _L0_ffn_setup():
        import math
        import jax, jax.numpy as jnp
        import numpy as np
        CAPACITY_FACTOR = 1.25
        TOP_K = 2
        LN_EPS = 1e-05

        def _layer_norm(x, gamma, beta):
            mu = jnp.mean(x, axis=-1, keepdims=True)
            var = jnp.var(x, axis=-1, keepdims=True)
            return (x - mu) * jax.lax.rsqrt(var + LN_EPS) * gamma + beta
        key = jax.random.key(seed)
        ks = jax.random.split(key, 4)
        B, S, D, F, E = (8, 512, 256, 512, 8)
        x = jax.random.normal(ks[0], (B, S, D), dtype=jnp.float32)
        Wr = jax.random.normal(ks[1], (D, E), dtype=jnp.float32) / np.sqrt(D)
        br = jnp.zeros((E,), jnp.float32)
        W1 = jax.random.normal(ks[2], (E, D, F), dtype=jnp.float32) / np.sqrt(D)
        b1 = jnp.zeros((E, F), jnp.float32)
        W2 = jax.random.normal(ks[3], (E, F, D), dtype=jnp.float32) / np.sqrt(F)
        b2 = jnp.zeros((E, D), jnp.float32)
        gamma = jnp.ones((D,), jnp.float32)
        beta = jnp.zeros((D,), jnp.float32)
        return {'x': x, 'Wr': Wr, 'br': br, 'W1': W1, 'b1': b1, 'W2': W2, 'b2': b2, 'gamma': gamma, 'beta': beta}
    _L0_ffn_all = _L0_ffn_setup()
    _L0_ffn_in = {k: v for k, v in _L0_ffn_all.items() if k in ('Wr', 'br', 'W1', 'b1', 'W2', 'b2', 'gamma', 'beta')}
    del _L0_ffn_all

    def _L1_gnn_setup():
        import jax, jax.numpy as jnp
        import numpy as np
        EPS = 1e-05

        def _gcn_conv(x, W, row, col, n_nodes):
            xl = x @ W.T
            ones = jnp.ones(row.shape[0], dtype=x.dtype)
            deg = jax.ops.segment_sum(ones, col, num_segments=n_nodes)
            dis = jnp.where(deg > 0, deg ** (-0.5), 0.0).astype(x.dtype)
            norm = dis[row] * dis[col]
            msg = xl[row] * norm[:, None]
            return jax.ops.segment_sum(msg, col, num_segments=n_nodes)

        def _batchnorm(x, gamma, beta):
            m = jnp.mean(x, axis=0)
            v = jnp.mean((x - m) ** 2, axis=0)
            return (x - m) * jax.lax.rsqrt(v + EPS) * gamma + beta
        key = jax.random.key(seed)
        k1, k2, k3, k4 = jax.random.split(key, 4)
        N, C, IC, E = (1250, 256, 512, 20000)
        x = jax.random.normal(k1, (N, C), dtype=jnp.float32)
        es = jax.random.randint(k2, (2, E), 0, N, dtype=jnp.int64)
        W1 = jax.random.normal(k3, (IC, C), dtype=jnp.float32) * (1.0 / np.sqrt(C))
        W2 = jax.random.normal(k4, (C, IC), dtype=jnp.float32) * (1.0 / np.sqrt(IC))
        g1 = jnp.ones((IC,), jnp.float32)
        b1 = jnp.zeros((IC,), jnp.float32)
        g2 = jnp.ones((C,), jnp.float32)
        b2 = jnp.zeros((C,), jnp.float32)
        return {'x': x, 'es': es, 'W1': W1, 'g1': g1, 'b1': b1, 'W2': W2, 'g2': g2, 'b2': b2}
    _L1_gnn_all = _L1_gnn_setup()
    _L1_gnn_in = {k: v for k, v in _L1_gnn_all.items() if k in ('W1', 'g1', 'b1', 'W2', 'g2', 'b2')}
    del _L1_gnn_all

    def _L1_ffn_setup():
        import math
        import jax, jax.numpy as jnp
        import numpy as np
        CAPACITY_FACTOR = 1.25
        key = jax.random.key(seed)
        ks = jax.random.split(key, 5)
        B, L, D, F, E = (8, 1024, 256, 1024, 8)
        h = jax.random.normal(ks[0], (B, L, D), dtype=jnp.float32)
        gate_w = jax.random.normal(ks[1], (D, E), dtype=jnp.float32) * 0.02
        gate_b = jnp.zeros((E,), dtype=jnp.float32)
        w1 = jax.random.normal(ks[2], (E, D, F), dtype=jnp.float32) * (1.0 / math.sqrt(D))
        b1 = jnp.zeros((E, F), dtype=jnp.float32)
        w2 = jax.random.normal(ks[3], (E, F, D), dtype=jnp.float32) * (1.0 / math.sqrt(F))
        b2 = jnp.zeros((E, D), dtype=jnp.float32)
        return {'h': h, 'gate_w': gate_w, 'gate_b': gate_b, 'w1': w1, 'b1': b1, 'w2': w2, 'b2': b2}
    _L1_ffn_all = _L1_ffn_setup()
    _L1_ffn_in = {k: v for k, v in _L1_ffn_all.items() if k in ('gate_w', 'gate_b', 'w1', 'b1', 'w2', 'b2')}
    del _L1_ffn_all
    return {'x': x, 'src': src, 'dst': dst, 'L0_gnn_W': _L0_gnn_in['W'], 'L0_gnn_a_l': _L0_gnn_in['a_l'], 'L0_gnn_a_r': _L0_gnn_in['a_r'], 'L0_ffn_Wr': _L0_ffn_in['Wr'], 'L0_ffn_br': _L0_ffn_in['br'], 'L0_ffn_W1': _L0_ffn_in['W1'], 'L0_ffn_b1': _L0_ffn_in['b1'], 'L0_ffn_W2': _L0_ffn_in['W2'], 'L0_ffn_b2': _L0_ffn_in['b2'], 'L0_ffn_gamma': _L0_ffn_in['gamma'], 'L0_ffn_beta': _L0_ffn_in['beta'], 'L1_gnn_W1': _L1_gnn_in['W1'], 'L1_gnn_g1': _L1_gnn_in['g1'], 'L1_gnn_b1': _L1_gnn_in['b1'], 'L1_gnn_W2': _L1_gnn_in['W2'], 'L1_gnn_g2': _L1_gnn_in['g2'], 'L1_gnn_b2': _L1_gnn_in['b2'], 'L1_ffn_gate_w': _L1_ffn_in['gate_w'], 'L1_ffn_gate_b': _L1_ffn_in['gate_b'], 'L1_ffn_w1': _L1_ffn_in['w1'], 'L1_ffn_b1': _L1_ffn_in['b1'], 'L1_ffn_w2': _L1_ffn_in['w2'], 'L1_ffn_b2': _L1_ffn_in['b2']}

def reference(x, src, dst, L0_gnn_W, L0_gnn_a_l, L0_gnn_a_r, L0_ffn_Wr, L0_ffn_br, L0_ffn_W1, L0_ffn_b1, L0_ffn_W2, L0_ffn_b2, L0_ffn_gamma, L0_ffn_beta, L1_gnn_W1, L1_gnn_g1, L1_gnn_b1, L1_gnn_W2, L1_gnn_g2, L1_gnn_b2, L1_ffn_gate_w, L1_ffn_gate_b, L1_ffn_w1, L1_ffn_b1, L1_ffn_w2, L1_ffn_b2):
    import jax
    import jax.numpy as jnp

    def _L0_gnn_ref(x, edge, W, a_l, a_r):
        import jax, jax.numpy as jnp
        import numpy as np
        N = 6250
        E = 100000
        IN_F = 256
        OUT_F = 64
        NHEAD = 4
        ALPHA = 0.2

        def _gat_forward(x, W, a_l, a_r, edge):
            n = x.shape[0]
            row, col = (edge[0], edge[1])
            h = (x @ W).reshape(n, NHEAD, OUT_F)
            hl = jnp.sum(a_l * h, axis=-1)
            hr = jnp.sum(a_r * h, axis=-1)
            e = jax.nn.leaky_relu(hl[row] + hr[col], negative_slope=ALPHA)
            e_max = jax.ops.segment_max(e, row, num_segments=n)
            e_max = jnp.where(jnp.isfinite(e_max), e_max, 0.0)
            ee = jnp.exp(e - e_max[row])
            denom = jax.ops.segment_sum(ee, row, num_segments=n)
            att = ee / denom[row]
            msg = att[:, :, None] * h[col]
            out_h = jax.ops.segment_sum(msg, row, num_segments=n)
            return out_h.reshape(n, NHEAD * OUT_F)
        return _gat_forward(x, W, a_l, a_r, edge)

    def _L0_ffn_ref(x, Wr, br, W1, b1, W2, b2, gamma, beta):
        import math
        import jax, jax.numpy as jnp
        import numpy as np
        CAPACITY_FACTOR = 1.25
        TOP_K = 2
        LN_EPS = 1e-05

        def _layer_norm(x, gamma, beta):
            mu = jnp.mean(x, axis=-1, keepdims=True)
            var = jnp.var(x, axis=-1, keepdims=True)
            return (x - mu) * jax.lax.rsqrt(var + LN_EPS) * gamma + beta
        B, S, D = x.shape
        E = Wr.shape[1]
        N = B * S
        K = TOP_K
        logits = jnp.mean(x, axis=1) @ Wr + br
        routing_weights = jax.nn.softmax(logits, axis=-1)
        capacity = float(math.ceil(N * CAPACITY_FACTOR / E))
        expected_loads = routing_weights.sum(axis=0) * (N / B)
        scale = jnp.where(expected_loads > capacity, capacity / expected_loads, 1.0)
        routing_weights = jax.nn.softmax(routing_weights * scale, axis=-1)
        rw_tok = jnp.broadcast_to(routing_weights[:, None, :], (B, S, E)).reshape(N, E)
        top_w, top_i = jax.lax.top_k(rw_tok, K)
        top_w = jax.nn.softmax(top_w, axis=-1)
        xf = x.reshape(N, D)
        h = jax.nn.gelu(jnp.einsum('nd,edf->enf', xf, W1) + b1[:, None, :], approximate=False)
        y = jnp.einsum('enf,efd->end', h, W2) + b2[:, None, :]
        w_dense = jnp.zeros((N, E), x.dtype).at[jnp.arange(N)[:, None], top_i].add(top_w)
        out = jnp.einsum('ne,end->nd', w_dense, y).reshape(B, S, D)
        out = _layer_norm(out + x, gamma, beta)
        return out

    def _L1_gnn_ref(x, es, W1, g1, b1, W2, g2, b2):
        import jax, jax.numpy as jnp
        import numpy as np
        EPS = 1e-05

        def _gcn_conv(x, W, row, col, n_nodes):
            xl = x @ W.T
            ones = jnp.ones(row.shape[0], dtype=x.dtype)
            deg = jax.ops.segment_sum(ones, col, num_segments=n_nodes)
            dis = jnp.where(deg > 0, deg ** (-0.5), 0.0).astype(x.dtype)
            norm = dis[row] * dis[col]
            msg = xl[row] * norm[:, None]
            return jax.ops.segment_sum(msg, col, num_segments=n_nodes)

        def _batchnorm(x, gamma, beta):
            m = jnp.mean(x, axis=0)
            v = jnp.mean((x - m) ** 2, axis=0)
            return (x - m) * jax.lax.rsqrt(v + EPS) * gamma + beta
        n_nodes = x.shape[0]
        loops = jnp.arange(n_nodes, dtype=es.dtype)
        row = jnp.concatenate([es[0], loops])
        col = jnp.concatenate([es[1], loops])
        res = x
        h = _gcn_conv(x, W1, row, col, n_nodes)
        h = jax.nn.relu(_batchnorm(h, g1, b1))
        h = _gcn_conv(h, W2, row, col, n_nodes)
        h = _batchnorm(h, g2, b2)
        return jax.nn.relu(h + res)

    def _L1_ffn_ref(h, gate_w, gate_b, w1, b1, w2, b2):
        import math
        import jax, jax.numpy as jnp
        import numpy as np
        CAPACITY_FACTOR = 1.25
        B, L, D = h.shape
        E = gate_w.shape[1]
        T = B * L
        C = max(1, math.ceil(CAPACITY_FACTOR * T / E))
        x = h.reshape(T, D)
        logits = x @ gate_w + gate_b
        probs = jax.nn.softmax(logits, axis=-1)
        idx = jnp.argmax(probs, axis=-1)
        prb = jnp.take_along_axis(probs, idx[:, None], axis=1)[:, 0]
        one_hot = jax.nn.one_hot(idx, E, dtype=jnp.float32)
        pos = (jnp.cumsum(one_hot, axis=0) * one_hot).sum(-1).astype(jnp.int32) - 1
        kept = pos < C
        pos_safe = jnp.where(kept, pos, C)
        buf = jnp.zeros((E, C, D), dtype=h.dtype).at[idx, pos_safe].set(x, mode='drop')
        hmid = jax.nn.relu(jnp.einsum('ecd,edf->ecf', buf, w1) + b1[:, None, :])
        ybuf = jnp.einsum('ecf,efd->ecd', hmid, w2) + b2[:, None, :]
        pos_g = jnp.minimum(pos, C - 1)
        y_tok = ybuf[idx, pos_g] * (prb * kept)[:, None]
        y = y_tok.reshape(B, L, D)
        y = jnp.nan_to_num(y, nan=0.0, posinf=10000.0, neginf=-10000.0)
        return y
    edge_index = jnp.stack([src, dst])
    x = x + _L0_gnn_ref(_layernorm(x, axis=-1), edge_index, L0_gnn_W, L0_gnn_a_l, L0_gnn_a_r)
    x = x + _L0_ffn_ref(_layernorm(x, axis=-1)[None], L0_ffn_Wr, L0_ffn_br, L0_ffn_W1, L0_ffn_b1, L0_ffn_W2, L0_ffn_b2, L0_ffn_gamma, L0_ffn_beta)[0]
    x = x + _L1_gnn_ref(_layernorm(x, axis=-1), edge_index, L1_gnn_W1, L1_gnn_g1, L1_gnn_b1, L1_gnn_W2, L1_gnn_g2, L1_gnn_b2)
    x = x + _L1_ffn_ref(_layernorm(x, axis=-1)[None], L1_ffn_gate_w, L1_ffn_gate_b, L1_ffn_w1, L1_ffn_b1, L1_ffn_w2, L1_ffn_b2)[0]
    return x

_drawn_inputs = setup_inputs


def setup_inputs(seed=0):
    import zlib

    import numpy as np

    out = dict(_drawn_inputs(seed))
    spreads = {'L0_ffn_br': (0.0, 2.0),
     'L0_ffn_b1': (0.0, 0.36),
     'L0_ffn_b2': (0.0, 0.1),
     'L0_ffn_gamma': (1.0, 0.2),
     'L0_ffn_beta': (0.0, 0.1),
     'L1_gnn_g1': (1.0, 0.2),
     'L1_gnn_b1': (0.0, 0.33),
     'L1_gnn_g2': (1.0, 0.2),
     'L1_gnn_b2': (0.0, 0.1),
     'L1_ffn_gate_b': (0.0, 0.312),
     'L1_ffn_b1': (0.0, 0.8),
     'L1_ffn_b2': (0.0, 0.8)}
    factors = {'L0_ffn_Wr': 64.0}
    for name, (base, spread) in spreads.items():
        noise = np.random.default_rng([zlib.crc32(name.encode()), seed]).standard_normal(out[name].shape)
        drawn = base * np.exp(spread * noise) if base else spread * noise
        out[name] = jnp.asarray(drawn.astype(out[name].dtype))
    for name, factor in factors.items():
        out[name] = (out[name] * factor).astype(out[name].dtype)
    return out
```

```python
from contextlib import ExitStack

import concourse.bass as bass
from concourse import mybir

ALU = mybir.AluOpType
ACT = mybir.ActivationFunctionType
AX = mybir.AxisListType
F32 = mybir.dt.float32
F16 = mybir.dt.float16
I32 = mybir.dt.int32

P = 128
N = 6250
D = 256
TILES = 49
NP = TILES * P
PADS = NP - N
UNROLL = 7
GROUPS = TILES // UNROLL
E = 100000
EP, EC = 125, 800
ET = 832
HALF = ET // 2
RING = 8
HEADS, HD = 4, 64
ZROW = NP - 1
LOW = -3.0e38
F0, X0 = 512, 8
F1, X1 = 1024, 8
CAP0 = 977.0
CAP = 977
IC = 512
SLOTS = 1024
EPS = 1e-5
assert E == EP * EC and (E + TILES * (P - 1)) // P < ET


class Ctx:
    pass


def groups(eng, body):
    with eng.Fori(0, GROUPS // 2) as i:
        body(2 * i, 0, i)
        body(2 * i + 1, 1, i)
    body(GROUPS - 1, 0, GROUPS // 2)


def rows(dram, g, width):
    return dram[bass.ds(g * (UNROLL * P), UNROLL * P), 0:width].rearrange("(k p) d -> p k d", p=P)


def setup(nc, c, ctx, x):
    sb = lambda name, shape, dt: ctx.enter_context(nc.sbuf_tensor(name, shape, dt))
    c.iota = sb("iota", [P, ET], F32)
    c.iota16 = sb("iota16", [P, ET], F16)
    c.pidx = sb("pidx", [P, 1], F32)
    c.ident = sb("ident", [P, P], F32)
    c.ones = sb("ones", [P, P], F32)
    c.below = sb("below", [P, P], F32)
    c.upto = sb("upto", [P, P], F32)
    c.zeros = sb("zeros", [P, EC], F32)
    c.zeros16 = sb("zeros16", [P, HALF], F16)
    c.neghalf = sb("neghalf", [P, UNROLL], F32)
    c.valid = sb("valid", [P, 1], F32)
    c.headsel = sb("headsel", [4, HEADS, P], F32)
    made = nc_sem(nc, c, "consts_made")
    copied = nc_sem(nc, c, "x_copied")
    with nc.Block() as block:
        @block.gpsimd
        def _(pool):
            nc.gpsimd.iota(c.iota[:, :], [[1, ET]], base=0, channel_multiplier=0,
                           allow_small_or_imprecise_dtypes=True).then_inc(made, 1)
            nc.gpsimd.iota(c.iota16[:, :], [[1, ET]], base=0, channel_multiplier=0,
                           allow_small_or_imprecise_dtypes=True).then_inc(made, 1)
            nc.gpsimd.iota(c.pidx[:, :], [[1, 1]], base=0, channel_multiplier=1,
                           allow_small_or_imprecise_dtypes=True).then_inc(made, 1)
            nc.gpsimd.memset(c.neghalf[:, :], -0.5).then_inc(made, 1)
            nc.gpsimd.memset(c.ones[:, :], 1.0).then_inc(made, 1)
            nc.gpsimd.memset(c.zeros[:, :], 0.0).then_inc(made, 1)
            nc.gpsimd.memset(c.zeros16[:, :], 0.0).then_inc(made, 1)

        @block.vector
        def _(dve):
            dve.wait_ge(made, 7)
            dve.tensor_scalar(c.ident[:, :], c.iota[:, 0:P], c.pidx[:, 0:1], None, ALU.is_equal)
            dve.tensor_scalar(c.valid[:, :], c.pidx[:, :], float(P - PADS), None, ALU.is_lt)
            dve.tensor_scalar(c.below[:, :], c.iota[:, 0:P], c.pidx[:, 0:1], None, ALU.is_gt)
            dve.tensor_scalar(c.upto[:, :], c.iota[:, 0:P], c.pidx[:, 0:1], None, ALU.is_ge)
            for h in range(HEADS):
                dve.tensor_scalar(c.headsel[:, h, :], c.ones[0:4, :], c.pidx[0:4, 0:1], float(h), ALU.mult,
                                  ALU.is_equal)

        @block.sync
        def _(sp):
            sp.dma_start(c.x0[0:N, :], x[:, :]).then_inc(copied, 16)
            sp.wait_ge(made, 7)
            sp.dma_start(c.x0[N:NP, :], c.zeros[0:PADS, 0:D]).then_inc(copied, 16)
            sp.dma_start(c.slots_in[0:X1 * SLOTS, :].rearrange("(p r) d -> p r d", p=P),
                         c.zeros[:, 0:D].unsqueeze(1).broadcast_to([P, X1 * SLOTS // P, D])).then_inc(copied, 16)
            sp.wait_ge(copied, 48)


def nc_sem(nc, c, name):
    c.sems.append(nc.alloc_semaphore(name=f"{c.phase}_{name}"))
    return c.sems[-1]


def recycle(nc, c):
    nc.clear_and_free_semaphores(c.sems)
    nc.all_engine_barrier()
    c.sems = []


def sort_edges(nc, c, key, other, idx, local, bucket_of, degree, tag):
    c.phase = tag
    sem = lambda name: nc_sem(nc, c, name)
    loaded, split, counted, summed, based, ended, table, placed = (
        sem(s) for s in "loaded split counted summed based ended table placed".split())
    masked, scanned, picked = (sem(s) for s in "masked scanned picked".split())
    onehot, spread, unpacked, zeroed = (sem(s) for s in "onehot spread unpacked zeroed".split())
    U = 4
    with ExitStack() as ctx:
        sb = lambda name, shape, dt: ctx.enter_context(nc.sbuf_tensor(f"{tag}_{name}", shape, dt))
        ps = lambda name, shape: ctx.enter_context(nc.psum_tensor(f"{tag}_{name}", shape, F32))
        key_i, oth_i, tmp_i = (sb(n, [EP, EC], I32) for n in ("key_i", "oth_i", "tmp_i"))
        hi, lo, pay1, pay2 = (sb(n, [EP, EC], F32) for n in ("hi", "lo", "pay1", "pay2"))
        mask, cum, pos, hit = (sb(n, [EP, EC], F32) for n in ("mask", "cum", "pos", "hit"))
        plo, ptile = sb("plo", [EP, EC], F32), sb("ptile", [EP, EC], F32)
        tot = sb("tot", [EP, TILES], F32)
        small_i = sb("small_i", [P, 2, TILES], I32)
        nt, inc, off = (sb(n, [P, TILES], F32) for n in ("nt", "inc", "off"))
        col_i, col_f, endc = sb("col_i", [TILES, 2], I32), sb("col_f", [TILES, 1], F32), sb("endc", [TILES, 1], F32)
        ge = sb("ge", [TILES, ET], F32)
        l1, l2 = sb("l1", [EP, U, P], F16), sb("l2", [EP, U, P], F16)
        hot = sb("hot", [EP, U, ET], F16)
        dlo, dhi = sb("dlo", [EP, U, P], F16), sb("dhi", [EP, U, TILES], F16)
        u1, u2, u3 = (sb(n, [P, ET], I32) for n in ("u1", "u2", "u3"))
        acc1, acc2 = ps("acc1", [P, 2, 512]), ps("acc2", [P, 2, 512])
        psd, pss = ps("psd", [P, 512]), ps("pss", [P, 512])
        block = ctx.enter_context(nc.Block())

        @block.sync
        def _(sp):
            sp.dma_start(key_i[:, :], key.rearrange("(p c) -> p c", p=EP)).then_inc(loaded, 16)
            sp.dma_start(oth_i[:, :], other.rearrange("(p c) -> p c", p=EP)).then_inc(loaded, 16)

        @block.vector
        def _(dve):
            n = [0]

            def step(ins):
                ins.then_inc(split, 1)
                n[0] += 1
                dve.wait_ge(split, n[0])

            dve.wait_ge(loaded, 32)
            step(dve.tensor_scalar(tmp_i[:, :], key_i[:, :], 7, None, ALU.arith_shift_right))
            step(dve.tensor_copy(hi[:, :], tmp_i[:, :]))
            step(dve.tensor_scalar(key_i[:, :], key_i[:, :], 127, None, ALU.bitwise_and))
            step(dve.tensor_copy(lo[:, :], key_i[:, :]))
            step(dve.tensor_scalar(oth_i[:, :], oth_i[:, :], -1.0, float(ZROW), ALU.mult, ALU.add))
            step(dve.tensor_scalar(tmp_i[:, :], oth_i[:, :], 7, None, ALU.bitwise_and))
            step(dve.tensor_scalar(oth_i[:, :], oth_i[:, :], 3, None, ALU.arith_shift_right))
            step(dve.tensor_copy(pay2[:, :], oth_i[:, :]))
            step(dve.tensor_scalar(hit[:, :], lo[:, :], 8.0, 8.0, ALU.mult, ALU.add))
            step(dve.tensor_tensor(pay1[:, :], hit[:, :], tmp_i[:, :], ALU.add))
            with dve.Fori(0, TILES) as b:
                dve.tensor_scalar(mask[:, :], hi[:, :], c.iota[0:EP, bass.ds(b, 1)], 0.0, ALU.is_equal, ALU.add,
                                  accum_out=tot[:, bass.ds(b, 1)]).then_inc(counted, 1)
                dve.wait_ge(counted, b + 1)
            dve.wait_ge(summed, 1)
            step(dve.tensor_scalar(small_i[:, 0, :], pss[:, 64:64 + TILES], 127.0, None, ALU.add))
            step(dve.tensor_scalar(small_i[:, 1, :], small_i[:, 0, :], 7, None, ALU.arith_shift_right))
            step(dve.tensor_copy(nt[:, :], small_i[:, 1, :]))
            step(dve.tensor_tensor_scan(inc[:, :], nt[:, :], c.zeros[:, 0:TILES], 0.0, ALU.add, ALU.add))
            step(dve.tensor_tensor(inc[:, :], inc[:, :], nt[:, :], ALU.subtract))
            step(dve.tensor_scalar(inc[:, :], inc[:, :], 128.0, -1.0, ALU.mult, ALU.add))
            step(dve.tensor_tensor(off[0:EP, :], inc[0:EP, :], pss[0:EP, 0:TILES], ALU.add))
            step(dve.tensor_scalar(col_i[:, 0:1], pss[0:TILES, 128:129], 127.0, None, ALU.add))
            step(dve.tensor_scalar(col_i[:, 1:2], col_i[:, 0:1], 7, None, ALU.arith_shift_right))
            dve.tensor_copy(col_f[:, :], col_i[:, 1:2]).then_inc(based, 1)
            dve.wait_ge(ended, 1)
            step(dve.tensor_copy(endc[:, :], pss[0:TILES, 192:193]))
            dve.tensor_scalar(ge[:, :], c.iota[0:TILES, :], endc[:, 0:1], None, ALU.is_ge).then_inc(based, 1)
            dve.wait_ge(table, 1)
            step(dve.tensor_copy(bucket_of[0:1, :].rearrange("p (a b) -> p a b", a=2), acc1[0:1, :, 0:HALF]))
            step(dve.memset(pos[:, :], 0.0))
            with dve.Fori(0, TILES) as b:
                dve.tensor_scalar(mask[:, :], hi[:, :], c.iota[0:EP, bass.ds(b, 1)], None,
                                  ALU.is_equal).then_inc(masked, 1)
                dve.wait_ge(masked, b + 1)
                dve.tensor_tensor_scan(cum[:, :], mask[:, :], c.zeros[0:EP, :], off[0:EP, bass.ds(b, 1)],
                                       ALU.add, ALU.add).then_inc(scanned, 1)
                dve.wait_ge(scanned, b + 1)
                dve.tensor_tensor(hit[:, :], mask[:, :], cum[:, :], ALU.mult).then_inc(picked, 1)
                dve.wait_ge(picked, 2 * b + 1)
                dve.tensor_tensor(pos[:, :], pos[:, :], hit[:, :], ALU.add).then_inc(picked, 1)
                dve.wait_ge(picked, 2 * b + 2)
            step(dve.tensor_copy(tmp_i[:, :], pos[:, :]))
            step(dve.tensor_scalar(key_i[:, :], tmp_i[:, :], 127, None, ALU.bitwise_and))
            step(dve.tensor_copy(plo[:, :], key_i[:, :]))
            step(dve.tensor_scalar(key_i[:, :], tmp_i[:, :], 7, None, ALU.arith_shift_right))
            step(dve.tensor_copy(ptile[:, :], key_i[:, :]))
            with dve.Fori(0, EC // U) as i:
                for k in range(U):
                    t = i * U + k
                    dve.wait_ge(spread, t + 1)
                    dve.tensor_scalar(hot[:, k, :], c.iota16[0:EP, :], ptile[:, bass.ds(t, 1)], None, ALU.is_equal)
                    dve.tensor_scalar(l1[:, k, :], c.iota16[0:EP, 0:P], plo[:, bass.ds(t, 1)],
                                      pay1[:, bass.ds(t, 1)], ALU.is_equal, ALU.mult)
                    last = dve.tensor_scalar(l2[:, k, :], c.iota16[0:EP, 0:P], plo[:, bass.ds(t, 1)],
                                             pay2[:, bass.ds(t, 1)], ALU.is_equal, ALU.mult)
                    if degree is not None:
                        dve.tensor_scalar(dlo[:, k, :], c.iota16[0:EP, 0:P], lo[:, bass.ds(t, 1)], None, ALU.is_equal)
                        last = dve.tensor_scalar(dhi[:, k, :], c.iota16[0:EP, 0:TILES], hi[:, bass.ds(t, 1)], None,
                                                 ALU.is_equal)
                    last.then_inc(onehot, 1)
            dve.wait_ge(placed, 1)
            view = lambda t: t[:, :].rearrange("p (a b) -> p a b", a=2)
            step(dve.tensor_copy(view(u1), acc1[:, :, 0:HALF]))
            step(dve.tensor_scalar(u2[:, :], u1[:, :], 3, None, ALU.arith_shift_right))
            step(dve.tensor_scalar(local[:, :], u2[:, :], -1.0, None, ALU.add))
            step(dve.tensor_scalar(u2[:, :], u1[:, :], 7, None, ALU.bitwise_and))
            step(dve.tensor_scalar(view(u3), acc2[:, :, 0:HALF], -8.0, float(ZROW), ALU.mult, ALU.add))
            step(dve.tensor_tensor(idx[:, :], u3[:, :], u2[:, :], ALU.subtract))
            if degree is not None:
                step(dve.tensor_copy(degree[:, :], psd[:, 0:TILES]))

        @block.tensor
        def _(pe):
            pe.wait_ge(counted, TILES)
            pe.matmul(pss[0:EP, 0:TILES], c.below[0:EP, 0:EP], tot[:, :], start=True, stop=True)
            pe.matmul(pss[:, 64:64 + TILES], c.ones[0:EP, :], tot[:, :], start=True, stop=True)
            pe.matmul(pss[0:TILES, 128:129], tot[:, :], c.ones[0:EP, 0:1], start=True, stop=True).then_inc(summed, 1)
            pe.wait_ge(based, 1)
            pe.matmul(pss[0:TILES, 192:193], c.upto[0:TILES, 0:TILES], col_f[:, :], start=True,
                      stop=True).then_inc(ended, 1)
            pe.wait_ge(based, 2)
            for a in range(2):
                last = pe.matmul(acc1[:, a, 0:HALF], c.ones[0:TILES - 1, :], ge[0:TILES - 1, a * HALF:(a + 1) * HALF],
                                 start=True, stop=True)
            last.then_inc(table, 1)
            pe.sem_inc(spread, U)
            pe.wait_ge(onehot, 1)
            for acc in (acc1, acc2):
                for a in range(2):
                    pe.matmul(acc[:, a, 0:HALF], c.zeros16[:, 0:P], c.zeros16[:, :], start=True, stop=False)
            pe.matmul(psd[:, 0:TILES], c.zeros16[:, 0:P], c.zeros16[:, 0:TILES], start=True, stop=False)
            with pe.Fori(0, EC // U) as i:
                for k in range(U):
                    pe.wait_ge(onehot, i * U + k + 1)
                    for acc, l in ((acc1, l1), (acc2, l2)):
                        for a in range(2):
                            last = pe.matmul(acc[:, a, 0:HALF], l[:, k, :], hot[:, k, a * HALF:(a + 1) * HALF],
                                             start=False, stop=False)
                    if degree is not None:
                        last = pe.matmul(psd[:, 0:TILES], dlo[:, k, :], dhi[:, k, :], start=False, stop=False)
                    last.then_inc(spread, 1)
            for acc in (acc1, acc2):
                for a in range(2):
                    pe.matmul(acc[:, a, 0:HALF], c.zeros16[:, 0:P], c.zeros16[:, :], start=False, stop=True)
            pe.matmul(psd[:, 0:TILES], c.zeros16[:, 0:P], c.zeros16[:, 0:TILES], start=False,
                      stop=True).then_inc(placed, 1)


def normalise(dve, sem, rooted, g, x, out, st, mean, rstd, var, done=0):
    tmp = var
    n = [0]

    def step(ins):
        ins.then_inc(sem, 1)
        n[0] += 1
        dve.wait_ge(sem, done + n[0])

    for k in range(UNROLL):
        last = dve.bn_stats(st[:, k, :], x[:, k, :])
    step(last)
    step(dve.tensor_tensor(mean[:, :], st[:, :, 1], st[:, :, 4], ALU.add))
    step(dve.tensor_tensor(tmp[:, :], st[:, :, 1], st[:, :, 4], ALU.subtract))
    step(dve.tensor_tensor(tmp[:, :], tmp[:, :], tmp[:, :], ALU.mult))
    step(dve.tensor_scalar(mean[:, :], mean[:, :], 0.5, None, ALU.mult))
    step(dve.tensor_scalar(tmp[:, :], tmp[:, :], D / 4.0, None, ALU.mult))
    step(dve.tensor_tensor(tmp[:, :], tmp[:, :], st[:, :, 2], ALU.add))
    step(dve.tensor_tensor(tmp[:, :], tmp[:, :], st[:, :, 5], ALU.add))
    step(dve.tensor_scalar(tmp[:, :], tmp[:, :], 1.0 / D, EPS, ALU.mult, ALU.add))
    dve.wait_ge(rooted, g + 1)
    for k in range(UNROLL):
        last = dve.tensor_scalar(out[:, k, :], x[:, k, :], mean[:, k:k + 1], rstd[:, k:k + 1], ALU.subtract,
                                 ALU.mult)
    step(last)
    assert n[0] == LN_STEPS


LN_STEPS = 10


def root(pool, c, sem, rooted, passed, g, rstd, var, done=0):
    pool.wait_ge(sem, done + g * LN_STEPS + LN_STEPS - 1)
    pool.sem_inc(passed, 1)
    pool.tensor_tensor(rstd[:, :], var[:, :], c.neghalf[:, :], ALU.pow).then_inc(rooted, 1)


def ln_buffers(sb):
    return (sb("st", [P, UNROLL, 6], F32), sb("mean", [P, UNROLL], F32), sb("rstd", [P, UNROLL], F32),
            sb("tmp", [P, UNROLL], F32))


def project_heads(nc, c, W, a_l, a_r):
    c.phase = "heads"
    sem = lambda name: nc_sem(nc, c, name)
    wloaded, rooted, lnstep, normed, turned, xt_made, projected, evac, passed = (
        sem(s) for s in "wloaded rooted lnstep normed turned xt_made projected evac passed".split())
    xin, stored = [sem("xin0"), sem("xin1")], [sem("stored0"), sem("stored1")]
    with ExitStack() as ctx:
        sb = lambda name, shape, dt: ctx.enter_context(nc.sbuf_tensor(f"heads_{name}", shape, dt))
        ps = lambda name, shape: ctx.enter_context(nc.psum_tensor(f"heads_ps_{name}", shape, F32))
        w = sb("w", [P, 2, D + 8], F32)
        al = sb("al", [P, 2, D], F32)
        prod = sb("prod", [P, D], F32)
        x, xn = sb("x", [P, 2, UNROLL, D], F32), sb("xn", [P, 2, UNROLL, D], F32)
        ln = ln_buffers(sb)
        xt = sb("xt", [P, 2, 2, P], F32)
        ht = sb("ht", [P, 2, UNROLL, D + 4], F32)
        pst, psh = ps("pst", [P, 2, 512]), ps("psh", [P, 2, 512])
        block = ctx.enter_context(nc.Block())

        @block.sync
        def _(sp):
            sp.dma_start(w[:, :, 0:D], W.rearrange("(k p) d -> p k d", p=P)).then_inc(wloaded, 16)
            for j, a in enumerate((a_l, a_r)):
                sp.dma_start(al[:, j, :], a.rearrange("a h d -> a (h d)").broadcast_to([P, D])).then_inc(wloaded, 16)

            def load(g, s, j):
                sp.wait_ge(normed, g + 1)
                sp.dma_start(x[:, s, :, :], rows(c.x0, g, D)).then_inc(xin[s], 16)
            groups(sp, load)

        @block.gpsimd
        def _(pool):
            groups(pool, lambda g, s, j: root(pool, c, lnstep, rooted, passed, g, ln[2], ln[3], done=8))

        @block.vector
        def _(dve):
            n = [0]

            def step(ins):
                ins.then_inc(lnstep, 1)
                n[0] += 1
                dve.wait_ge(lnstep, n[0])
            dve.sem_inc(normed, 2)
            dve.wait_ge(wloaded, 48)
            for k in range(2):
                for j in range(2):
                    step(dve.tensor_tensor(prod[:, :], w[:, k, 0:D], al[:, j, :], ALU.mult))
                    at = D + 4 * (1 - j)
                    step(dve.tensor_reduce(w[:, k, at:at + 4], prod[:, :].rearrange("p (h d) -> p h d", h=HEADS),
                                           AX.X, ALU.add))
            base = n[0]

            def body(g, s, j):
                dve.wait_ge(xin[s], 16 * j + 16)
                dve.wait_ge(turned, g * UNROLL + UNROLL)
                normalise(dve, lnstep, rooted, g, x[:, s], xn[:, s], *ln, done=base + g * LN_STEPS)
                dve.sem_inc(normed, 1)
            groups(dve, body)

        @block.scalar
        def _(act):
            act.sem_inc(xt_made, 2)
            act.sem_inc(evac, 2)
            act.sem_inc(stored[0], 32)
            act.sem_inc(stored[1], 32)

            def body(g, s, j):
                act.wait_ge(stored[s], 32 * j + 32)
                for k in range(UNROLL):
                    t, q = g * UNROLL + k, (s + k) % 2
                    act.wait_ge(turned, t + 15)
                    act.wait_ge(projected, t + 1)
                    nc.scalar.copy(xt[:, q, :, :], pst[:, q, 0:2 * P]).then_inc(xt_made, 1)
                    act.wait_ge(projected, t + 3)
                    nc.scalar.copy(ht[:, s, k, :], psh[:, q, 0:D + 4])
                    nc.scalar.copy(c.hlm[:, bass.ds(t * 8, 4)], psh[:, q, D + 4:D + 8]).then_inc(evac, 1)
                act.wait_ge(evac, g * UNROLL + UNROLL + 2)
                act.dma_start(rows(c.t_h, g, D + 4), ht[:, s, :, :]).then_inc(stored[s], 16)
                act.dma_start(rows(c.t_hr, g, 4), ht[:, s, :, D:D + 4]).then_inc(stored[s], 16)
            groups(act, body)
            act.wait_ge(stored[0], 32 * 5)
            act.wait_ge(stored[1], 32 * 4)

        @block.tensor
        def _(pe):
            pe.sem_inc(turned, 14)
            pe.sem_inc(projected, 2)
            pe.wait_ge(lnstep, 8)

            def body(g, s, j):
                pe.wait_ge(normed, g + 3)
                for k in range(UNROLL):
                    t, q = g * UNROLL + k, (s + k) % 2
                    pe.wait_ge(xt_made, t + 1)
                    for b in range(2):
                        last = pe.transpose(pst[:, q, b * P:(b + 1) * P], xn[:, s, k, b * P:(b + 1) * P], c.ident[:, :])
                    last.then_inc(turned, 1)
                    pe.wait_ge(xt_made, t + 3)
                    pe.wait_ge(evac, t + 1)
                    for b in range(2):
                        last = pe.matmul(psh[:, q, 0:D + 8], xt[:, q, b, :], w[:, b, :], start=(b == 0), stop=(b == 1))
                    last.then_inc(projected, 1)
            groups(pe, body)


def skewed(eng, stages, total, u):
    for t in range(u):
        for lag, body in stages:
            if t >= lag:
                body(t - lag, (t - lag) % u, (t - lag) // u)
    with eng.Fori(1, total // u) as i:
        for k in range(u):
            for lag, body in stages:
                body(i * u + (k - lag), (k - lag) % u, i - 1 if k < lag else i)
    for t in range(total, total + max(lag for lag, _ in stages)):
        for lag, body in stages:
            if t - lag < total:
                body(t - lag, (t - lag) % u, (t - lag) // u)


def gather_rows(pool, c, idx, few, table, ring, gathered, freed, copied, passed):
    with pool.Fori(0, ET // RING) as i:
        for h in range(2):
            pool.wait_ge(freed, i * RING + 4 * h + 4)
            pool.sem_inc(passed, 1)
            pool.tensor_copy(few[:, h, :], idx[:, bass.ds(i * RING + 4 * h, 4)]).then_inc(copied, 1)
            pool.wait_ge(copied, 2 * i + h + 1)
            pool.sem_inc(passed, 1)
            for k in range(4 * h, 4 * h + 4):
                pool.indirect_dma_start(out=ring[:, k, :], out_offset=None, in_=table[:, :],
                                        in_offset=bass.IndirectOffsetOnAxis(ap=few[:, h, k % 4:k % 4 + 1], axis=0)
                                        ).then_inc(gathered[k], 16)


def one_hots(dve, c, local, oh, t, k):
    return dve.tensor_tensor(oh[:, k:k + 4, :], c.iota[:, 0:P].unsqueeze(1).broadcast_to([P, 4, P]),
                             local[:, bass.ds(t, 4)].unsqueeze(2).broadcast_to([P, 4, P]), ALU.is_equal)


def neighbour_max(nc, c):
    c.phase = "nmax"
    sem = lambda name: nc_sem(nc, c, name)
    freed, copied, passed, oh_made, turned, brought, spread, step, cleared = (
        sem(s) for s in "freed copied passed oh_made turned brought spread step cleared".split())
    gathered = [sem(f"gathered{k}") for k in range(RING)]
    with ExitStack() as ctx:
        sb = lambda name, shape, dt: ctx.enter_context(nc.sbuf_tensor(f"nmax_{name}", shape, dt))
        ps = lambda name, shape: ctx.enter_context(nc.psum_tensor(f"nmax_ps_{name}", shape, F32))
        few = sb("few", [P, 2, 4], I32)
        hr = sb("hr", [P, RING, 4], F32)
        oh = sb("oh", [P, RING, P], F32)
        hrt = sb("hrt", [4, 2, P], F32)
        pen = sb("pen", [P, 2, P], F32)
        junk = sb("junk", [P, 2, HEADS, P], F32)
        tmax = sb("tmax", [P, 2, 4], F32)
        best = sb("best", [P, TILES * 4], F32)
        tmp = sb("tmp", [P, TILES, 4], F32)
        ps_hr, ps_oh, ps_all = ps("hr", [P, 2, 512]), ps("oh", [P, 2, 512]), ps("all", [P, 2, 512])
        block = ctx.enter_context(nc.Block())

        @block.gpsimd
        def _(pool):
            gather_rows(pool, c, c.idx_s, few, c.t_hr, hr, gathered, freed, copied, passed)

        @block.tensor
        def _(pe):
            pe.sem_inc(freed, RING)
            pe.sem_inc(spread, RING)

            def turn(t, k, turn_):
                q = k % 2
                pe.wait_ge(gathered[k], 16 * turn_ + 16)
                pe.wait_ge(brought, 2 * t + 1)
                pe.transpose(ps_hr[0:4, q, 0:P], hr[:, k, :], c.ident[:, :]).then_inc(freed, 1)
                pe.wait_ge(oh_made, 2 * turn_ + k // 4 + 1)
                pe.transpose(ps_oh[:, q, 0:P], oh[:, k, :], c.ident[:, :]).then_inc(turned, 1)

            def every_node(t, k, turn_):
                q = k % 2
                pe.wait_ge(brought, 2 * t + 6)
                pe.wait_ge(step, 2 * t + 1)
                for h in range(HEADS):
                    last = pe.matmul(ps_all[:, q, h * P:(h + 1) * P], c.headsel[:, h, :], hrt[:, q, :],
                                     start=True, stop=True)
                last.then_inc(spread, 1)
            skewed(pe, [(0, turn), (1, every_node)], ET, RING)

        @block.scalar
        def _(act):
            act.sem_inc(brought, 4)

            def body(t, k, turn_):
                q = k % 2
                act.wait_ge(turned, t + 1)
                act.wait_ge(spread, t + RING - 1)
                nc.scalar.copy(hrt[:, q, :], ps_hr[0:4, q, 0:P]).then_inc(brought, 1)
                act.wait_ge(step, 2 * t + 1)
                nc.scalar.activation(pen[:, q, :], ps_oh[:, q, 0:P], ACT.Copy, bias=LOW, scale=-LOW).then_inc(brought, 1)
            skewed(act, [(0, body)], ET, RING)

        @block.vector
        def _(dve):
            dve.memset(best[:, :], LOW).then_inc(cleared, 1)
            dve.sem_inc(step, 4)
            dve.wait_ge(cleared, 1)

            def hots(t, k, turn_):
                if k % 4 == 0:
                    dve.wait_ge(spread, t + 4)
                    one_hots(dve, c, c.loc_s, oh, t, k).then_inc(oh_made, 1)

            def reduce(t, k, turn_):
                q = k % 2
                dve.wait_ge(spread, t + RING + 1)
                dve.sem_inc(passed, 1)
                for h in range(HEADS):
                    last = dve.tensor_tensor_reduce(junk[:, q, h, :], pen[:, q, :], ps_all[:, q, h * P:(h + 1) * P],
                                                    1.0, LOW, ALU.add, ALU.max, tmax[:, q, h:h + 1])
                last.then_inc(step, 1)
                b = dve.value_load(c.buc_s[0:1, bass.ds(t, 1)], min_val=0, max_val=TILES - 1)
                dve.wait_ge(step, 2 * t + 5)
                here = best[:, bass.ds(b * 4, 4)]
                dve.tensor_tensor(here, here, tmax[:, q, :], ALU.max).then_inc(step, 1)
            skewed(dve, [(0, hots), (4, reduce)], ET, RING)
            dve.wait_ge(step, 2 * ET + 4)
            hl = c.hlm[:, :].rearrange("p (i e) -> p i e", e=8)
            dve.tensor_tensor(tmp[:, :, :], hl[:, :, 0:4], best[:, :].rearrange("p (i e) -> p i e", e=4),
                              ALU.add).then_inc(cleared, 1)
            dve.wait_ge(cleared, 2)
            dve.scalar_tensor_tensor(out=hl[:, :, 4:8], in0=tmp[:, :, :], scalar=0.2, in1=tmp[:, :, :], op0=ALU.mult,
                                     op1=ALU.max).then_inc(cleared, 1)
            dve.wait_ge(cleared, 3)


def attend(nc, c):
    c.phase = "attend"
    W = D + 4
    sem = lambda name: nc_sem(nc, c, name)
    (freed, copied, passed, oh_made, oh_turned, oht_made, looked, scored, exped, weighted, scattered, added,
     step, cleared) = (sem(s) for s in ("freed copied passed oh_made oh_turned oht_made looked scored exped weighted "
                                        "scattered added step cleared").split())
    gathered = [sem(f"gathered{k}") for k in range(RING)]
    with ExitStack() as ctx:
        sb = lambda name, shape, dt: ctx.enter_context(nc.sbuf_tensor(f"attend_{name}", shape, dt))
        ps = lambda name, shape: ctx.enter_context(nc.psum_tensor(f"attend_ps_{name}", shape, F32))
        few = sb("few", [P, 2, 4], I32)
        rows_h = sb("rows", [P, RING, W], F32)
        oh = sb("oh", [P, RING, P], F32)
        oht = sb("oht", [P, 2, P], F32)
        sc = sb("sc", [P, 2, 3, 4], F32)
        wr = sb("wr", [P, 2, W], F32)
        ps_oh, ps_look, ps_sum = ps("oh", [P, 2, 512]), ps("look", [P, 2, 512]), ps("sum", [P, 2, 512])
        block = ctx.enter_context(nc.Block())

        @block.gpsimd
        def _(pool):
            gather_rows(pool, c, c.idx_s, few, c.t_h, rows_h, gathered, weighted, copied, passed)

        @block.tensor
        def _(pe):
            pe.sem_inc(looked, 2)
            pe.sem_inc(scattered, RING)

            def turn(t, k, turn_):
                pe.wait_ge(oh_made, 2 * turn_ + k // 4 + 1)
                pe.wait_ge(oht_made, t + 1)
                pe.transpose(ps_oh[:, k % 2, 0:P], oh[:, k, :], c.ident[:, :]).then_inc(oh_turned, 1)

            def look(t, k, turn_):
                b = pe.value_load(c.buc_s[0:1, bass.ds(t, 1)], min_val=0, max_val=TILES - 1)
                pe.wait_ge(oht_made, t + 3)
                pe.wait_ge(scored, t + 1)
                pe.matmul(ps_look[:, k % 2, 0:8], oht[:, k % 2, :], c.hlm[:, bass.ds(b * 8, 8)], start=True,
                          stop=True).then_inc(looked, 1)

            def scatter(t, k, turn_):
                pe.wait_ge(weighted, t + RING + 1)
                pe.wait_ge(added, t + 1)
                pe.matmul(ps_sum[:, k % 2, 0:W], oh[:, k, :], wr[:, k % 2, :], start=True, stop=True
                          ).then_inc(scattered, 1)
            skewed(pe, [(0, turn), (1, look), (3, scatter)], ET, RING)

        @block.scalar
        def _(act):
            act.sem_inc(oht_made, 2)
            act.sem_inc(weighted, RING)

            def turned(t, k, turn_):
                act.wait_ge(oh_turned, t + 1)
                act.wait_ge(looked, t + 1)
                nc.scalar.copy(oht[:, k % 2, :], ps_oh[:, k % 2, 0:P]).then_inc(oht_made, 1)

            def weigh(t, k, turn_):
                q = k % 2
                act.wait_ge(scored, t + 3)
                act.wait_ge(scattered, t + RING - 1)
                nc.scalar.activation(wr[:, q, D:W], sc[:, q, 2, :], ACT.Exp).then_inc(exped, 1)
                act.wait_ge(exped, t + 1)
                for h in range(HEADS):
                    last = nc.scalar.activation(wr[:, q, h * HD:(h + 1) * HD], rows_h[:, k, h * HD:(h + 1) * HD],
                                                ACT.Copy, scale=wr[:, q, D + h:D + h + 1])
                last.then_inc(weighted, 1)
            skewed(act, [(0, turned), (2, weigh)], ET, RING)

        @block.vector
        def _(dve):
            dve.memset(c.acc[:, 0:TILES * W], 0.0).then_inc(cleared, 1)
            dve.sem_inc(scored, 2)
            dve.sem_inc(added, 2)
            dve.wait_ge(cleared, 1)

            def hots(t, k, turn_):
                if k % 4 == 0:
                    dve.wait_ge(scattered, t + 4)
                    one_hots(dve, c, c.loc_s, oh, t, k).then_inc(oh_made, 1)

            def score(t, k, turn_):
                q = k % 2
                dve.wait_ge(looked, t + 3)
                dve.wait_ge(gathered[k], 16 * turn_ + 16)
                dve.wait_ge(weighted, t + RING - 1)
                dve.tensor_tensor(sc[:, q, 0, :], ps_look[:, q, 0:4], rows_h[:, k, D:W], ALU.add).then_inc(step, 1)
                dve.wait_ge(step, 2 * t + 1)
                dve.scalar_tensor_tensor(out=sc[:, q, 1, :], in0=sc[:, q, 0, :], scalar=0.2, in1=sc[:, q, 0, :],
                                         op0=ALU.mult, op1=ALU.max).then_inc(step, 1)
                dve.wait_ge(step, 2 * t + 2)
                dve.tensor_tensor(sc[:, q, 2, :], sc[:, q, 1, :], ps_look[:, q, 4:8], ALU.subtract
                                  ).then_inc(scored, 1)

            def add(t, k, turn_):
                b = dve.value_load(c.buc_s[0:1, bass.ds(t, 1)], min_val=0, max_val=TILES - 1)
                dve.wait_ge(scattered, t + RING + 1)
                dve.wait_ge(added, t + 2)
                here = c.acc[:, bass.ds(b * W, W)]
                dve.tensor_tensor(here, here, ps_sum[:, k % 2, 0:W], ALU.add).then_inc(added, 1)
            skewed(dve, [(0, hots), (1, score), (3, add)], ET, RING)
            dve.wait_ge(added, ET + 2)


def close_attention(nc, c):
    c.phase = "close"
    W = D + 4
    sem = lambda name: nc_sem(nc, c, name)
    rooted, lnstep, summed, normed, used, passed, counted, allsummed = (
        sem(s) for s in "rooted lnstep summed normed used passed counted allsummed".split())
    xin, stored = [sem("xin0"), sem("xin1")], [sem("stored0"), sem("stored1")]
    with ExitStack() as ctx:
        sb = lambda name, shape, dt: ctx.enter_context(nc.sbuf_tensor(f"close_{name}", shape, dt))
        x, x1, xn = (sb(n, [P, 2, UNROLL, D], F32) for n in ("x", "x1", "xn"))
        den = sb("den", [P, UNROLL, HEADS], F32)
        ln = ln_buffers(sb)
        pcol = ctx.enter_context(nc.psum_tensor("close_pcol", [P, 2, 512], F32))
        block = ctx.enter_context(nc.Block())

        @block.sync
        def _(sp):
            def load(g, s, j):
                sp.wait_ge(summed, g + 1)
                sp.dma_start(x[:, s, :, :], rows(c.x0, g, D)).then_inc(xin[s], 16)
            groups(sp, load)

        @block.gpsimd
        def _(pool):
            groups(pool, lambda g, s, j: root(pool, c, lnstep, rooted, passed, g, ln[2], ln[3]))

        @block.vector
        def _(dve):
            dve.sem_inc(summed, 2)

            def body(g, s, j):
                acc = c.acc[:, bass.ds(g * (UNROLL * W), UNROLL * W)].rearrange("p (k w) -> p k w", w=W)
                att = acc[:, :, 0:D].rearrange("p k (h d) -> p k h d", h=HEADS)
                dve.tensor_scalar(den[:, :, :], acc[:, :, D:W], 1e-30, None, ALU.max).then_inc(counted, 1)
                dve.wait_ge(counted, 3 * g + 1)
                dve.reciprocal(den[:, :, :], den[:, :, :]).then_inc(counted, 1)
                dve.wait_ge(counted, 3 * g + 2)
                dve.tensor_tensor(att, att, den[:, :, :].unsqueeze(3).broadcast_to([P, UNROLL, HEADS, HD]), ALU.mult
                                  ).then_inc(counted, 1)
                dve.wait_ge(xin[s], 16 * j + 16)
                dve.wait_ge(stored[s], 32 * j + 32)
                dve.wait_ge(counted, 3 * g + 3)
                dve.tensor_tensor(x1[:, s], acc[:, :, 0:D], x[:, s], ALU.add).then_inc(summed, 1)
                dve.wait_ge(summed, g + 3)
                dve.wait_ge(used, g + 1)
                normalise(dve, lnstep, rooted, g, x1[:, s], xn[:, s], *ln, done=g * LN_STEPS)
                dve.sem_inc(normed, 1)
            groups(dve, body)
            dve.wait_ge(allsummed, 1)
            dve.tensor_copy(c.colsum[:, :], pcol[:, :, 0]).then_inc(counted, 1)
            dve.wait_ge(counted, 3 * GROUPS + 1)

        @block.scalar
        def _(act):
            act.sem_inc(stored[0], 32)
            act.sem_inc(stored[1], 32)

            def store(g, s, j):
                act.wait_ge(normed, g + 1)
                act.dma_start(rows(c.x1, g, D), x1[:, s]).then_inc(stored[s], 16)
                act.dma_start(rows(c.xn1, g, D), xn[:, s]).then_inc(stored[s], 16)
            groups(act, store)
            act.wait_ge(stored[0], 32 * 5)
            act.wait_ge(stored[1], 32 * 4)

        @block.tensor
        def _(pe):
            pe.sem_inc(used, 2)
            for b in range(2):
                pe.matmul(pcol[:, b, 0:1], c.zeros[:, 0:P], c.ones[:, 0:1], start=True, stop=False)

            def body(g, s, j):
                pe.wait_ge(normed, g + 1)
                for k in range(UNROLL):
                    for b in range(2):
                        last = pe.matmul(pcol[:, b, 0:1], xn[:, s, k, b * P:(b + 1) * P], c.ones[:, 0:1],
                                         start=False, stop=False)
                last.then_inc(used, 1)
            groups(pe, body)
            for b in range(2):
                last = pe.matmul(pcol[:, b, 0:1], c.zeros[:, 0:P], c.ones[:, 0:1], start=False, stop=True)
            last.then_inc(allsummed, 1)


def choose_experts(nc, c, Wr, br):
    c.phase = "choose"
    sem = lambda name: nc_sem(nc, c, name)
    loaded, step, given, expd = (sem(s) for s in "loaded step given expd".split())
    with ExitStack() as ctx:
        sb = lambda name, shape, dt: ctx.enter_context(nc.sbuf_tensor(f"choose_{name}", shape, dt))
        wr, brow = sb("wr", [P, 2, X0], F32), sb("brow", [P, X0], F32)
        mean = sb("mean", [P, 2, P], F32)
        v, e, w, eq, cand = (sb(n, [P, X0], F32) for n in ("v", "e", "w", "eq", "cand"))
        one, two = sb("one", [P, 8], F32), sb("two", [P, 8], F32)
        plog = ctx.enter_context(nc.psum_tensor("choose_plog", [P, 512], F32))
        block = ctx.enter_context(nc.Block())

        @block.sync
        def _(sp):
            sp.dma_start(wr[:, :, :], Wr.rearrange("(k p) e -> p k e", p=P)).then_inc(loaded, 16)
            sp.dma_start(brow[:, :], br.rearrange("(a e) -> a e", a=1).broadcast_to([P, X0])).then_inc(loaded, 16)

        @block.tensor
        def _(pe):
            pe.wait_ge(loaded, 32)
            pe.wait_ge(step, 2)
            for b in range(2):
                last = pe.matmul(plog[:, 0:X0], mean[:, b, :], wr[:, b, :], start=(b == 0), stop=(b == 1))
            last.then_inc(given, 1)

        @block.scalar
        def _(act):
            act.wait_ge(expd, 1)
            nc.scalar.activation(e[:, :], v[:, :], ACT.Exp).then_inc(given, 1)
            act.wait_ge(expd, 2)
            nc.scalar.activation(e[:, :], v[:, :], ACT.Exp).then_inc(given, 1)
            act.wait_ge(expd, 3)
            nc.scalar.activation(two[:, 2:3], two[:, 0:1], ACT.Exp).then_inc(given, 1)

        @block.vector
        def _(dve):
            n = [0]

            def do(ins):
                ins.then_inc(step, 1)
                n[0] += 1
                dve.wait_ge(step, n[0])

            def softmax(nth):
                do(dve.tensor_reduce(one[:, 0:1], v[:, :], AX.X, ALU.max))
                do(dve.tensor_scalar(v[:, :], v[:, :], one[:, 0:1], None, ALU.subtract))
                dve.sem_inc(expd, 1)
                dve.wait_ge(given, nth + 1)
                do(dve.tensor_reduce(one[:, 1:2], e[:, :], AX.X, ALU.add))
                do(dve.reciprocal(one[:, 1:2], one[:, 1:2]))
                do(dve.tensor_scalar(w[:, :], e[:, :], one[:, 1:2], None, ALU.mult))

            for b in range(2):
                do(dve.tensor_scalar(mean[:, b, :], c.ones[:, :], c.colsum[:, b:b + 1], 1.0 / N, ALU.mult, ALU.mult))
            dve.wait_ge(given, 1)
            do(dve.tensor_tensor(v[:, :], plog[:, 0:X0], brow[:, :], ALU.add))
            softmax(1)
            do(dve.tensor_scalar(v[:, :], w[:, :], float(N), CAP0, ALU.mult, ALU.max))
            do(dve.reciprocal(v[:, :], v[:, :]))
            do(dve.tensor_scalar(v[:, :], v[:, :], CAP0, None, ALU.mult))
            do(dve.tensor_tensor(v[:, :], v[:, :], w[:, :], ALU.mult))
            softmax(2)
            for m in range(2):
                do(dve.tensor_reduce(one[:, 2 + m:3 + m], w[:, :], AX.X, ALU.max))
                do(dve.tensor_scalar(eq[:, :], w[:, :], one[:, 2 + m:3 + m], 100.0, ALU.not_equal, ALU.mult))
                do(dve.tensor_tensor(cand[:, :], eq[:, :], c.iota[:, 0:X0], ALU.add))
                do(dve.tensor_reduce(one[:, 4 + m:5 + m], cand[:, :], AX.X, ALU.min))
                do(dve.tensor_scalar(eq[:, :], c.iota[:, 0:X0], one[:, 4 + m:5 + m], 4.0, ALU.is_equal, ALU.mult))
                do(dve.tensor_tensor(w[:, :], w[:, :], eq[:, :], ALU.subtract))
            do(dve.tensor_copy(c.chosen[0:1, :], one[0:1, 4:6]))
            do(dve.tensor_tensor(two[:, 0:1], one[:, 3:4], one[:, 2:3], ALU.subtract))
            dve.sem_inc(expd, 1)
            dve.wait_ge(given, 4)
            do(dve.tensor_scalar(two[:, 3:4], two[:, 2:3], 1.0, None, ALU.add))
            do(dve.reciprocal(c.share[:, 0:1], two[:, 3:4]))
            do(dve.tensor_tensor(c.share[:, 1:2], c.share[:, 0:1], two[:, 2:3], ALU.mult))


def experts0(nc, c, W1, b1, W2, b2, gamma, beta):
    c.phase = "experts0"
    FC = F0 // P
    NH = UNROLL * P // 2
    sem = lambda name: nc_sem(nc, c, name)
    (wloaded, wready, rooted, lnstep, turned, xt_made, hidden, gelued, mixed, emptied, passed, step, out) = (
        sem(s) for s in ("wloaded wready rooted lnstep turned xt_made hidden gelued mixed emptied passed step "
                         "out").split())
    xin, stored = [sem("xin0"), sem("xin1")], [sem("stored0"), sem("stored1")]
    with ExitStack() as ctx:
        sb = lambda name, shape, dt: ctx.enter_context(nc.sbuf_tensor(f"experts0_{name}", shape, dt))
        ps = lambda name, shape: ctx.enter_context(nc.psum_tensor(f"experts0_ps_{name}", shape, F32))
        w1 = sb("w1", [P, 2, 2, F0], F32)
        w2 = sb("w2", [P, 2, FC, D], F32)
        b1s = sb("b1", [P, 2, FC], F32)
        b2s = sb("b2", [P, 2, D], F32)
        gam, bet = sb("gam", [P, D], F32), sb("bet", [P, D], F32)
        xn, xr = sb("xn", [P, 2, UNROLL, D], F32), sb("xr", [P, 2, UNROLL, D], F32)
        xt = sb("xt", [P, 2, UNROLL * P], F32)
        hid = sb("hid", [P, 2 * FC, UNROLL * P], F32)
        y = sb("y", [P, UNROLL, D], F32)
        yo = sb("yo", [P, 2, UNROLL, D], F32)
        ln = ln_buffers(sb)
        pst, psh, psy = ps("t", [P, 2, 512]), ps("h", [P, 2, 512]), ps("y", [P, 2, 512])
        block = ctx.enter_context(nc.Block())

        @block.sync
        def _(sp):
            for m in range(2):
                e = sp.value_load(c.chosen[0:1, m:m + 1], min_val=0, max_val=X0 - 1)
                sp.dma_start(w1[:, m], W1[bass.ds(e, 1)].rearrange("a (k p) f -> p (a k) f", p=P)).then_inc(wloaded, 16)
                sp.dma_start(w2[:, m], W2[bass.ds(e, 1)].rearrange("a (k p) f -> p (a k) f", p=P)).then_inc(wloaded, 16)
                with nc.allow_non_contiguous_dma("a bias, one element to a partition"):
                    sp.dma_start(b1s[:, m, :], b1[bass.ds(e, 1)].rearrange("a (k p) -> p (a k)", p=P)
                                 ).then_inc(wloaded, 16)
                sp.dma_start(b2s[:, m, :], b2[bass.ds(e, 1)].broadcast_to([P, D])).then_inc(wloaded, 16)
            for t, d in ((gam, gamma), (bet, beta)):
                sp.dma_start(t[:, :], d.rearrange("(a e) -> a e", a=1).broadcast_to([P, D])).then_inc(wloaded, 16)

            def load(g, s, j):
                sp.wait_ge(out, g + 1)
                sp.dma_start(xn[:, s], rows(c.xn1, g, D)).then_inc(xin[s], 16)
                sp.dma_start(xr[:, s], rows(c.x1, g, D)).then_inc(xin[s], 16)
            groups(sp, load)

        @block.gpsimd
        def _(pool):
            groups(pool, lambda g, s, j: root(pool, c, lnstep, rooted, passed, g, ln[2], ln[3]))

        @block.tensor
        def _(pe):
            pe.sem_inc(hidden, 2)
            pe.wait_ge(wready, 1)

            def body(g, s, j):
                pe.wait_ge(xin[s], 32 * j + 32)
                for k in range(UNROLL):
                    q = (s + k) % 2
                    pe.wait_ge(xt_made, g * UNROLL + k + 1)
                    for b in range(2):
                        last = pe.transpose(pst[:, q, b * P:(b + 1) * P], xn[:, s, k, b * P:(b + 1) * P], c.ident[:, :])
                    last.then_inc(turned, 1)
                pe.wait_ge(xt_made, g * UNROLL + UNROLL + 2)
                for m in range(4 * FC):
                    f, half, q = m // 2, m % 2, m % 2
                    pe.wait_ge(gelued, g * (4 * FC) + m + 1)
                    for b in range(2):
                        last = pe.matmul(psh[:, q, 0:NH], w1[:, f // FC, b, (f % FC) * P:(f % FC + 1) * P],
                                         xt[:, b, half * NH:(half + 1) * NH], start=(b == 0), stop=(b == 1))
                    last.then_inc(hidden, 1)
                pe.wait_ge(gelued, g * (4 * FC) + 4 * FC + 2)
                for k in range(UNROLL):
                    q = (s + k) % 2
                    pe.wait_ge(emptied, g * UNROLL + k + 1)
                    for f in range(2 * FC):
                        last = pe.matmul(psy[:, q, 0:D], hid[:, f, k * P:(k + 1) * P], w2[:, f // FC, f % FC, :],
                                         start=(f == 0), stop=(f == 2 * FC - 1))
                    last.then_inc(mixed, 1)
            groups(pe, body)

        @block.scalar
        def _(act):
            act.sem_inc(xt_made, 2)
            act.sem_inc(gelued, 2)
            act.sem_inc(stored[0], 16)
            act.sem_inc(stored[1], 16)
            act.wait_ge(wloaded, 160)

            def body(g, s, j):
                act.wait_ge(hidden, g * (4 * FC) + 2)
                for k in range(UNROLL):
                    act.wait_ge(turned, g * UNROLL + k + 1)
                    nc.scalar.copy(xt[:, :, k * P:(k + 1) * P],
                                   pst[:, (s + k) % 2, 0:2 * P].rearrange("p (b n) -> p b n", b=2)).then_inc(xt_made, 1)
                act.wait_ge(mixed, g * UNROLL + 1)
                for m in range(4 * FC):
                    f, half = m // 2, m % 2
                    act.wait_ge(hidden, g * (4 * FC) + m + 3)
                    nc.scalar.activation(hid[:, f, half * NH:(half + 1) * NH], psh[:, m % 2, 0:NH], ACT.Gelu,
                                         bias=b1s[:, f // FC, f % FC:f % FC + 1]).then_inc(gelued, 1)
                act.wait_ge(out, g + 3)
                act.dma_start(rows(c.x2, g, D), yo[:, s]).then_inc(stored[s], 16)
            groups(act, body)
            act.wait_ge(stored[0], 16 * 5)
            act.wait_ge(stored[1], 16 * 4)

        @block.vector
        def _(dve):
            n = [0]

            def do(ins):
                ins.then_inc(step, 1)
                n[0] += 1
                dve.wait_ge(step, n[0])

            dve.sem_inc(mixed, 1)
            dve.sem_inc(emptied, 2)
            dve.sem_inc(out, 2)
            dve.wait_ge(wloaded, 160)
            for m in range(2):
                do(dve.tensor_scalar(w2[:, m], w2[:, m], c.share[:, m:m + 1], None, ALU.mult))
                do(dve.tensor_scalar(b2s[:, m, :], b2s[:, m, :], c.share[:, m:m + 1], None, ALU.mult))
            do(dve.tensor_tensor(b2s[:, 0, :], b2s[:, 0, :], b2s[:, 1, :], ALU.add))
            dve.sem_inc(wready, 1)
            base = n[0]
            bias = b2s[:, 0:1, :].broadcast_to([P, UNROLL, D])
            wide = lambda t: t[:, :].unsqueeze(1).broadcast_to([P, UNROLL, D])

            def body(g, s, j):
                dve.wait_ge(xin[s], 32 * j + 32)
                at = base + g * (UNROLL + 4)
                for k in range(UNROLL):
                    dve.wait_ge(mixed, g * UNROLL + k + 2)
                    dve.tensor_tensor(y[:, k, :], psy[:, (s + k) % 2, 0:D], xn[:, s, k, :], ALU.add).then_inc(step, 1)
                    dve.wait_ge(step, at + k + 1)
                    dve.sem_inc(emptied, 1)
                dve.tensor_tensor(y[:, :, :], y[:, :, :], bias, ALU.add).then_inc(step, 1)
                dve.wait_ge(step, at + UNROLL + 1)
                dve.wait_ge(stored[s], 16 * j + 16)
                normalise(dve, lnstep, rooted, g, y, yo[:, s], *ln, done=g * LN_STEPS)
                dve.tensor_tensor(yo[:, s], yo[:, s], wide(gam), ALU.mult).then_inc(step, 1)
                dve.wait_ge(step, at + UNROLL + 2)
                dve.tensor_tensor(yo[:, s], yo[:, s], wide(bet), ALU.add).then_inc(step, 1)
                dve.wait_ge(step, at + UNROLL + 3)
                dve.tensor_tensor(yo[:, s], yo[:, s], xr[:, s], ALU.add).then_inc(step, 1)
                dve.wait_ge(step, at + UNROLL + 4)
                dve.sem_inc(out, 1)
            groups(dve, body)


def prepare_conv(nc, c):
    c.phase = "prep"
    sem = lambda name: nc_sem(nc, c, name)
    rooted, lnstep, normed, passed, step, powd = (sem(s) for s in "rooted lnstep normed passed step powd".split())
    xin, stored = [sem("xin0"), sem("xin1")], [sem("stored0"), sem("stored1")]
    with ExitStack() as ctx:
        sb = lambda name, shape, dt: ctx.enter_context(nc.sbuf_tensor(f"prep_{name}", shape, dt))
        x, xn, xs = (sb(n, [P, 2, UNROLL, D], F32) for n in ("x", "xn", "xs"))
        half = sb("half", [P, TILES], F32)
        ln = ln_buffers(sb)
        block = ctx.enter_context(nc.Block())

        @block.sync
        def _(sp):
            def load(g, s, j):
                sp.wait_ge(normed, g + 1)
                sp.dma_start(x[:, s], rows(c.x2, g, D)).then_inc(xin[s], 16)
            groups(sp, load)

        @block.gpsimd
        def _(pool):
            pool.wait_ge(step, 2)
            pool.tensor_tensor(c.dis[:, :], c.deg[:, :], half[:, :], ALU.pow).then_inc(powd, 1)
            groups(pool, lambda g, s, j: root(pool, c, lnstep, rooted, passed, g, ln[2], ln[3]))

        @block.scalar
        def _(act):
            act.sem_inc(stored[0], 32)
            act.sem_inc(stored[1], 32)

            def store(g, s, j):
                act.wait_ge(normed, g + 3)
                act.dma_start(rows(c.xn2, g, D), xn[:, s]).then_inc(stored[s], 16)
                act.dma_start(rows(c.t_x, g, D), xs[:, s]).then_inc(stored[s], 16)
            groups(act, store)
            act.wait_ge(stored[0], 32 * 5)
            act.wait_ge(stored[1], 32 * 4)

        @block.vector
        def _(dve):
            dve.sem_inc(normed, 2)
            dve.tensor_scalar(half[:, :], c.zeros[:, 0:TILES], -0.5, None, ALU.add).then_inc(step, 1)
            dve.tensor_scalar(c.deg[:, :], c.deg[:, :], 1.0, None, ALU.add).then_inc(step, 1)
            dve.wait_ge(powd, 1)
            dve.tensor_tensor(c.dis[:, TILES - 1:TILES], c.dis[:, TILES - 1:TILES], c.valid[:, 0:1], ALU.mult
                              ).then_inc(step, 1)
            dve.wait_ge(step, 3)

            def body(g, s, j):
                dve.wait_ge(xin[s], 16 * j + 16)
                dve.wait_ge(stored[s], 32 * j + 32)
                normalise(dve, lnstep, rooted, g, x[:, s], xn[:, s], *ln, done=g * LN_STEPS)
                dis = c.dis[:, bass.ds(g * UNROLL, UNROLL)].unsqueeze(2).broadcast_to([P, UNROLL, D])
                dve.tensor_tensor(xs[:, s], xn[:, s], dis, ALU.mult).then_inc(step, 1)
                dve.wait_ge(step, 2 * g + 4)
                dve.sem_inc(passed, 1)
                dve.tensor_copy(c.acc[:, bass.ds(g * (UNROLL * D), UNROLL * D)],
                                xs[:, s].rearrange("p k d -> p (k d)")).then_inc(step, 1)
                dve.wait_ge(step, 2 * g + 5)
                dve.sem_inc(normed, 1)
            groups(dve, body)


def aggregate(nc, c, tag, table):
    c.phase = tag
    sem = lambda name: nc_sem(nc, c, name)
    copied, passed, oh_made, scattered, added = (sem(s) for s in "copied passed oh_made scattered added".split())
    gathered = [sem(f"gathered{k}") for k in range(RING)]
    with ExitStack() as ctx:
        few = ctx.enter_context(nc.sbuf_tensor(f"{tag}_few", [P, 2, 4], I32))
        sent = ctx.enter_context(nc.sbuf_tensor(f"{tag}_sent", [P, RING, D], F32))
        oh = ctx.enter_context(nc.sbuf_tensor(f"{tag}_oh", [P, RING, P], F32))
        ps_sum = ctx.enter_context(nc.psum_tensor(f"{tag}_sum", [P, 4, 512], F32))
        block = ctx.enter_context(nc.Block())

        @block.gpsimd
        def _(pool):
            gather_rows(pool, c, c.idx_d, few, table, sent, gathered, scattered, copied, passed)

        @block.tensor
        def _(pe):
            pe.sem_inc(scattered, RING)

            def scatter(t, k, turn_):
                if k % 4 == 0:
                    pe.wait_ge(oh_made, 2 * turn_ + k // 4 + 1)
                pe.wait_ge(gathered[k], 16 * turn_ + 16)
                pe.wait_ge(added, t + 1)
                pe.matmul(ps_sum[:, k % 4, 0:D], oh[:, k, :], sent[:, k, :], start=True, stop=True
                          ).then_inc(scattered, 1)
            skewed(pe, [(0, scatter)], ET, RING)

        @block.vector
        def _(dve):
            dve.sem_inc(added, 4)

            def hots(t, k, turn_):
                if k % 4 == 0:
                    dve.wait_ge(scattered, t + 4)
                    one_hots(dve, c, c.loc_d, oh, t, k).then_inc(oh_made, 1)

            def add(t, k, turn_):
                b = dve.value_load(c.buc_d[0:1, bass.ds(t, 1)], min_val=0, max_val=TILES - 1)
                dve.wait_ge(scattered, t + RING + 1)
                dve.wait_ge(added, t + 4)
                here = c.acc[:, bass.ds(b * D, D)]
                dve.tensor_tensor(here, here, ps_sum[:, k % 4, 0:D], ALU.add).then_inc(added, 1)
            skewed(dve, [(0, hots), (3, add)], ET, RING)
            dve.wait_ge(added, ET + 4)


def conv_hidden(nc, c, W1t, g1, b1, W2t):
    c.phase = "conv"
    FC = IC // P
    NH = UNROLL * P // 2
    LAST = N - (GROUPS - 1) * UNROLL * P - NH
    sem = lambda name: nc_sem(nc, c, name)
    (wloaded, scaled, turned, xt_made, hidden, statted, kept, passed, step, rooted, relued, sent, emptied, out) = (
        sem(s) for s in ("wloaded scaled turned xt_made hidden statted kept passed step rooted relued sent emptied "
                         "out").split())
    stored = [sem("stored0"), sem("stored1")]
    with ExitStack() as ctx:
        sb = lambda name, shape, dt: ctx.enter_context(nc.sbuf_tensor(f"conv_{name}", shape, dt))
        ps = lambda name, shape: ctx.enter_context(nc.psum_tensor(f"conv_ps_{name}", shape, F32))
        w1, w2 = sb("w1", [P, 2, IC], F32), sb("w2", [P, FC, D], F32)
        gb = sb("gb", [P, 2, FC], F32)
        y1 = sb("y1", [P, FC, NP], F32)
        st = sb("st", [P, FC, 2 * GROUPS * 6], F32)
        mv = sb("mv", [P, FC, 2], F32)
        coef = sb("coef", [P, 5, FC], F32)
        ag = sb("ag", [P, UNROLL, D], F32)
        hid = sb("hid", [P, FC, UNROLL * P], F32)
        xt = hid[:, 0:2, :]
        pst, psh = ps("t", [P, 2, 512]), ps("h", [P, 4, 512])
        with nc.Block() as block:
            @block.sync
            def _(sp):
                sp.dma_start(w1[:, :, :], W1t.rearrange("(k p) f -> p k f", p=P)).then_inc(wloaded, 16)
                sp.dma_start(w2[:, :, :], W2t.rearrange("(k p) f -> p k f", p=P)).then_inc(wloaded, 16)
                with nc.allow_non_contiguous_dma("norm weights, one element to a partition"):
                    sp.dma_start(gb[:, 0, :], g1.rearrange("(k p) -> p k", p=P)).then_inc(wloaded, 16)
                    sp.dma_start(gb[:, 1, :], b1.rearrange("(k p) -> p k", p=P)).then_inc(wloaded, 16)
                sp.wait_ge(wloaded, 64)

            @block.vector
            def _(dve):
                dve.sem_inc(turned, 14)

                def body(g, s, j):
                    acc = c.acc[:, bass.ds(g * (UNROLL * D), UNROLL * D)].rearrange("p (k d) -> p k d", d=D)
                    dis = c.dis[:, bass.ds(g * UNROLL, UNROLL)].unsqueeze(2).broadcast_to([P, UNROLL, D])
                    dve.wait_ge(turned, g * UNROLL + 14)
                    dve.tensor_tensor(ag[:, :, :], acc, dis, ALU.mult).then_inc(scaled, 1)
                    for m in range(2 * FC):
                        f, half = m // 2, m % 2
                        n = LAST if isinstance(g, int) and half else NH
                        dve.wait_ge(kept, g * (2 * FC) + m + 5)
                        dve.bn_stats(st[:, f, bass.ds((2 * g + half) * 6, 6)],
                                     y1[:, f, bass.ds(g * (UNROLL * P) + half * NH, n)]).then_inc(statted, 1)
                groups(dve, body)

            @block.scalar
            def _(act):
                act.sem_inc(xt_made, 2)
                act.sem_inc(kept, 4)

                def body(g, s, j):
                    act.wait_ge(hidden, g * (2 * FC) + 4)
                    for k in range(UNROLL):
                        act.wait_ge(turned, g * UNROLL + k + 15)
                        nc.scalar.copy(xt[:, :, k * P:(k + 1) * P],
                                       pst[:, (s + k) % 2, 0:2 * P].rearrange("p (b n) -> p b n", b=2)).then_inc(xt_made, 1)
                    for m in range(2 * FC):
                        f, half = m // 2, m % 2
                        act.wait_ge(hidden, g * (2 * FC) + m + 5)
                        nc.scalar.copy(y1[:, f, bass.ds(g * (UNROLL * P) + half * NH, NH)], psh[:, m % 4, 0:NH]
                                       ).then_inc(kept, 1)
                groups(act, body)

            @block.tensor
            def _(pe):
                pe.sem_inc(hidden, 4)
                pe.wait_ge(wloaded, 64)

                def body(g, s, j):
                    pe.wait_ge(scaled, g + 1)
                    for k in range(UNROLL):
                        pe.wait_ge(xt_made, g * UNROLL + k + 1)
                        for b in range(2):
                            last = pe.transpose(pst[:, (s + k) % 2, b * P:(b + 1) * P], ag[:, k, b * P:(b + 1) * P],
                                                c.ident[:, :])
                        last.then_inc(turned, 1)
                    pe.wait_ge(xt_made, g * UNROLL + UNROLL + 2)
                    for m in range(2 * FC):
                        f, half = m // 2, m % 2
                        pe.wait_ge(kept, g * (2 * FC) + m + 1)
                        for b in range(2):
                            last = pe.matmul(psh[:, m % 4, 0:NH], w1[:, b, f * P:(f + 1) * P],
                                             xt[:, b, half * NH:(half + 1) * NH], start=(b == 0), stop=(b == 1))
                        last.then_inc(hidden, 1)
                groups(pe, body)

        psy = ps("y", [P, 2, 512])
        block = ctx.enter_context(nc.Block())

        @block.gpsimd
        def _(pool):
            pool.wait_ge(step, 2)
            pool.tensor_tensor(coef[:, 1, :], coef[:, 0, :], c.neghalf[:, 0:FC], ALU.pow).then_inc(rooted, 1)

        @block.vector
        def _(dve):
            n = [0]

            def do(ins):
                ins.then_inc(step, 1)
                n[0] += 1
                dve.wait_ge(step, n[0])

            dve.sem_inc(emptied, 2)
            for f in range(FC):
                last = dve.bn_aggr(mv[:, f, :], st[:, f, :])
            do(last)
            do(dve.tensor_scalar(coef[:, 0, :], mv[:, :, 1], EPS, None, ALU.add))
            dve.wait_ge(rooted, 1)
            do(dve.tensor_tensor(coef[:, 2, :], coef[:, 1, :], gb[:, 0, :], ALU.mult))
            do(dve.tensor_tensor(coef[:, 3, :], mv[:, :, 0], coef[:, 2, :], ALU.mult))
            do(dve.tensor_tensor(coef[:, 4, :], gb[:, 1, :], coef[:, 3, :], ALU.subtract))
            base = n[0]

            def body(g, s, j):
                for k in range(UNROLL):
                    if k == 0:
                        dve.wait_ge(stored[0], 16 * g + 16)
                    at = base + g * (UNROLL + 1)
                    dve.wait_ge(sent, g * UNROLL + k + 2)
                    dve.tensor_scalar(ag[:, k, :], psy[:, (s + k) % 2, 0:D], c.dis[:, bass.ds(g * UNROLL + k, 1)], None,
                                      ALU.mult).then_inc(step, 1)
                    dve.wait_ge(step, at + k + 1)
                    dve.sem_inc(emptied, 1)
                dve.sem_inc(passed, 1)
                dve.tensor_copy(c.acc[:, bass.ds(g * (UNROLL * D), UNROLL * D)],
                                ag[:, :, :].rearrange("p k d -> p (k d)")).then_inc(step, 1)
                dve.wait_ge(step, base + g * (UNROLL + 1) + UNROLL + 1)
                dve.sem_inc(out, 1)
            groups(dve, body)

        @block.sync
        def _(sp):
            sp.sem_inc(stored[0], 16)

            def store(g, s, j):
                sp.wait_ge(out, g + 1)
                sp.dma_start(rows(c.t_x, g, D), ag[:, :, :]).then_inc(stored[0], 16)
            groups(sp, store)
            sp.wait_ge(stored[0], 16 * 8)

        @block.scalar
        def _(act):
            act.wait_ge(step, 5)

            def body(g, s, j):
                act.wait_ge(sent, g * UNROLL + 1)
                for f in range(FC):
                    last = nc.scalar.activation(hid[:, f, :], y1[:, f, bass.ds(g * (UNROLL * P), UNROLL * P)], ACT.Relu,
                                                bias=coef[:, 4, f:f + 1], scale=coef[:, 2, f:f + 1])
                last.then_inc(relued, 1)
            groups(act, body)

        @block.tensor
        def _(pe):
            pe.sem_inc(sent, 1)

            def body(g, s, j):
                pe.wait_ge(relued, g + 1)
                for k in range(UNROLL):
                    pe.wait_ge(emptied, g * UNROLL + k + 1)
                    for f in range(FC):
                        last = pe.matmul(psy[:, (s + k) % 2, 0:D], hid[:, f, k * P:(k + 1) * P], w2[:, f, :], start=(f == 0),
                                         stop=(f == FC - 1))
                    last.then_inc(sent, 1)
            groups(pe, body)


def close_conv(nc, c, g2, b2, gate_w, gate_b):
    c.phase = "closeconv"
    sem = lambda name: nc_sem(nc, c, name)
    (loaded, scaled, meaned, squared, used, varied, step, rooted, lnstep, passed, normed, turned, xt_made, given,
     taken, done2) = (sem(s) for s in ("loaded scaled meaned squared used varied step rooted lnstep passed normed "
                                       "turned xt_made given taken done2").split())
    xin, stored = [sem("xin0"), sem("xin1")], [sem("stored0"), sem("stored1")]
    with ExitStack() as ctx:
        sb = lambda name, shape, dt: ctx.enter_context(nc.sbuf_tensor(f"closeconv_{name}", shape, dt))
        ps = lambda name, shape: ctx.enter_context(nc.psum_tensor(f"closeconv_ps_{name}", shape, F32))
        gam, bet, mean, rstd, nh = (sb(n, [P, D], F32) for n in ("gam", "bet", "bmean", "brstd", "nh"))
        gw, gb = sb("gw", [P, 2, X1], F32), sb("gb", [P, X1], F32)
        vones = sb("vones", [P, P], F32)
        sq = sb("sq", [P, 2, UNROLL, D], F32)
        ps_m, ps_v = ps("m", [P, 512]), ps("v", [P, 512])
        with nc.Block() as block:
            @block.sync
            def _(sp):
                for t, d in ((gam, g2), (bet, b2), (gb, gate_b)):
                    sp.dma_start(t[:, :], d.rearrange("(a e) -> a e", a=1).broadcast_to([P, d.shape[0]])
                                 ).then_inc(loaded, 16)
                sp.dma_start(gw[:, :, :], gate_w.rearrange("(k p) e -> p k e", p=P)).then_inc(loaded, 16)
                sp.wait_ge(loaded, 64)

            @block.tensor
            def _(pe):
                pe.sem_inc(used, 2)
                pe.wait_ge(step, 2)
                pe.matmul(ps_m[:, 0:D], c.zeros[:, 0:P], c.zeros[:, 0:D], start=True, stop=False)

                def add(g, s, j):
                    pe.wait_ge(scaled, g + 1)
                    for k in range(UNROLL):
                        last = pe.matmul(ps_m[:, 0:D], c.ones[:, :], sq[:, s, k, :], start=False, stop=False)
                    last.then_inc(used, 1)
                groups(pe, add)
                pe.matmul(ps_m[:, 0:D], c.zeros[:, 0:P], c.zeros[:, 0:D], start=False, stop=True).then_inc(meaned, 1)
                pe.matmul(ps_v[:, 0:D], c.zeros[:, 0:P], c.zeros[:, 0:D], start=True, stop=False)

                def add_squares(g, s, j):
                    pe.wait_ge(squared, g + 1)
                    for k in range(UNROLL):
                        real = vones if isinstance(g, int) and k == UNROLL - 1 else c.ones
                        last = pe.matmul(ps_v[:, 0:D], real[:, :], sq[:, s, k, :], start=False, stop=False)
                    last.then_inc(used, 1)
                groups(pe, add_squares)
                pe.matmul(ps_v[:, 0:D], c.zeros[:, 0:P], c.zeros[:, 0:D], start=False, stop=True).then_inc(meaned, 1)

            @block.gpsimd
            def _(pool):
                pool.wait_ge(varied, 1)
                pool.tensor_tensor(rstd[:, :], mean[:, :], nh[:, :], ALU.pow).then_inc(rooted, 1)

            @block.vector
            def _(dve):
                n = [0]

                def do(ins):
                    ins.then_inc(step, 1)
                    n[0] += 1
                    dve.wait_ge(step, n[0])

                do(dve.tensor_scalar(vones[:, :], c.ones[:, :], c.valid[:, 0:1], None, ALU.mult))
                do(dve.tensor_scalar(nh[:, :], c.zeros[:, 0:D], -0.5, None, ALU.add))
                view = lambda g: c.acc[:, bass.ds(g * (UNROLL * D), UNROLL * D)].rearrange("p (k d) -> p k d", d=D)

                def scale(g, s, j):
                    dis = c.dis[:, bass.ds(g * UNROLL, UNROLL)].unsqueeze(2).broadcast_to([P, UNROLL, D])
                    dve.wait_ge(used, g + 1)
                    dve.tensor_tensor(sq[:, s], view(g), dis, ALU.mult).then_inc(scaled, 1)
                    dve.wait_ge(scaled, g + 1)
                    dve.sem_inc(passed, 1)
                    dve.tensor_copy(view(g), sq[:, s]).then_inc(done2, 1)
                groups(dve, scale)
                dve.wait_ge(meaned, 1)
                dve.wait_ge(done2, GROUPS)
                do(dve.tensor_scalar(mean[:, :], ps_m[:, 0:D], 1.0 / N, None, ALU.mult))
                wide = mean[:, :].unsqueeze(1).broadcast_to([P, UNROLL, D])

                def square(g, s, j):
                    dve.wait_ge(used, g + GROUPS + 1)
                    dve.tensor_tensor(view(g), view(g), wide, ALU.subtract).then_inc(done2, 1)
                    dve.wait_ge(done2, g + GROUPS + 1)
                    dve.tensor_tensor(sq[:, s], view(g), view(g), ALU.mult).then_inc(squared, 1)
                groups(dve, square)
                dve.wait_ge(meaned, 2)
                dve.wait_ge(squared, GROUPS)
                dve.tensor_scalar(mean[:, :], ps_v[:, 0:D], 1.0 / N, EPS, ALU.mult, ALU.add).then_inc(varied, 1)
                dve.wait_ge(rooted, 1)
                dve.wait_ge(loaded, 64)
                do(dve.tensor_tensor(gam[:, :], gam[:, :], rstd[:, :], ALU.mult))

        x, xn, xr = (sb(n, [P, 2, UNROLL, D], F32) for n in ("x", "xn", "xr"))
        x3 = sq
        ln = ln_buffers(sb)
        xt = sb("xt", [P, 2, 2, P], F32)
        pst, psg = ps("t", [P, 2, 512]), ps("g", [P, 2, 512])
        block = ctx.enter_context(nc.Block())
        base = 4

        @block.sync
        def _(sp):
            def load(g, s, j):
                sp.wait_ge(normed, g + 1)
                sp.dma_start(xr[:, s], rows(c.x2, g, D)).then_inc(xin[s], 16)
                sp.dma_start(x[:, s], rows(c.xn2, g, D)).then_inc(xin[s], 16)
            groups(sp, load)

        @block.gpsimd
        def _(pool):
            groups(pool, lambda g, s, j: root(pool, c, lnstep, rooted, passed, g + 1, ln[2], ln[3], done=-LN_STEPS))

        @block.vector
        def _(dve):
            dve.sem_inc(normed, 2)
            view = lambda g: c.acc[:, bass.ds(g * (UNROLL * D), UNROLL * D)].rearrange("p (k d) -> p k d", d=D)
            wide = lambda t: t[:, :].unsqueeze(1).broadcast_to([P, UNROLL, D])

            def body(g, s, j):
                at = base + 4 * g

                def do(ins, n):
                    ins.then_inc(step, 1)
                    dve.wait_ge(step, at + n)
                dve.wait_ge(xin[s], 32 * j + 32)
                dve.wait_ge(stored[s], 32 * j + 32)
                dve.wait_ge(turned, g * UNROLL + UNROLL)
                do(dve.tensor_tensor(x3[:, s], view(g), wide(gam), ALU.mult), 1)
                do(dve.tensor_tensor(x3[:, s], x3[:, s], wide(bet), ALU.add), 2)
                do(dve.tensor_tensor(x3[:, s], x3[:, s], x[:, s], ALU.add), 3)
                do(dve.scalar_tensor_tensor(out=x3[:, s].rearrange("p k d -> p (k d)"),
                                            in0=x3[:, s].rearrange("p k d -> p (k d)"), scalar=0.0,
                                            in1=xr[:, s].rearrange("p k d -> p (k d)"), op0=ALU.max, op1=ALU.add), 4)
                normalise(dve, lnstep, rooted, g + 1, x3[:, s], xn[:, s], *ln, done=g * LN_STEPS)
                dve.sem_inc(normed, 1)
                dve.wait_ge(given, g + 1)
                dve.tensor_tensor(c.logit[:, bass.ds(g * (UNROLL * X1), UNROLL * X1)].rearrange("p (k e) -> p k e", e=X1),
                                  psg[:, s, 0:UNROLL * X1].rearrange("p (k e) -> p k e", e=X1),
                                  gb[:, :].unsqueeze(1).broadcast_to([P, UNROLL, X1]), ALU.add).then_inc(taken, 1)
            groups(dve, body)
            dve.wait_ge(taken, GROUPS)

        @block.scalar
        def _(act):
            act.sem_inc(xt_made, 2)
            act.sem_inc(stored[0], 32)
            act.sem_inc(stored[1], 32)

            def body(g, s, j):
                act.wait_ge(normed, g + 3)
                act.dma_start(rows(c.x3, g, D), x3[:, s]).then_inc(stored[s], 16)
                act.dma_start(rows(c.xn3, g, D), xn[:, s]).then_inc(stored[s], 16)
                for k in range(UNROLL):
                    act.wait_ge(turned, g * UNROLL + k + 15)
                    nc.scalar.copy(xt[:, (s + k) % 2], pst[:, (s + k) % 2, 0:2 * P].rearrange("p (b n) -> p b n", b=2)
                                   ).then_inc(xt_made, 1)
            groups(act, body)
            act.wait_ge(stored[0], 32 * 5)
            act.wait_ge(stored[1], 32 * 4)

        @block.tensor
        def _(pe):
            pe.sem_inc(turned, 14)

            def body(g, s, j):
                pe.wait_ge(normed, g + 3)
                for k in range(UNROLL):
                    q = (s + k) % 2
                    pe.wait_ge(xt_made, g * UNROLL + k + 1)
                    for b in range(2):
                        last = pe.transpose(pst[:, q, b * P:(b + 1) * P], xn[:, s, k, b * P:(b + 1) * P], c.ident[:, :])
                    last.then_inc(turned, 1)
                    pe.wait_ge(xt_made, g * UNROLL + k + 3)
                    for b in range(2):
                        last = pe.matmul(psg[:, s, k * X1:(k + 1) * X1], xt[:, q, b, :], gw[:, b, :], start=(b == 0),
                                         stop=(b == 1))
                last.then_inc(given, 1)
            groups(pe, body)


def route(nc, c):
    c.phase = "route"
    sem = lambda name: nc_sem(nc, c, name)
    step, given, peed = (sem(s) for s in "step given peed".split())
    T8 = TILES * X1
    with ExitStack() as ctx:
        sb = lambda name, shape, dt: ctx.enter_context(nc.sbuf_tensor(f"route_{name}", shape, dt))
        p, e, oh, inc, tot, before, tmp = (sb(n, [P, T8], F32) for n in "p e oh inc tot before tmp".split())
        mx, sm, pm, idx, pos, kept, to, node = (sb(n, [P, TILES], F32) for n in "mx sm pm idx pos kept to node".split())
        ps1, ps2 = (ctx.enter_context(nc.psum_tensor(f"route_ps{m}", [P, 512], F32)) for m in range(2))
        block = ctx.enter_context(nc.Block())
        te = lambda t: t[:, :].rearrange("p (t e) -> p t e", e=X1)
        et = lambda t: t[:, :].rearrange("p (e t) -> p e t", e=X1)
        w8 = lambda t: t[:, :].unsqueeze(2).broadcast_to([P, TILES, X1])

        @block.gpsimd
        def _(pool):
            nc.gpsimd.iota(node[:, :], [[P, TILES]], base=0, channel_multiplier=1,
                           allow_small_or_imprecise_dtypes=True).then_inc(peed, 1)

        @block.scalar
        def _(act):
            act.wait_ge(given, 1)
            nc.scalar.activation(e[:, :], p[:, :], ACT.Exp).then_inc(peed, 1)

        @block.tensor
        def _(pe):
            pe.wait_ge(given, 2)
            pe.matmul(ps1[:, 0:T8], c.below[:, :], oh[:, :], start=True, stop=True)
            pe.matmul(ps2[:, 0:T8], c.ones[:, :], oh[:, :], start=True, stop=True).then_inc(peed, 1)

        @block.vector
        def _(dve):
            n = [0]

            def do(ins):
                ins.then_inc(step, 1)
                n[0] += 1
                dve.wait_ge(step, n[0])

            do(dve.tensor_reduce(mx[:, :], te(c.logit), AX.X, ALU.max))
            do(dve.tensor_tensor(te(p), te(c.logit), w8(mx), ALU.subtract))
            dve.sem_inc(given, 1)
            dve.wait_ge(peed, 2)
            do(dve.tensor_reduce(sm[:, :], te(e), AX.X, ALU.add))
            do(dve.reciprocal(sm[:, :], sm[:, :]))
            do(dve.tensor_tensor(te(p), te(e), w8(sm), ALU.mult))
            do(dve.tensor_reduce(pm[:, :], te(p), AX.X, ALU.max))
            do(dve.tensor_tensor(te(oh), te(p), w8(pm), ALU.is_lt))
            eight = c.iota[:, 0:X1].unsqueeze(1).broadcast_to([P, TILES, X1])
            do(dve.tensor_scalar(oh[:, :], oh[:, :], 100.0, None, ALU.mult))
            do(dve.tensor_tensor(te(tmp), te(oh), eight, ALU.add))
            do(dve.tensor_reduce(idx[:, :], te(tmp), AX.X, ALU.min))
            do(dve.tensor_tensor(te(oh), w8(idx), eight, ALU.is_equal))
            do(dve.tensor_scalar(oh[:, T8 - X1:T8], oh[:, T8 - X1:T8], c.valid[:, 0:1], None, ALU.mult))
            dve.sem_inc(given, 1)
            dve.wait_ge(peed, 3)
            do(dve.tensor_copy(et(tot), ps2[:, 0:T8].rearrange("p (t e) -> p e t", e=X1)))
            for x in range(X1):
                last = dve.tensor_tensor_scan(inc[:, x * TILES:(x + 1) * TILES], tot[:, x * TILES:(x + 1) * TILES],
                                              c.zeros[:, 0:TILES], 0.0, ALU.add, ALU.add)
            do(last)
            do(dve.tensor_tensor(before[:, :], inc[:, :], tot[:, :], ALU.subtract))
            do(dve.tensor_tensor(te(tmp), before[:, :].rearrange("p (e t) -> p t e", e=X1), te(ps1[:, 0:T8]), ALU.add))
            do(dve.tensor_tensor(tmp[:, :], tmp[:, :], oh[:, :], ALU.mult))
            do(dve.tensor_reduce(pos[:, :], te(tmp), AX.X, ALU.add))
            do(dve.tensor_scalar(kept[:, :], pos[:, :], float(CAP), None, ALU.is_lt))
            do(dve.tensor_scalar(kept[:, TILES - 1:TILES], kept[:, TILES - 1:TILES], c.valid[:, 0:1], None, ALU.mult))
            do(dve.tensor_tensor(c.gate[:, :], pm[:, :], kept[:, :], ALU.mult))
            do(dve.tensor_scalar(pos[:, :], pos[:, :], float(CAP - 1), None, ALU.min))
            do(dve.tensor_scalar(sm[:, :], idx[:, :], float(CAP), None, ALU.mult))
            do(dve.tensor_tensor(c.take[:, :], pos[:, :], sm[:, :], ALU.add))
            do(dve.tensor_scalar(idx[:, :], idx[:, :], float(SLOTS), None, ALU.mult))
            do(dve.tensor_tensor(pos[:, :], pos[:, :], idx[:, :], ALU.add))
            do(dve.tensor_scalar(node[:, :], node[:, :], float(X1 * SLOTS), None, ALU.add))
            do(dve.tensor_tensor(to[:, :], pos[:, :], node[:, :], ALU.subtract))
            do(dve.tensor_tensor(to[:, :], to[:, :], kept[:, :], ALU.mult))
            do(dve.tensor_tensor(c.put[:, :], to[:, :], node[:, :], ALU.add))


def dispatch(nc, c):
    c.phase = "dispatch"
    sem = lambda name: nc_sem(nc, c, name)
    copied, passed, free = (sem(s) for s in "copied passed free".split())
    xin, sent = [sem("xin0"), sem("xin1")], [sem("sent0"), sem("sent1")]
    with ExitStack() as ctx:
        sb = lambda name, shape, dt: ctx.enter_context(nc.sbuf_tensor(f"dispatch_{name}", shape, dt))
        x = sb("x", [P, 2, UNROLL, D], F32)
        few = sb("few", [P, 2, UNROLL], I32)
        block = ctx.enter_context(nc.Block())

        @block.sync
        def _(sp):
            def load(g, s, j):
                sp.wait_ge(free, g + 1)
                sp.dma_start(x[:, s], rows(c.xn3, g, D)).then_inc(xin[s], 16)
            groups(sp, load)

        @block.gpsimd
        def _(pool):
            pool.sem_inc(free, 2)

            def send(g, s, j):
                pool.wait_ge(xin[s], 16 * j + 16)
                pool.sem_inc(passed, 1)
                pool.tensor_copy(few[:, s, :], c.put[:, bass.ds(g * UNROLL, UNROLL)]).then_inc(copied, 1)
                pool.wait_ge(copied, g + 1)
                pool.sem_inc(passed, 1)
                for k in range(UNROLL):
                    pool.indirect_dma_start(out=c.slots_in[:, :], in_=x[:, s, k, :], in_offset=None,
                                            out_offset=bass.IndirectOffsetOnAxis(ap=few[:, s, k:k + 1], axis=0)
                                            ).then_inc(sent[s], 16)
                pool.wait_ge(sent[s], 16 * UNROLL * j + 16 * UNROLL)
                pool.sem_inc(free, 1)
            groups(pool, send)


def experts1(nc, c, w1, b1, w2, b2):
    c.phase = "experts1"
    FC, TC = F1 // P, SLOTS // P
    HALVES = ((0, 489), (489, CAP))
    LASTM = CAP - (TC - 1) * P
    sem = lambda name: nc_sem(nc, c, name)
    (turned, xt_made, hidden, relued, mixed, emptied, wfree, yfree, passed) = (
        sem(s) for s in "turned xt_made hidden relued mixed emptied wfree yfree passed".split())
    loaded, stored = [sem("loaded0"), sem("loaded1")], [sem("stored0"), sem("stored1")]
    with ExitStack() as ctx:
        sb = lambda name, shape, dt: ctx.enter_context(nc.sbuf_tensor(f"experts1_{name}", shape, dt))
        ps = lambda name, shape: ctx.enter_context(nc.psum_tensor(f"experts1_ps_{name}", shape, F32))
        x = sb("x", [P, 2, TC, D], F32)
        w1s, w2s = sb("w1", [P, 2, 2, F1], F32), sb("w2", [P, 2, FC, D], F32)
        b1s, b2s = sb("b1", [P, 2, FC], F32), sb("b2", [P, 2, D], F32)
        xt = sb("xt", [P, 2, SLOTS], F32)
        hid = sb("hid", [P, FC, SLOTS], F32)
        y = sb("y", [P, 2, TC, D], F32)
        pst, psh, psy = ps("t", [P, 2, 512]), ps("h", [P, 2, 512]), ps("y", [P, 2, 512])
        block = ctx.enter_context(nc.Block())

        def experts(eng, body):
            with eng.Fori(0, X1 // 2) as i:
                body(2 * i, 0, i)
                body(2 * i + 1, 1, i)

        @block.sync
        def _(sp):
            def load(e, s, j):
                sp.wait_ge(wfree, e + 1)
                one = bass.ds(e, 1)
                sp.dma_start(x[:, s], c.slots_in[bass.ds(e * SLOTS, SLOTS), :].rearrange("(k p) d -> p k d", p=P)
                             ).then_inc(loaded[s], 16)
                sp.dma_start(w1s[:, s], w1[one].rearrange("a (k p) f -> p (a k) f", p=P)).then_inc(loaded[s], 16)
                sp.dma_start(w2s[:, s], w2[one].rearrange("a (k p) f -> p (a k) f", p=P)).then_inc(loaded[s], 16)
                with nc.allow_non_contiguous_dma("a bias, one element to a partition"):
                    sp.dma_start(b1s[:, s, :], b1[one].rearrange("a (k p) -> p (a k)", p=P)).then_inc(loaded[s], 16)
                sp.dma_start(b2s[:, s, :], b2[one].broadcast_to([P, D])).then_inc(loaded[s], 16)
            experts(sp, load)

        @block.tensor
        def _(pe):
            pe.sem_inc(hidden, 2)
            pe.sem_inc(mixed, 1)

            def body(e, s, j):
                pe.wait_ge(loaded[s], 80 * j + 80)
                for k in range(TC):
                    pe.wait_ge(xt_made, e * TC + k + 1)
                    for b in range(2):
                        last = pe.transpose(pst[:, k % 2, b * P:(b + 1) * P], x[:, s, k, b * P:(b + 1) * P],
                                            c.ident[:, :])
                    last.then_inc(turned, 1)
                pe.wait_ge(xt_made, e * TC + TC + 2)
                for m in range(2 * FC):
                    f, (lo, hi) = m // 2, HALVES[m % 2]
                    pe.wait_ge(relued, e * (2 * FC) + m + 1)
                    for b in range(2):
                        last = pe.matmul(psh[:, m % 2, 0:hi - lo], w1s[:, s, b, f * P:(f + 1) * P], xt[:, b, lo:hi],
                                         start=(b == 0), stop=(b == 1))
                    last.then_inc(hidden, 1)
                pe.wait_ge(relued, e * (2 * FC) + 2 * FC + 2)
                for k in range(TC):
                    n = LASTM if k == TC - 1 else P
                    pe.wait_ge(emptied, e * TC + k + 1)
                    for f in range(FC):
                        last = pe.matmul(psy[0:n, k % 2, 0:D], hid[:, f, k * P:k * P + n], w2s[:, s, f, :],
                                         start=(f == 0), stop=(f == FC - 1))
                    last.then_inc(mixed, 1)
            experts(pe, body)

        @block.scalar
        def _(act):
            act.sem_inc(xt_made, 2)
            act.sem_inc(relued, 2)

            def body(e, s, j):
                act.wait_ge(loaded[s], 80 * j + 80)
                act.wait_ge(hidden, e * (2 * FC) + 2)
                for k in range(TC):
                    act.wait_ge(turned, e * TC + k + 1)
                    nc.scalar.copy(xt[:, :, k * P:(k + 1) * P],
                                   pst[:, k % 2, 0:2 * P].rearrange("p (b n) -> p b n", b=2)).then_inc(xt_made, 1)
                act.wait_ge(mixed, e * TC + 1)
                for m in range(2 * FC):
                    f, (lo, hi) = m // 2, HALVES[m % 2]
                    act.wait_ge(hidden, e * (2 * FC) + m + 3)
                    nc.scalar.activation(hid[:, f, lo:hi], psh[:, m % 2, 0:hi - lo], ACT.Relu,
                                         bias=b1s[:, s, f:f + 1]).then_inc(relued, 1)
            experts(act, body)

        @block.vector
        def _(dve):
            dve.sem_inc(emptied, 2)
            dve.sem_inc(wfree, 2)

            def body(e, s, j):
                dve.wait_ge(loaded[s], 80 * j + 80)
                dve.wait_ge(yfree, e + 1)
                for k in range(TC):
                    n = LASTM if k == TC - 1 else P
                    dve.wait_ge(mixed, e * TC + k + 2)
                    last = dve.tensor_tensor(y[0:n, s, k, :], psy[0:n, k % 2, 0:D], b2s[0:n, s, :], ALU.add)
                    last.then_inc(emptied, 1)
                dve.wait_ge(emptied, e * TC + TC + 2)
                dve.sem_inc(wfree, 1)
            experts(dve, body)

        @block.gpsimd
        def _(pool):
            pool.sem_inc(yfree, 2)

            def store(e, s, j):
                pool.wait_ge(wfree, e + 3)
                pool.sem_inc(passed, 1)
                pool.dma_start(c.slots_out[bass.ds(e * CAP, (TC - 1) * P), :].rearrange("(k p) d -> p k d", p=P),
                               y[:, s, 0:TC - 1, :]).then_inc(stored[s], 16)
                pool.dma_start(c.slots_out[bass.ds(e * CAP + (TC - 1) * P, LASTM), :], y[0:LASTM, s, TC - 1, :]
                               ).then_inc(stored[s], 16)
                pool.wait_ge(stored[s], 32 * j + 32)
                pool.sem_inc(yfree, 1)
            experts(pool, store)


def combine(nc, c, out):
    c.phase = "combine"
    BIG = 3.4028234663852886e38
    sem = lambda name: nc_sem(nc, c, name)
    copied, passed, summed, step = (sem(s) for s in "copied passed summed step".split())
    xin, got, stored = ([sem(f"{n}0"), sem(f"{n}1")] for n in ("xin", "got", "stored"))
    with ExitStack() as ctx:
        sb = lambda name, shape, dt: ctx.enter_context(nc.sbuf_tensor(f"combine_{name}", shape, dt))
        x, y, z, o = (sb(n, [P, 2, UNROLL * D], F32) for n in "xyzo")
        fill = sb("fill", [P, 3, UNROLL * D], F32)
        mask = sb("mask", [P, 2, 3, UNROLL * D], I32)
        few = sb("few", [P, 2, UNROLL], I32)
        block = ctx.enter_context(nc.Block())
        tiles = lambda t, s: t[:, s, :].rearrange("p (k d) -> p k d", d=D)

        @block.sync
        def _(sp):
            def load(g, s, j):
                sp.wait_ge(summed, g + 1)
                sp.dma_start(tiles(x, s), rows(c.x3, g, D)).then_inc(xin[s], 16)
            groups(sp, load)

        @block.gpsimd
        def _(pool):
            def fetch(g, s, j):
                pool.wait_ge(summed, g + 1)
                pool.sem_inc(passed, 1)
                pool.tensor_copy(few[:, s, :], c.take[:, bass.ds(g * UNROLL, UNROLL)]).then_inc(copied, 1)
                pool.wait_ge(copied, g + 1)
                pool.sem_inc(passed, 1)
                for k in range(UNROLL):
                    pool.indirect_dma_start(out=y[:, s, k * D:(k + 1) * D], out_offset=None, in_=c.slots_out[:, :],
                                            in_offset=bass.IndirectOffsetOnAxis(ap=few[:, s, k:k + 1], axis=0)
                                            ).then_inc(got[s], 16)
            groups(pool, fetch)

        @block.vector
        def _(dve):
            dve.sem_inc(summed, 2)
            dve.memset(fill[:, 0, :], 0.0).then_inc(step, 1)
            dve.memset(fill[:, 1, :], 1e4).then_inc(step, 1)
            dve.memset(fill[:, 2, :], -1e4).then_inc(step, 1)
            dve.wait_ge(step, 3)

            def body(g, s, j):
                def do(ins, n):
                    ins.then_inc(step, 1)
                    dve.wait_ge(step, 8 * g + 3 + n)
                gate = c.gate[:, bass.ds(g * UNROLL, UNROLL)].unsqueeze(2).broadcast_to([P, UNROLL, D])
                dve.wait_ge(got[s], 16 * UNROLL * j + 16 * UNROLL)
                dve.wait_ge(xin[s], 16 * j + 16)
                dve.wait_ge(stored[s], 16 * j + 16)
                do(dve.tensor_tensor(tiles(z, s), tiles(y, s), gate, ALU.mult), 1)
                do(dve.tensor_tensor(mask[:, s, 0, :], z[:, s], z[:, s], ALU.not_equal), 2)
                do(dve.tensor_scalar(mask[:, s, 1, :], z[:, s], BIG, None, ALU.is_gt), 3)
                do(dve.tensor_scalar(mask[:, s, 2, :], z[:, s], -BIG, None, ALU.is_lt), 4)
                for m in range(3):
                    dve.sem_inc(passed, 1)
                    dve.copy_predicated(z[:, s], mask[:, s, m, :], fill[:, m, :]).then_inc(step, 1)
                    dve.wait_ge(step, 8 * g + 8 + m)
                do(dve.tensor_tensor(o[:, s], z[:, s], x[:, s], ALU.add), 8)
                dve.sem_inc(summed, 1)
            groups(dve, body)

        @block.scalar
        def _(act):
            act.sem_inc(stored[0], 16)
            act.sem_inc(stored[1], 16)

            def store(g, s, j):
                act.wait_ge(summed, g + 3)
                if isinstance(g, int):
                    at = g * UNROLL * P
                    full = (N - at) // P
                    act.dma_start(out[at:at + full * P, :].rearrange("(k p) d -> p k d", p=P), tiles(o, s)[:, 0:full]
                                  ).then_inc(stored[s], 16)
                    act.dma_start(out[at + full * P:N, :], tiles(o, s)[0:(N - at) % P, full, :]
                                  ).then_inc(stored[s], 16)
                else:
                    act.dma_start(rows(out, g, D), tiles(o, s)).then_inc(stored[s], 16)
            groups(act, store)
            act.wait_ge(stored[0], 16 * 6)
            act.wait_ge(stored[1], 16 * 4)



def build(nc, a, out):
    c = Ctx()
    with ExitStack() as ctx:
        c.ctx = ctx
        c.phase, c.sems = "setup", []
        dram = lambda name, shape, dt=F32: nc.dram_tensor(name, shape, dt, kind="Internal").ap()
        sb = lambda name, shape, dt: ctx.enter_context(nc.sbuf_tensor(name, shape, dt))
        c.x0, c.x1, c.xn1, c.x2, c.xn2, c.x3, c.xn3, c.t_x = (
            dram(name, [NP, D]) for name in ("x0", "x1", "xn1", "x2", "xn2", "x3", "xn3", "t_x"))
        c.t_h, c.t_hr = dram("t_h", [NP, D + 4]), dram("t_hr", [NP, 4])
        c.slots_in = dram("slots_in", [X1 * SLOTS + NP, D])
        c.slots_out = dram("slots_out", [X1 * CAP, D])
        setup(nc, c, ctx, a["x"])
        c.idx_d, c.loc_d, c.buc_d = sb("idx_d", [P, ET], I32), sb("loc_d", [P, ET], F32), sb("buc_d", [1, ET], I32)
        c.deg, c.dis = sb("deg", [P, TILES], F32), sb("dis", [P, TILES], F32)
        c.colsum, c.share, c.chosen = sb("colsum", [P, 2], F32), sb("share", [P, 2], F32), sb("chosen", [1, 2], I32)
        c.logit = sb("logit", [P, TILES * X1], F32)
        c.put, c.take, c.gate = sb("put", [P, TILES], I32), sb("take", [P, TILES], I32), sb("gate", [P, TILES], F32)
        sort_edges(nc, c, a["dst"], a["src"], c.idx_d, c.loc_d, c.buc_d, c.deg, "by_dst")
        with ExitStack() as att:
            sa = lambda name, shape, dt: att.enter_context(nc.sbuf_tensor(name, shape, dt))
            c.idx_s, c.loc_s, c.buc_s = sa("idx_s", [P, ET], I32), sa("loc_s", [P, ET], F32), sa("buc_s", [1, ET], I32)
            sort_edges(nc, c, a["src"], a["dst"], c.idx_s, c.loc_s, c.buc_s, None, "by_src")
            c.hlm = sa("hlm", [P, TILES * 8], F32)
            c.acc = sa("acc_heads", [P, TILES * (D + 4)], F32)
            project_heads(nc, c, a["L0_gnn_W"], a["L0_gnn_a_l"], a["L0_gnn_a_r"])
            neighbour_max(nc, c)
            attend(nc, c)
            close_attention(nc, c)
        recycle(nc, c)
        choose_experts(nc, c, a["L0_ffn_Wr"], a["L0_ffn_br"])
        experts0(nc, c, a["L0_ffn_W1"], a["L0_ffn_b1"], a["L0_ffn_W2"], a["L0_ffn_b2"], a["L0_ffn_gamma"],
                 a["L0_ffn_beta"])
        with ExitStack() as conv:
            c.acc = conv.enter_context(nc.sbuf_tensor("acc_conv", [P, TILES * D], F32))
            prepare_conv(nc, c)
            aggregate(nc, c, "conv1", c.t_x)
            conv_hidden(nc, c, a["L1_gnn_W1"], a["L1_gnn_g1"], a["L1_gnn_b1"], a["L1_gnn_W2"])
            aggregate(nc, c, "conv2", c.t_x)
            recycle(nc, c)
            close_conv(nc, c, a["L1_gnn_g2"], a["L1_gnn_b2"], a["L1_ffn_gate_w"], a["L1_ffn_gate_b"])
        route(nc, c)
        dispatch(nc, c)
        experts1(nc, c, a["L1_ffn_w1"], a["L1_ffn_b1"], a["L1_ffn_w2"], a["L1_ffn_b2"])
        combine(nc, c, out)


_INS = ['x', 'src', 'dst', 'L0_gnn_W', 'L0_gnn_a_l', 'L0_gnn_a_r', 'L0_ffn_Wr', 'L0_ffn_br', 'L0_ffn_W1',
        'L0_ffn_b1', 'L0_ffn_W2', 'L0_ffn_b2', 'L0_ffn_gamma', 'L0_ffn_beta', 'L1_gnn_W1', 'L1_gnn_g1', 'L1_gnn_b1',
        'L1_gnn_W2', 'L1_gnn_g2', 'L1_gnn_b2', 'L1_ffn_gate_w', 'L1_ffn_gate_b', 'L1_ffn_w1', 'L1_ffn_b1',
        'L1_ffn_w2', 'L1_ffn_b2']
_TURNED = ('L1_gnn_W1', 'L1_gnn_W2')
_OUTS = [((N, D), 'float32')]


def kernel(**inputs):
    import numpy as _np
    import concourse.bacc as _bacc
    from concourse import mybir as _mybir
    from concourse.bass_utils import run_bass_kernel_spmd as _run

    nc = _bacc.Bacc("TRN2", target_bir_lowering=False, num_devices=1)
    arrays, args = {}, {}
    for name in _INS:
        a = _np.asarray(inputs[name])
        a = _np.ascontiguousarray(a.T if name in _TURNED else a)
        arrays[f"in_{name}_dram"] = a
        args[name] = nc.dram_tensor(f"in_{name}_dram", a.shape, _mybir.dt.from_np(a.dtype), kind="ExternalInput").ap()
    outs = []
    for i, (shape, dtype) in enumerate(_OUTS):
        dt = _mybir.dt.from_np(_np.dtype(dtype))
        outs.append(nc.dram_tensor(f"out_{i}_dram", shape, dt, kind="ExternalOutput").ap())
    build(nc, args, outs[0])
    r = _run(nc, [arrays], core_ids=[0])
    got = tuple(r.results[0][f"out_{i}_dram"] for i in range(len(_OUTS)))
    return got[0]
```

```python
from contextlib import ExitStack

import concourse.bass as bass
from concourse import mybir

ALU = mybir.AluOpType
ACT = mybir.ActivationFunctionType
AX = mybir.AxisListType
F32 = mybir.dt.float32
F16 = mybir.dt.float16
I32 = mybir.dt.int32

P = 128
N = 6250
D = 256
TILES = 49
NP = TILES * P
PADS = NP - N
UNROLL = 7
GROUPS = TILES // UNROLL
E = 100000
EP, EC = 125, 800
ET = 832
HALF = ET // 2
RING = 16
HEADS, HD = 4, 64
ZROW = NP - 1
LOW = -3.0e38
F0, X0 = 512, 8
F1, X1 = 1024, 8
CAP0 = 977.0
CAP = 977
IC = 512
SLOTS = 1024
EPS = 1e-5
assert E == EP * EC and (E + TILES * (P - 1)) // P < ET


class Ctx:
    pass


def groups(eng, body):
    with eng.Fori(0, GROUPS // 2) as i:
        body(2 * i, 0, i)
        body(2 * i + 1, 1, i)
    body(GROUPS - 1, 0, GROUPS // 2)


def rows(dram, g, width):
    return dram[bass.ds(g * (UNROLL * P), UNROLL * P), 0:width].rearrange("(k p) d -> p k d", p=P)


def setup(nc, c, ctx, x):
    sb = lambda name, shape, dt: ctx.enter_context(nc.sbuf_tensor(name, shape, dt))
    c.iota = sb("iota", [P, ET], F32)
    c.iota16 = sb("iota16", [P, ET], F16)
    c.pidx = sb("pidx", [P, 1], F32)
    c.ident = sb("ident", [P, P], F32)
    c.ones = sb("ones", [P, P], F32)
    c.below = sb("below", [P, P], F32)
    c.upto = sb("upto", [P, P], F32)
    c.zeros = sb("zeros", [P, EC], F32)
    c.zeros16 = sb("zeros16", [P, HALF], F16)
    c.neghalf = sb("neghalf", [P, UNROLL], F32)
    c.valid = sb("valid", [P, 1], F32)
    c.headsel = sb("headsel", [4, HEADS, P], F32)
    made = nc_sem(nc, c, "consts_made")
    copied = nc_sem(nc, c, "x_copied")
    with nc.Block() as block:
        @block.gpsimd
        def _(pool):
            nc.gpsimd.iota(c.iota[:, :], [[1, ET]], base=0, channel_multiplier=0,
                           allow_small_or_imprecise_dtypes=True).then_inc(made, 1)
            nc.gpsimd.iota(c.iota16[:, :], [[1, ET]], base=0, channel_multiplier=0,
                           allow_small_or_imprecise_dtypes=True).then_inc(made, 1)
            nc.gpsimd.iota(c.pidx[:, :], [[1, 1]], base=0, channel_multiplier=1,
                           allow_small_or_imprecise_dtypes=True).then_inc(made, 1)
            nc.gpsimd.memset(c.neghalf[:, :], -0.5).then_inc(made, 1)
            nc.gpsimd.memset(c.ones[:, :], 1.0).then_inc(made, 1)
            nc.gpsimd.memset(c.zeros[:, :], 0.0).then_inc(made, 1)
            nc.gpsimd.memset(c.zeros16[:, :], 0.0).then_inc(made, 1)

        @block.vector
        def _(dve):
            dve.wait_ge(made, 7)
            dve.tensor_scalar(c.ident[:, :], c.iota[:, 0:P], c.pidx[:, 0:1], None, ALU.is_equal)
            dve.tensor_scalar(c.valid[:, :], c.pidx[:, :], float(P - PADS), None, ALU.is_lt)
            dve.tensor_scalar(c.below[:, :], c.iota[:, 0:P], c.pidx[:, 0:1], None, ALU.is_gt)
            dve.tensor_scalar(c.upto[:, :], c.iota[:, 0:P], c.pidx[:, 0:1], None, ALU.is_ge)
            for h in range(HEADS):
                dve.tensor_scalar(c.headsel[:, h, :], c.ones[0:4, :], c.pidx[0:4, 0:1], float(h), ALU.mult,
                                  ALU.is_equal)

        @block.sync
        def _(sp):
            sp.dma_start(c.x0[0:N, :], x[:, :]).then_inc(copied, 16)
            sp.wait_ge(made, 7)
            sp.dma_start(c.x0[N:NP, :], c.zeros[0:PADS, 0:D]).then_inc(copied, 16)
            sp.dma_start(c.slots_in[0:X1 * SLOTS, :].rearrange("(p r) d -> p r d", p=P),
                         c.zeros[:, 0:D].unsqueeze(1).broadcast_to([P, X1 * SLOTS // P, D])).then_inc(copied, 16)
            sp.wait_ge(copied, 48)


def nc_sem(nc, c, name):
    c.sems.append(nc.alloc_semaphore(name=f"{c.phase}_{name}"))
    return c.sems[-1]


def recycle(nc, c):
    nc.clear_and_free_semaphores(c.sems)
    nc.all_engine_barrier()
    c.sems = []


def skewed(eng, stages, total, u):
    for t in range(u):
        for lag, body in stages:
            if t >= lag:
                body(t - lag, (t - lag) % u, (t - lag) // u)
    with eng.Fori(1, total // u) as i:
        for k in range(u):
            for lag, body in stages:
                body(i * u + (k - lag), (k - lag) % u, i - 1 if k < lag else i)
    for t in range(total, total + max(lag for lag, _ in stages)):
        for lag, body in stages:
            if t - lag < total:
                body(t - lag, (t - lag) % u, (t - lag) // u)


def sort_edges(nc, c, src, dst):
    c.phase = "sort"
    sem = lambda name: nc_sem(nc, c, name)
    place_ready, onehot, paid, spread, placed, unpacked = (
        sem(s) for s in "place_ready onehot paid spread placed unpacked".split())
    cleared, emptied_table, positioned, copied, passed, returned = (
        sem(s) for s in "cleared emptied_table positioned copied passed returned".split())
    sent = [sem(f"sent{s}") for s in range(4)]
    loaded = {"dst": sem("loaded_dst"), "src": sem("loaded_src")}
    split, counted, summed, based, ended, table, masked, scanned, picked, gathered_pos, usedhit, pos_whole = (
        {t: sem(f"{s}_{t}") for t in ("dst", "src")}
        for s in ("split counted summed based ended table masked scanned picked gathered_pos usedhit "
                  "pos_whole").split())
    U = 4
    B = 10
    HC = EC // 2
    with ExitStack() as ctx:
        sb = lambda name, shape, dt: ctx.enter_context(nc.sbuf_tensor(f"sort_{name}", shape, dt))
        ps = lambda name, shape: ctx.enter_context(nc.psum_tensor(f"sort_{name}", shape, F32))
        keys = {t: sb(f"key_{t}", [EP, EC], I32) for t in ("src", "dst")}
        others = {t: sb(f"oth_{t}", [EP, EC], I32) for t in ("src", "dst")}
        tmp_i = sb("tmp_i", [EP, EC], I32)
        pay1, pay2 = sb("pay1", [EP, EC], F32), sb("pay2", [EP, EC], F32)
        hi16, mask = sb("hi16", [EP, EC], F16), sb("mask", [EP, EC], F16)
        cum, hit = sb("cum", [EP, EC], F32), sb("hit", [EP, 2, EC], F32)
        plo, ptile = sb("plo", [EP, EC], F32), sb("ptile", [EP, EC], F32)
        dst_lo, dst_hi = sb("dst_lo", [EP, EC], F32), sb("dst_hi", [EP, EC], F32)
        tot = sb("tot", [EP, TILES], F32)
        small_i = sb("small_i", [P, 2, TILES], I32)
        nt, inc, off = (sb(n, [P, TILES], F32) for n in ("nt", "inc", "off"))
        col_i, col_f, endc = sb("col_i", [TILES, 2], I32), sb("col_f", [TILES, 1], F32), sb("endc", [TILES, 1], F32)
        ge = sb("ge", [TILES, ET], F32)
        lo1 = sb("lo1", [EP, U, P], F16)
        l12 = sb("l12", [EP, U, 2, P], F16)
        hot = sb("hot", [EP, U, ET], F16)
        dlo, dhi = sb("dlo", [EP, U, P], F16), sb("dhi", [EP, U, TILES], F16)
        u1, u2, u3 = (sb(n, [P, ET], I32) for n in ("u1", "u2", "u3"))
        trio = sb("trio", [EP, 3, EC], I32)
        few = sb("few", [EP, 4, B, 3], I32)
        back = sb("back", [P, ET, 2], I32)
        accs = [ps("acc1", [P, 2, 512]), ps("acc2", [P, 2, 512])]
        psd, pss = ps("psd", [P, 512]), ps("pss", [P, 512])
        ps_pos = ps("pos", [P, 2, 512])
        block = ctx.enter_context(nc.Block())
        halves = lambda t: t.rearrange("p (a b) -> p a b", a=2)

        @block.sync
        def _(sp):
            for t, (key, other) in (("dst", (dst, src)), ("src", (src, dst))):
                sp.dma_start(keys[t][:, :], key.rearrange("(p c) -> p c", p=EP)).then_inc(loaded[t], 16)
                sp.dma_start(others[t][:, :], other.rearrange("(p c) -> p c", p=EP)).then_inc(loaded[t], 16)
            sp.wait_ge(cleared, 1)
            sp.dma_start(c.slots_dst[:, :].rearrange("(p t) w -> p t w", p=P), back[:, :, :]
                         ).then_inc(emptied_table, 16)
            sp.wait_ge(returned, 1)
            sp.dma_start(back[:, :, :], c.slots_dst[:, :].rearrange("(p t) w -> p t w", p=P)).then_inc(returned, 16)

        @block.gpsimd
        def _(pool):
            pool.memset(back[:, :, :], 0).then_inc(cleared, 1)
            pool.wait_ge(emptied_table, 16)
            pool.wait_ge(positioned, 3)

            def batch(i, s):
                pool.sem_inc(passed, 1)
                pool.tensor_copy(few[:, s, :, :].rearrange("p b w -> p w b"),
                                 trio[:, :, bass.ds((4 * i + s) * B, B)]).then_inc(copied, 1)
                pool.wait_ge(copied, 4 * i + s + 1)
                pool.sem_inc(passed, 1)
                for k in range(B):
                    pool.indirect_dma_start(out=c.slots_dst[:, :], in_=few[:, s, k, 1:3], in_offset=None,
                                            out_offset=bass.IndirectOffsetOnAxis(ap=few[:, s, k, 0:1], axis=0)
                                            ).then_inc(sent[s], 16)
            for s in range(4):
                batch(0, s)
            with pool.Fori(1, EC // (4 * B)) as i:
                for s in range(4):
                    pool.wait_ge(sent[s], i * (16 * B))
                    batch(i, s)
            for s in range(4):
                pool.wait_ge(sent[s], 16 * B * (EC // (4 * B)))
            pool.sem_inc(returned, 1)

        def dve_positions(dve, t, bucket_of):
            n = [0]

            def step(ins):
                ins.then_inc(split[t], 1)
                n[0] += 1
                dve.wait_ge(split[t], n[0])

            key, oth = keys[t], others[t]
            dve.wait_ge(loaded[t], 32)
            step(dve.tensor_scalar(tmp_i[:, :], key[:, :], 7, None, ALU.arith_shift_right))
            step(dve.tensor_copy(hi16[:, :], tmp_i[:, :]))
            if t == "dst":
                step(dve.tensor_copy(dst_hi[:, :], tmp_i[:, :]))
            step(dve.tensor_scalar(key[:, :], key[:, :], 127, None, ALU.bitwise_and))
            step(dve.tensor_scalar(oth[:, :], oth[:, :], -1.0, float(ZROW), ALU.mult, ALU.add))
            if t == "dst":
                step(dve.tensor_copy(dst_lo[:, :], key[:, :]))
                step(dve.tensor_copy(trio[:, 1, :], oth[:, :]))
                dve.tensor_scalar(trio[:, 2, :], key[:, :], 1.0, None, ALU.add).then_inc(positioned, 1)
            else:
                step(dve.tensor_copy(plo[:, :], key[:, :]))
                step(dve.tensor_scalar(tmp_i[:, :], oth[:, :], 7, None, ALU.bitwise_and))
                step(dve.tensor_scalar(oth[:, :], oth[:, :], 3, None, ALU.arith_shift_right))
                step(dve.tensor_copy(pay2[:, :], oth[:, :]))
                step(dve.tensor_scalar(cum[:, :], plo[:, :], 8.0, 8.0, ALU.mult, ALU.add))
                step(dve.tensor_tensor(pay1[:, :], cum[:, :], tmp_i[:, :], ALU.add))
            with dve.Fori(0, TILES) as b:
                dve.tensor_scalar(mask[:, :], hi16[:, :], c.iota[0:EP, bass.ds(b, 1)], 0.0, ALU.is_equal, ALU.add,
                                  accum_out=tot[:, bass.ds(b, 1)]).then_inc(counted[t], 1)
                dve.wait_ge(counted[t], b + 1)
            dve.wait_ge(summed[t], 1)
            step(dve.tensor_scalar(small_i[:, 0, :], pss[:, 64:64 + TILES], 127.0, None, ALU.add))
            step(dve.tensor_scalar(small_i[:, 1, :], small_i[:, 0, :], 7, None, ALU.arith_shift_right))
            step(dve.tensor_copy(nt[:, :], small_i[:, 1, :]))
            step(dve.tensor_tensor_scan(inc[:, :], nt[:, :], c.zeros[:, 0:TILES], 0.0, ALU.add, ALU.add))
            step(dve.tensor_tensor(inc[:, :], inc[:, :], nt[:, :], ALU.subtract))
            step(dve.tensor_scalar(inc[:, :], inc[:, :], 128.0, -1.0, ALU.mult, ALU.add))
            step(dve.tensor_tensor(off[0:EP, :], inc[0:EP, :], pss[0:EP, 0:TILES], ALU.add))
            step(dve.tensor_scalar(col_i[:, 0:1], pss[0:TILES, 128:129], 127.0, None, ALU.add))
            step(dve.tensor_scalar(col_i[:, 1:2], col_i[:, 0:1], 7, None, ALU.arith_shift_right))
            dve.tensor_copy(col_f[:, :], col_i[:, 1:2]).then_inc(based[t], 1)
            dve.wait_ge(ended[t], 1)
            step(dve.tensor_copy(endc[:, :], pss[0:TILES, 192:193]))
            dve.tensor_scalar(ge[:, :], c.iota[0:TILES, :], endc[:, 0:1], None, ALU.is_ge).then_inc(based[t], 1)
            dve.wait_ge(table[t], 1)
            step(dve.tensor_copy(halves(bucket_of[0:1, :]), accs[0][0:1, :, 0:HALF]))

            def bucket(b, q):
                dve.tensor_scalar(mask[:, :], hi16[:, :], c.iota[0:EP, bass.ds(b, 1)], None,
                                  ALU.is_equal).then_inc(masked[t], 1)
                dve.wait_ge(masked[t], b + 1)
                dve.tensor_tensor_scan(cum[:, :], mask[:, :], c.zeros[0:EP, :], off[0:EP, bass.ds(b, 1)],
                                       ALU.add, ALU.add).then_inc(scanned[t], 1)
                dve.wait_ge(scanned[t], b + 1)
                dve.wait_ge(usedhit[t], b + 1)
                dve.tensor_tensor(hit[:, q, :], mask[:, :], cum[:, :], ALU.mult).then_inc(picked[t], 1)
                dve.wait_ge(picked[t], b + 1)
            with dve.Fori(0, TILES // 2) as i:
                bucket(2 * i, 0)
                bucket(2 * i + 1, 1)
            bucket(TILES - 1, 0)
            dve.wait_ge(pos_whole[t], 1)
            step(dve.tensor_copy(halves(tmp_i[:, :]), ps_pos[0:EP, :, 0:HC]))
            step(dve.tensor_scalar(key[:, :], tmp_i[:, :], 127, None, ALU.bitwise_and))
            step(dve.tensor_copy(plo[:, :], key[:, :]))
            step(dve.tensor_scalar(key[:, :], tmp_i[:, :], 7, None, ALU.arith_shift_right))
            step(dve.tensor_copy(ptile[:, :], key[:, :]))
            if t == "dst":
                step(dve.tensor_scalar(cum[:, :], plo[:, :], float(ET), None, ALU.mult))
                step(dve.tensor_tensor(trio[:, 0, :], cum[:, :], ptile[:, :], ALU.add))
                dve.sem_inc(positioned, 2)

        @block.vector
        def _(dve):
            dve_positions(dve, "dst", c.buc_d)
            dve_positions(dve, "src", c.buc_s)

            def factors(t, k, turn):
                dve.wait_ge(spread, t + 1)
                dve.tensor_scalar(lo1[:, k, :], c.iota16[0:EP, 0:P], plo[:, bass.ds(t, 1)], None, ALU.is_equal
                                  ).then_inc(place_ready, 1)
                dve.tensor_scalar(hot[:, k, :], c.iota16[0:EP, :], ptile[:, bass.ds(t, 1)], None, ALU.is_equal)
                dve.tensor_scalar(dlo[:, k, :], c.iota16[0:EP, 0:P], dst_lo[:, bass.ds(t, 1)], None, ALU.is_equal)
                dve.tensor_scalar(dhi[:, k, :], c.iota16[0:EP, 0:TILES], dst_hi[:, bass.ds(t, 1)], None,
                                  ALU.is_equal).then_inc(onehot, 1)
            skewed(dve, [(0, factors)], EC, U)

            n = [0]

            def step(ins):
                ins.then_inc(unpacked, 1)
                n[0] += 1
                dve.wait_ge(unpacked, n[0])
            dve.wait_ge(placed, 1)
            step(dve.tensor_copy(halves(u1[:, :]), accs[0][:, :, 0:HALF]))
            step(dve.tensor_scalar(u2[:, :], u1[:, :], 3, None, ALU.arith_shift_right))
            step(dve.tensor_scalar(c.loc_s[:, :], u2[:, :], -1.0, None, ALU.add))
            step(dve.tensor_scalar(u2[:, :], u1[:, :], 7, None, ALU.bitwise_and))
            step(dve.tensor_scalar(halves(u3[:, :]), accs[1][:, :, 0:HALF], -8.0, float(ZROW), ALU.mult, ALU.add))
            step(dve.tensor_tensor(c.idx_s[:, 0:ET], u3[:, :], u2[:, :], ALU.subtract))
            step(dve.tensor_copy(c.deg[:, :], psd[:, 0:TILES]))
            dve.wait_ge(returned, 17)
            step(dve.tensor_scalar(c.idx_d[:, 0:ET], back[:, :, 0], -1.0, float(ZROW), ALU.mult, ALU.add))
            step(dve.tensor_scalar(c.loc_d[:, :], back[:, :, 1], -1.0, None, ALU.add))
            step(dve.tensor_scalar(c.idx_d[:, ET:ET + 4], u2[:, 0:4], 0.0, None, ALU.mult))
            step(dve.tensor_scalar(c.idx_s[:, ET:ET + 4], u2[:, 0:4], 0.0, None, ALU.mult))

        @block.scalar
        def _(act):
            def pay(t, k, turn):
                act.wait_ge(place_ready, t + 1)
                act.wait_ge(spread, t + 1)
                nc.scalar.activation(l12[:, k, 0, :], lo1[:, k, :], ACT.Copy, scale=pay1[:, bass.ds(t, 1)])
                nc.scalar.activation(l12[:, k, 1, :], lo1[:, k, :], ACT.Copy, scale=pay2[:, bass.ds(t, 1)]
                                     ).then_inc(paid, 1)
            skewed(act, [(0, pay)], EC, U)

        def pe_positions(pe, t):
            pe.sem_inc(usedhit[t], 2)
            pe.wait_ge(counted[t], TILES)
            pe.matmul(pss[0:EP, 0:TILES], c.below[0:EP, 0:EP], tot[:, :], start=True, stop=True)
            pe.matmul(pss[:, 64:64 + TILES], c.ones[0:EP, :], tot[:, :], start=True, stop=True)
            pe.matmul(pss[0:TILES, 128:129], tot[:, :], c.ones[0:EP, 0:1], start=True, stop=True
                      ).then_inc(summed[t], 1)
            pe.wait_ge(based[t], 1)
            pe.matmul(pss[0:TILES, 192:193], c.upto[0:TILES, 0:TILES], col_f[:, :], start=True,
                      stop=True).then_inc(ended[t], 1)
            pe.wait_ge(based[t], 2)
            for a in range(2):
                last = pe.matmul(accs[0][:, a, 0:HALF], c.ones[0:TILES - 1, :],
                                 ge[0:TILES - 1, a * HALF:(a + 1) * HALF], start=True, stop=True)
            last.then_inc(table[t], 1)
            for a in range(2):
                pe.matmul(ps_pos[0:EP, a, 0:HC], c.zeros[0:EP, 0:EP], c.zeros[0:EP, 0:HC], start=True, stop=False)

            def add(b, q):
                pe.wait_ge(picked[t], b + 1)
                for a in range(2):
                    last = pe.matmul(ps_pos[0:EP, a, 0:HC], c.ident[0:EP, 0:EP], hit[:, q, a * HC:(a + 1) * HC],
                                     start=False, stop=False)
                last.then_inc(usedhit[t], 1)
            with pe.Fori(0, TILES // 2) as i:
                add(2 * i, 0)
                add(2 * i + 1, 1)
            add(TILES - 1, 0)
            for a in range(2):
                last = pe.matmul(ps_pos[0:EP, a, 0:HC], c.zeros[0:EP, 0:EP], c.zeros[0:EP, 0:HC], start=False,
                                 stop=True)
            last.then_inc(pos_whole[t], 1)

        @block.tensor
        def _(pe):
            pe_positions(pe, "dst")
            pe_positions(pe, "src")
            pe.sem_inc(spread, U)
            pe.wait_ge(onehot, 1)
            for acc in accs:
                for a in range(2):
                    pe.matmul(acc[:, a, 0:HALF], c.zeros16[:, 0:P], c.zeros16[:, :], start=True, stop=False)
            pe.matmul(psd[:, 0:TILES], c.zeros16[:, 0:P], c.zeros16[:, 0:TILES], start=True, stop=False)

            def place(t, k, turn):
                pe.wait_ge(onehot, t + 1)
                pe.wait_ge(paid, t + 1)
                for m, acc in enumerate(accs):
                    for a in range(2):
                        pe.matmul(acc[:, a, 0:HALF], l12[:, k, m, :], hot[:, k, a * HALF:(a + 1) * HALF],
                                  start=False, stop=False)
                pe.matmul(psd[:, 0:TILES], dlo[:, k, :], dhi[:, k, :], start=False, stop=False
                          ).then_inc(spread, 1)
            skewed(pe, [(0, place)], EC, U)
            for acc in accs:
                for a in range(2):
                    pe.matmul(acc[:, a, 0:HALF], c.zeros16[:, 0:P], c.zeros16[:, :], start=False, stop=True)
            pe.matmul(psd[:, 0:TILES], c.zeros16[:, 0:P], c.zeros16[:, 0:TILES], start=False,
                      stop=True).then_inc(placed, 1)


def normalise(dve, sem, rooted, g, x, out, st, mean, rstd, var, done=0):
    tmp = var
    n = [0]

    def step(ins):
        ins.then_inc(sem, 1)
        n[0] += 1
        dve.wait_ge(sem, done + n[0])

    for k in range(UNROLL):
        last = dve.bn_stats(st[:, k, :], x[:, k, :])
    step(last)
    step(dve.tensor_tensor(mean[:, :], st[:, :, 1], st[:, :, 4], ALU.add))
    step(dve.tensor_tensor(tmp[:, :], st[:, :, 1], st[:, :, 4], ALU.subtract))
    step(dve.tensor_tensor(tmp[:, :], tmp[:, :], tmp[:, :], ALU.mult))
    step(dve.tensor_scalar(mean[:, :], mean[:, :], 0.5, None, ALU.mult))
    step(dve.tensor_scalar(tmp[:, :], tmp[:, :], D / 4.0, None, ALU.mult))
    step(dve.tensor_tensor(tmp[:, :], tmp[:, :], st[:, :, 2], ALU.add))
    step(dve.tensor_tensor(tmp[:, :], tmp[:, :], st[:, :, 5], ALU.add))
    step(dve.tensor_scalar(tmp[:, :], tmp[:, :], 1.0 / D, EPS, ALU.mult, ALU.add))
    dve.wait_ge(rooted, g + 1)
    for k in range(UNROLL):
        last = dve.tensor_scalar(out[:, k, :], x[:, k, :], mean[:, k:k + 1], rstd[:, k:k + 1], ALU.subtract,
                                 ALU.mult)
    step(last)
    assert n[0] == LN_STEPS


LN_STEPS = 10


def root(pool, c, sem, rooted, passed, g, rstd, var, done=0):
    pool.wait_ge(sem, done + g * LN_STEPS + LN_STEPS - 1)
    pool.sem_inc(passed, 1)
    pool.tensor_tensor(rstd[:, :], var[:, :], c.neghalf[:, :], ALU.pow).then_inc(rooted, 1)


def ln_buffers(sb):
    return (sb("st", [P, UNROLL, 6], F32), sb("mean", [P, UNROLL], F32), sb("rstd", [P, UNROLL], F32),
            sb("tmp", [P, UNROLL], F32))


def project_heads(nc, c, W, a_l, a_r):
    c.phase = "heads"
    sem = lambda name: nc_sem(nc, c, name)
    wloaded, rooted, lnstep, normed, turned, xt_made, projected, evac, passed = (
        sem(s) for s in "wloaded rooted lnstep normed turned xt_made projected evac passed".split())
    xin, stored = [sem("xin0"), sem("xin1")], [sem("stored0"), sem("stored1")]
    with ExitStack() as ctx:
        sb = lambda name, shape, dt: ctx.enter_context(nc.sbuf_tensor(f"heads_{name}", shape, dt))
        ps = lambda name, shape: ctx.enter_context(nc.psum_tensor(f"heads_ps_{name}", shape, F32))
        w = sb("w", [P, 2, D + 8], F32)
        al = sb("al", [P, 2, D], F32)
        prod = sb("prod", [P, D], F32)
        x, xn = sb("x", [P, 2, UNROLL, D], F32), sb("xn", [P, 2, UNROLL, D], F32)
        ln = ln_buffers(sb)
        xt = sb("xt", [P, 2, 2, P], F32)
        ht = sb("ht", [P, 2, UNROLL, D + 4], F32)
        pst, psh = ps("pst", [P, 2, 512]), ps("psh", [P, 2, 512])
        block = ctx.enter_context(nc.Block())

        @block.sync
        def _(sp):
            sp.dma_start(w[:, :, 0:D], W.rearrange("(k p) d -> p k d", p=P)).then_inc(wloaded, 16)
            for j, a in enumerate((a_l, a_r)):
                sp.dma_start(al[:, j, :], a.rearrange("a h d -> a (h d)").broadcast_to([P, D])).then_inc(wloaded, 16)

            def load(g, s, j):
                sp.wait_ge(normed, g + 1)
                sp.dma_start(x[:, s, :, :], rows(c.x0, g, D)).then_inc(xin[s], 16)
            groups(sp, load)

        @block.gpsimd
        def _(pool):
            groups(pool, lambda g, s, j: root(pool, c, lnstep, rooted, passed, g, ln[2], ln[3], done=8))

        @block.vector
        def _(dve):
            n = [0]

            def step(ins):
                ins.then_inc(lnstep, 1)
                n[0] += 1
                dve.wait_ge(lnstep, n[0])
            dve.sem_inc(normed, 2)
            dve.wait_ge(wloaded, 48)
            for k in range(2):
                for j in range(2):
                    step(dve.tensor_tensor(prod[:, :], w[:, k, 0:D], al[:, j, :], ALU.mult))
                    at = D + 4 * (1 - j)
                    step(dve.tensor_reduce(w[:, k, at:at + 4], prod[:, :].rearrange("p (h d) -> p h d", h=HEADS),
                                           AX.X, ALU.add))
            base = n[0]

            def body(g, s, j):
                dve.wait_ge(xin[s], 16 * j + 16)
                dve.wait_ge(turned, g * UNROLL + UNROLL)
                normalise(dve, lnstep, rooted, g, x[:, s], xn[:, s], *ln, done=base + g * LN_STEPS)
                dve.sem_inc(normed, 1)
            groups(dve, body)

        @block.scalar
        def _(act):
            act.sem_inc(xt_made, 2)
            act.sem_inc(evac, 2)
            act.sem_inc(stored[0], 32)
            act.sem_inc(stored[1], 32)

            def body(g, s, j):
                act.wait_ge(stored[s], 32 * j + 32)
                for k in range(UNROLL):
                    t, q = g * UNROLL + k, (s + k) % 2
                    act.wait_ge(turned, t + 15)
                    act.wait_ge(projected, t + 1)
                    nc.scalar.copy(xt[:, q, :, :], pst[:, q, 0:2 * P]).then_inc(xt_made, 1)
                    act.wait_ge(projected, t + 3)
                    nc.scalar.copy(ht[:, s, k, :], psh[:, q, 0:D + 4])
                    nc.scalar.copy(c.hlm[:, bass.ds(t * 8, 4)], psh[:, q, D + 4:D + 8]).then_inc(evac, 1)
                act.wait_ge(evac, g * UNROLL + UNROLL + 2)
                act.dma_start(rows(c.t_h, g, D + 4), ht[:, s, :, :]).then_inc(stored[s], 16)
                act.dma_start(rows(c.t_hr, g, 4), ht[:, s, :, D:D + 4]).then_inc(stored[s], 16)
            groups(act, body)
            act.wait_ge(stored[0], 32 * 5)
            act.wait_ge(stored[1], 32 * 4)

        @block.tensor
        def _(pe):
            pe.sem_inc(turned, 14)
            pe.sem_inc(projected, 2)
            pe.wait_ge(lnstep, 8)

            def body(g, s, j):
                pe.wait_ge(normed, g + 3)
                for k in range(UNROLL):
                    t, q = g * UNROLL + k, (s + k) % 2
                    pe.wait_ge(xt_made, t + 1)
                    for b in range(2):
                        last = pe.transpose(pst[:, q, b * P:(b + 1) * P], xn[:, s, k, b * P:(b + 1) * P], c.ident[:, :])
                    last.then_inc(turned, 1)
                    pe.wait_ge(xt_made, t + 3)
                    pe.wait_ge(evac, t + 1)
                    for b in range(2):
                        last = pe.matmul(psh[:, q, 0:D + 8], xt[:, q, b, :], w[:, b, :], start=(b == 0), stop=(b == 1))
                    last.then_inc(projected, 1)
            groups(pe, body)


def gather_rows(pool, idx, few, table, ring, gathered, freed, copied, passed):
    def indices(batch, at):
        pool.tensor_copy(few[:, at, :], idx[:, bass.ds(batch * 4, 4)]).then_inc(copied, 1)

    def turn(i):
        for h in range(4):
            n = 4 * i + h
            if h == 3:
                pool.wait_ge(gathered[0], 64 * i + 64)
            elif not isinstance(i, int):
                pool.wait_ge(gathered[h + 1], 64 * i)
            pool.wait_ge(freed, n * 4 + 4)
            pool.sem_inc(passed, 1)
            indices(n + 1, (h + 1) % 4)
            pool.wait_ge(copied, n + 1)
            pool.sem_inc(passed, 1)
            for k in range(4):
                pool.indirect_dma_start(out=ring[:, 4 * h + k, :], out_offset=None, in_=table[:, :],
                                        in_offset=bass.IndirectOffsetOnAxis(ap=few[:, h, k:k + 1], axis=0)
                                        ).then_inc(gathered[h], 16)
    indices(0, 0)
    turn(0)
    with pool.Fori(1, ET // RING) as i:
        turn(i)


def one_hots(dve, c, local, oh, t, k):
    return dve.tensor_tensor(oh[:, k:k + 4, :], c.iota[:, 0:P].unsqueeze(1).broadcast_to([P, 4, P]),
                             local[:, bass.ds(t, 4)].unsqueeze(2).broadcast_to([P, 4, P]), ALU.is_equal)


def neighbour_max(nc, c):
    c.phase = "nmax"
    R = 4
    sem = lambda name: nc_sem(nc, c, name)
    copied, passed, oh_made, turned, pen_made, diag_act, diag_dve, spread, reduced, bested, cleared = (
        sem(s) for s in "copied passed oh_made turned pen_made diag_act diag_dve spread reduced bested cleared".split())
    gathered = [sem(f"gathered{k}") for k in range(RING // 4)]
    with ExitStack() as ctx:
        sb = lambda name, shape, dt: ctx.enter_context(nc.sbuf_tensor(f"nmax_{name}", shape, dt))
        ps = lambda name, shape: ctx.enter_context(nc.psum_tensor(f"nmax_ps_{name}", shape, F32))
        few = sb("few", [P, 4, 4], I32)
        hr = sb("hr", [P, RING, 4], F32)
        oh = sb("oh", [P, RING, P], F32)
        diag = sb("diag", [P, R, HEADS, P], F32)
        pen = sb("pen", [P, R, P], F32)
        junk = sb("junk", [P, HEADS, P], F32)
        tmax = sb("tmax", [P, R, 4], F32)
        best = sb("best", [P, TILES * 4], F32)
        tmp = sb("tmp", [P, TILES, 4], F32)
        ps_oh, ps_all = ps("oh", [P, R, 512]), ps("all", [P, R, 512])
        block = ctx.enter_context(nc.Block())

        @block.gpsimd
        def _(pool):
            gather_rows(pool, c.idx_s, few, c.t_hr, hr, gathered, spread, copied, passed)

        @block.tensor
        def _(pe):
            pe.sem_inc(turned, RING)
            pe.sem_inc(spread, RING)

            def turn(t, k, turn_):
                if k % 4 == 0:
                    pe.wait_ge(oh_made, 4 * turn_ + k // 4 + 1)
                pe.wait_ge(pen_made, t + 1)
                pe.transpose(ps_oh[:, k % R, 0:P], oh[:, k, :], c.ident[:, :]).then_inc(turned, 1)

            def every_node(t, k, turn_):
                pe.wait_ge(diag_act, t + 1)
                pe.wait_ge(diag_dve, t + 1)
                pe.wait_ge(reduced, t + 1)
                pe.matmul(ps_all[:, k % R, :], c.ones[:, :], diag[:, k % R, :, :].rearrange("p h e -> p (h e)"),
                          start=True, stop=True).then_inc(spread, 1)
            skewed(pe, [(0, turn), (1, every_node)], ET, RING)

        @block.scalar
        def _(act):
            act.sem_inc(pen_made, R)

            def diagonal(t, k, turn_):
                if k % 4 == 0:
                    act.wait_ge(gathered[k // 4], 64 * turn_ + 64)
                act.wait_ge(spread, t + RING - R + 1)
                for h in range(3):
                    last = nc.scalar.activation(diag[:, k % R, h, :], c.ident[:, :], ACT.Copy, scale=hr[:, k, h:h + 1])
                last.then_inc(diag_act, 1)

            def penalty(t, k, turn_):
                act.wait_ge(turned, t + RING + 1)
                act.wait_ge(reduced, t + 1)
                nc.scalar.activation(pen[:, k % R, :], ps_oh[:, k % R, 0:P], ACT.Copy, bias=LOW, scale=-LOW
                                     ).then_inc(pen_made, 1)
            skewed(act, [(0, penalty), (0, diagonal)], ET, RING)

        @block.vector
        def _(dve):
            dve.memset(best[:, :], LOW).then_inc(cleared, 1)
            dve.sem_inc(reduced, R)
            dve.sem_inc(bested, R)
            dve.wait_ge(cleared, 1)

            def hots(t, k, turn_):
                if k % 4 == 0:
                    dve.wait_ge(turned, t + 4)
                    one_hots(dve, c, c.loc_s, oh, t, k).then_inc(oh_made, 1)

            def diagonal(t, k, turn_):
                if k % 4 == 0:
                    dve.wait_ge(gathered[k // 4], 64 * turn_ + 64)
                dve.wait_ge(spread, t + RING - R + 1)
                dve.tensor_scalar(diag[:, k % R, 3, :], c.ident[:, :], hr[:, k, 3:4], None, ALU.mult
                                  ).then_inc(diag_dve, 1)

            def reduce(t, k, turn_):
                q = k % R
                dve.wait_ge(spread, t + RING + 1)
                dve.wait_ge(pen_made, t + R + 1)
                dve.wait_ge(reduced, t + R)
                dve.wait_ge(bested, t + 1)
                dve.sem_inc(passed, 1)
                for h in range(HEADS):
                    last = dve.tensor_tensor_reduce(junk[:, h, :], pen[:, q, :], ps_all[:, q, h * P:(h + 1) * P],
                                                    1.0, LOW, ALU.add, ALU.max, tmax[:, q, h:h + 1])
                last.then_inc(reduced, 1)

            def keep(t, k, turn_):
                b = dve.value_load(c.buc_s[0:1, bass.ds(t, 1)], min_val=0, max_val=TILES - 1)
                dve.wait_ge(reduced, t + R + 1)
                dve.wait_ge(bested, t + R)
                here = best[:, bass.ds(b * 4, 4)]
                dve.tensor_tensor(here, here, tmax[:, k % R, :], ALU.max).then_inc(bested, 1)
            skewed(dve, [(0, hots), (1, diagonal), (3, reduce), (4, keep)], ET, RING)
            dve.wait_ge(bested, ET + R)
            hl = c.hlm[:, :].rearrange("p (i e) -> p i e", e=8)
            dve.tensor_tensor(tmp[:, :, :], hl[:, :, 0:4], best[:, :].rearrange("p (i e) -> p i e", e=4),
                              ALU.add).then_inc(cleared, 1)
            dve.wait_ge(cleared, 2)
            dve.scalar_tensor_tensor(out=hl[:, :, 4:8], in0=tmp[:, :, :], scalar=0.2, in1=tmp[:, :, :], op0=ALU.mult,
                                     op1=ALU.max).then_inc(cleared, 1)
            dve.wait_ge(cleared, 3)


def attend(nc, c):
    c.phase = "attend"
    W = D + 4
    R = 4
    sem = lambda name: nc_sem(nc, c, name)
    (copied, passed, oh_made, oh_turned, oht_made, looked, scored, exped, weighed_act, weighed_dve, scattered, added,
     step, cleared) = (sem(s) for s in ("copied passed oh_made oh_turned oht_made looked scored exped weighed_act "
                                        "weighed_dve scattered added step cleared").split())
    gathered = [sem(f"gathered{k}") for k in range(RING // 4)]
    with ExitStack() as ctx:
        sb = lambda name, shape, dt: ctx.enter_context(nc.sbuf_tensor(f"attend_{name}", shape, dt))
        ps = lambda name, shape: ctx.enter_context(nc.psum_tensor(f"attend_ps_{name}", shape, F32))
        few = sb("few", [P, 4, 4], I32)
        rows_h = sb("rows", [P, RING, W], F32)
        oh = sb("oh", [P, RING, P], F32)
        oht = sb("oht", [P, R, P], F32)
        sc = sb("sc", [P, R, 3, 4], F32)
        wr = sb("wr", [P, R, W], F32)
        ps_oh, ps_look, ps_sum = ps("oh", [P, 2, 512]), ps("look", [P, 2, 512]), ps("sum", [P, R, 512])
        block = ctx.enter_context(nc.Block())

        @block.gpsimd
        def _(pool):
            gather_rows(pool, c.idx_s, few, c.t_h, rows_h, gathered, scattered, copied, passed)

        @block.tensor
        def _(pe):
            pe.sem_inc(looked, R)
            pe.sem_inc(scattered, RING)

            def turn(t, k, turn_):
                if k % 4 == 0:
                    pe.wait_ge(oh_made, 4 * turn_ + k // 4 + 1)
                pe.wait_ge(oht_made, t + 1)
                pe.transpose(ps_oh[:, k % 2, 0:P], oh[:, k, :], c.ident[:, :]).then_inc(oh_turned, 1)

            def look(t, k, turn_):
                b = pe.value_load(c.buc_s[0:1, bass.ds(t, 1)], min_val=0, max_val=TILES - 1)
                pe.wait_ge(oht_made, t + 3)
                pe.wait_ge(scored, t + 1)
                pe.matmul(ps_look[:, k % 2, 0:8], oht[:, k % R, :], c.hlm[:, bass.ds(b * 8, 8)], start=True,
                          stop=True).then_inc(looked, 1)

            def scatter(t, k, turn_):
                pe.wait_ge(weighed_act, t + 1)
                pe.wait_ge(weighed_dve, t + 1)
                pe.wait_ge(added, t + 1)
                pe.matmul(ps_sum[:, k % R, 0:W], oh[:, k, :], wr[:, k % R, :], start=True, stop=True
                          ).then_inc(scattered, 1)
            skewed(pe, [(0, turn), (5, scatter), (1, look)], ET, RING)

        @block.scalar
        def _(act):
            act.sem_inc(oht_made, 2)
            act.sem_inc(exped, R)

            def turned(t, k, turn_):
                act.wait_ge(oh_turned, t + 1)
                act.wait_ge(looked, t + 1)
                nc.scalar.copy(oht[:, k % R, :], ps_oh[:, k % 2, 0:P]).then_inc(oht_made, 1)

            def exponentials(t, k, turn_):
                act.wait_ge(scored, t + 3)
                act.wait_ge(scattered, t + RING - R + 1)
                nc.scalar.activation(wr[:, k % R, D:W], sc[:, k % R, 2, :], ACT.Exp).then_inc(exped, 1)

            def weigh(t, k, turn_):
                act.wait_ge(exped, t + R + 1)
                for h in range(3):
                    last = nc.scalar.activation(wr[:, k % R, h * HD:(h + 1) * HD], rows_h[:, k, h * HD:(h + 1) * HD],
                                                ACT.Copy, scale=wr[:, k % R, D + h:D + h + 1])
                last.then_inc(weighed_act, 1)
            skewed(act, [(0, turned), (3, exponentials), (4, weigh)], ET, RING)

        @block.vector
        def _(dve):
            dve.memset(c.acc[:, 0:TILES * W], 0.0).then_inc(cleared, 1)
            dve.sem_inc(scored, 2)
            dve.sem_inc(added, R)
            dve.wait_ge(cleared, 1)

            def hots(t, k, turn_):
                if k % 4 == 0:
                    dve.wait_ge(scattered, t + 4)
                    one_hots(dve, c, c.loc_s, oh, t, k).then_inc(oh_made, 1)

            def score(t, k, turn_):
                dve.wait_ge(looked, t + R + 1)
                if k % 4 == 0:
                    dve.wait_ge(gathered[k // 4], 64 * turn_ + 64)
                dve.wait_ge(exped, t + 1)
                dve.tensor_tensor(sc[:, k % R, 0, :], ps_look[:, k % 2, 0:4], rows_h[:, k, D:W], ALU.add
                                  ).then_inc(step, 1)

            def leaky(t, k, turn_):
                dve.wait_ge(step, 2 * t + 1)
                dve.scalar_tensor_tensor(out=sc[:, k % R, 1, :], in0=sc[:, k % R, 0, :], scalar=0.2,
                                         in1=sc[:, k % R, 0, :], op0=ALU.mult, op1=ALU.max).then_inc(step, 1)

            def stabilise(t, k, turn_):
                dve.wait_ge(step, 2 * t + 2)
                dve.tensor_tensor(sc[:, k % R, 2, :], sc[:, k % R, 1, :], ps_look[:, k % 2, 4:8], ALU.subtract
                                  ).then_inc(scored, 1)

            def weigh(t, k, turn_):
                dve.wait_ge(exped, t + R + 1)
                dve.tensor_scalar(wr[:, k % R, 3 * HD:D], rows_h[:, k, 3 * HD:D], wr[:, k % R, D + 3:W], None,
                                  ALU.mult).then_inc(weighed_dve, 1)

            def add(t, k, turn_):
                b = dve.value_load(c.buc_s[0:1, bass.ds(t, 1)], min_val=0, max_val=TILES - 1)
                dve.wait_ge(scattered, t + RING + 1)
                dve.wait_ge(added, t + R)
                here = c.acc[:, bass.ds(b * W, W)]
                dve.tensor_tensor(here, here, ps_sum[:, k % R, 0:W], ALU.add).then_inc(added, 1)
            skewed(dve, [(0, hots), (2, score), (4, weigh), (2, leaky), (6, add), (2, stabilise)], ET, RING)
            dve.wait_ge(added, ET + R)


def close_attention(nc, c):
    c.phase = "close"
    W = D + 4
    sem = lambda name: nc_sem(nc, c, name)
    rooted, lnstep, summed, normed, used, passed, counted, allsummed = (
        sem(s) for s in "rooted lnstep summed normed used passed counted allsummed".split())
    xin, stored = [sem("xin0"), sem("xin1")], [sem("stored0"), sem("stored1")]
    with ExitStack() as ctx:
        sb = lambda name, shape, dt: ctx.enter_context(nc.sbuf_tensor(f"close_{name}", shape, dt))
        x, x1, xn = (sb(n, [P, 2, UNROLL, D], F32) for n in ("x", "x1", "xn"))
        den = sb("den", [P, UNROLL, HEADS], F32)
        ln = ln_buffers(sb)
        pcol = ctx.enter_context(nc.psum_tensor("close_pcol", [P, 2, 512], F32))
        block = ctx.enter_context(nc.Block())

        @block.sync
        def _(sp):
            def load(g, s, j):
                sp.wait_ge(summed, g + 1)
                sp.dma_start(x[:, s, :, :], rows(c.x0, g, D)).then_inc(xin[s], 16)
            groups(sp, load)

        @block.gpsimd
        def _(pool):
            groups(pool, lambda g, s, j: root(pool, c, lnstep, rooted, passed, g, ln[2], ln[3]))

        @block.vector
        def _(dve):
            dve.sem_inc(summed, 2)

            def body(g, s, j):
                acc = c.acc[:, bass.ds(g * (UNROLL * W), UNROLL * W)].rearrange("p (k w) -> p k w", w=W)
                att = acc[:, :, 0:D].rearrange("p k (h d) -> p k h d", h=HEADS)
                dve.tensor_scalar(den[:, :, :], acc[:, :, D:W], 1e-30, None, ALU.max).then_inc(counted, 1)
                dve.wait_ge(counted, 3 * g + 1)
                dve.reciprocal(den[:, :, :], den[:, :, :]).then_inc(counted, 1)
                dve.wait_ge(counted, 3 * g + 2)
                dve.tensor_tensor(att, att, den[:, :, :].unsqueeze(3).broadcast_to([P, UNROLL, HEADS, HD]), ALU.mult
                                  ).then_inc(counted, 1)
                dve.wait_ge(xin[s], 16 * j + 16)
                dve.wait_ge(stored[s], 32 * j + 32)
                dve.wait_ge(counted, 3 * g + 3)
                dve.tensor_tensor(x1[:, s], acc[:, :, 0:D], x[:, s], ALU.add).then_inc(summed, 1)
                dve.wait_ge(summed, g + 3)
                dve.wait_ge(used, g + 1)
                normalise(dve, lnstep, rooted, g, x1[:, s], xn[:, s], *ln, done=g * LN_STEPS)
                dve.sem_inc(normed, 1)
            groups(dve, body)
            dve.wait_ge(allsummed, 1)
            dve.tensor_copy(c.colsum[:, :], pcol[:, :, 0]).then_inc(counted, 1)
            dve.wait_ge(counted, 3 * GROUPS + 1)

        @block.scalar
        def _(act):
            act.sem_inc(stored[0], 32)
            act.sem_inc(stored[1], 32)

            def store(g, s, j):
                act.wait_ge(normed, g + 1)
                act.dma_start(rows(c.x1, g, D), x1[:, s]).then_inc(stored[s], 16)
                act.dma_start(rows(c.xn1, g, D), xn[:, s]).then_inc(stored[s], 16)
            groups(act, store)
            act.wait_ge(stored[0], 32 * 5)
            act.wait_ge(stored[1], 32 * 4)

        @block.tensor
        def _(pe):
            pe.sem_inc(used, 2)
            for b in range(2):
                pe.matmul(pcol[:, b, 0:1], c.zeros[:, 0:P], c.ones[:, 0:1], start=True, stop=False)

            def body(g, s, j):
                pe.wait_ge(normed, g + 1)
                for k in range(UNROLL):
                    for b in range(2):
                        last = pe.matmul(pcol[:, b, 0:1], xn[:, s, k, b * P:(b + 1) * P], c.ones[:, 0:1],
                                         start=False, stop=False)
                last.then_inc(used, 1)
            groups(pe, body)
            for b in range(2):
                last = pe.matmul(pcol[:, b, 0:1], c.zeros[:, 0:P], c.ones[:, 0:1], start=False, stop=True)
            last.then_inc(allsummed, 1)


def choose_experts(nc, c, Wr, br):
    c.phase = "choose"
    sem = lambda name: nc_sem(nc, c, name)
    loaded, step, given, expd = (sem(s) for s in "loaded step given expd".split())
    with ExitStack() as ctx:
        sb = lambda name, shape, dt: ctx.enter_context(nc.sbuf_tensor(f"choose_{name}", shape, dt))
        wr, brow = sb("wr", [P, 2, X0], F32), sb("brow", [P, X0], F32)
        mean = sb("mean", [P, 2, P], F32)
        v, e, w, eq, cand = (sb(n, [P, X0], F32) for n in ("v", "e", "w", "eq", "cand"))
        one, two = sb("one", [P, 8], F32), sb("two", [P, 8], F32)
        plog = ctx.enter_context(nc.psum_tensor("choose_plog", [P, 512], F32))
        block = ctx.enter_context(nc.Block())

        @block.sync
        def _(sp):
            sp.dma_start(wr[:, :, :], Wr.rearrange("(k p) e -> p k e", p=P)).then_inc(loaded, 16)
            sp.dma_start(brow[:, :], br.rearrange("(a e) -> a e", a=1).broadcast_to([P, X0])).then_inc(loaded, 16)

        @block.tensor
        def _(pe):
            pe.wait_ge(loaded, 32)
            pe.wait_ge(step, 2)
            for b in range(2):
                last = pe.matmul(plog[:, 0:X0], mean[:, b, :], wr[:, b, :], start=(b == 0), stop=(b == 1))
            last.then_inc(given, 1)

        @block.scalar
        def _(act):
            act.wait_ge(expd, 1)
            nc.scalar.activation(e[:, :], v[:, :], ACT.Exp).then_inc(given, 1)
            act.wait_ge(expd, 2)
            nc.scalar.activation(e[:, :], v[:, :], ACT.Exp).then_inc(given, 1)
            act.wait_ge(expd, 3)
            nc.scalar.activation(two[:, 2:3], two[:, 0:1], ACT.Exp).then_inc(given, 1)

        @block.vector
        def _(dve):
            n = [0]

            def do(ins):
                ins.then_inc(step, 1)
                n[0] += 1
                dve.wait_ge(step, n[0])

            def softmax(nth):
                do(dve.tensor_reduce(one[:, 0:1], v[:, :], AX.X, ALU.max))
                do(dve.tensor_scalar(v[:, :], v[:, :], one[:, 0:1], None, ALU.subtract))
                dve.sem_inc(expd, 1)
                dve.wait_ge(given, nth + 1)
                do(dve.tensor_reduce(one[:, 1:2], e[:, :], AX.X, ALU.add))
                do(dve.reciprocal(one[:, 1:2], one[:, 1:2]))
                do(dve.tensor_scalar(w[:, :], e[:, :], one[:, 1:2], None, ALU.mult))

            for b in range(2):
                do(dve.tensor_scalar(mean[:, b, :], c.ones[:, :], c.colsum[:, b:b + 1], 1.0 / N, ALU.mult, ALU.mult))
            dve.wait_ge(given, 1)
            do(dve.tensor_tensor(v[:, :], plog[:, 0:X0], brow[:, :], ALU.add))
            softmax(1)
            do(dve.tensor_scalar(v[:, :], w[:, :], float(N), CAP0, ALU.mult, ALU.max))
            do(dve.reciprocal(v[:, :], v[:, :]))
            do(dve.tensor_scalar(v[:, :], v[:, :], CAP0, None, ALU.mult))
            do(dve.tensor_tensor(v[:, :], v[:, :], w[:, :], ALU.mult))
            softmax(2)
            for m in range(2):
                do(dve.tensor_reduce(one[:, 2 + m:3 + m], w[:, :], AX.X, ALU.max))
                do(dve.tensor_scalar(eq[:, :], w[:, :], one[:, 2 + m:3 + m], 100.0, ALU.not_equal, ALU.mult))
                do(dve.tensor_tensor(cand[:, :], eq[:, :], c.iota[:, 0:X0], ALU.add))
                do(dve.tensor_reduce(one[:, 4 + m:5 + m], cand[:, :], AX.X, ALU.min))
                do(dve.tensor_scalar(eq[:, :], c.iota[:, 0:X0], one[:, 4 + m:5 + m], 4.0, ALU.is_equal, ALU.mult))
                do(dve.tensor_tensor(w[:, :], w[:, :], eq[:, :], ALU.subtract))
            do(dve.tensor_copy(c.chosen[0:1, :], one[0:1, 4:6]))
            do(dve.tensor_tensor(two[:, 0:1], one[:, 3:4], one[:, 2:3], ALU.subtract))
            dve.sem_inc(expd, 1)
            dve.wait_ge(given, 4)
            do(dve.tensor_scalar(two[:, 3:4], two[:, 2:3], 1.0, None, ALU.add))
            do(dve.reciprocal(c.share[:, 0:1], two[:, 3:4]))
            do(dve.tensor_tensor(c.share[:, 1:2], c.share[:, 0:1], two[:, 2:3], ALU.mult))


def experts0(nc, c, W1, b1, W2, b2, gamma, beta):
    c.phase = "experts0"
    FC = F0 // P
    NH = UNROLL * P // 2
    sem = lambda name: nc_sem(nc, c, name)
    (wloaded, wready, rooted, lnstep, turned, xt_made, hidden, gelued, mixed, emptied, passed, step, out) = (
        sem(s) for s in ("wloaded wready rooted lnstep turned xt_made hidden gelued mixed emptied passed step "
                         "out").split())
    xin, stored = [sem("xin0"), sem("xin1")], [sem("stored0"), sem("stored1")]
    with ExitStack() as ctx:
        sb = lambda name, shape, dt: ctx.enter_context(nc.sbuf_tensor(f"experts0_{name}", shape, dt))
        ps = lambda name, shape: ctx.enter_context(nc.psum_tensor(f"experts0_ps_{name}", shape, F32))
        w1 = sb("w1", [P, 2, 2, F0], F32)
        w2 = sb("w2", [P, 2, FC, D], F32)
        b1s = sb("b1", [P, 2, FC], F32)
        b2s = sb("b2", [P, 2, D], F32)
        gam, bet = sb("gam", [P, D], F32), sb("bet", [P, D], F32)
        xn, xr = sb("xn", [P, 2, UNROLL, D], F32), sb("xr", [P, 2, UNROLL, D], F32)
        xt = sb("xt", [P, 2, UNROLL * P], F32)
        hid = sb("hid", [P, 2 * FC, UNROLL * P], F32)
        y = sb("y", [P, UNROLL, D], F32)
        yo = sb("yo", [P, 2, UNROLL, D], F32)
        ln = ln_buffers(sb)
        pst, psh, psy = ps("t", [P, 2, 512]), ps("h", [P, 2, 512]), ps("y", [P, 2, 512])
        block = ctx.enter_context(nc.Block())

        @block.sync
        def _(sp):
            for m in range(2):
                e = sp.value_load(c.chosen[0:1, m:m + 1], min_val=0, max_val=X0 - 1)
                sp.dma_start(w1[:, m], W1[bass.ds(e, 1)].rearrange("a (k p) f -> p (a k) f", p=P)).then_inc(wloaded, 16)
                sp.dma_start(w2[:, m], W2[bass.ds(e, 1)].rearrange("a (k p) f -> p (a k) f", p=P)).then_inc(wloaded, 16)
                with nc.allow_non_contiguous_dma("a bias, one element to a partition"):
                    sp.dma_start(b1s[:, m, :], b1[bass.ds(e, 1)].rearrange("a (k p) -> p (a k)", p=P)
                                 ).then_inc(wloaded, 16)
                sp.dma_start(b2s[:, m, :], b2[bass.ds(e, 1)].broadcast_to([P, D])).then_inc(wloaded, 16)
            for t, d in ((gam, gamma), (bet, beta)):
                sp.dma_start(t[:, :], d.rearrange("(a e) -> a e", a=1).broadcast_to([P, D])).then_inc(wloaded, 16)

            def load(g, s, j):
                sp.wait_ge(out, g + 1)
                sp.dma_start(xn[:, s], rows(c.xn1, g, D)).then_inc(xin[s], 16)
                sp.dma_start(xr[:, s], rows(c.x1, g, D)).then_inc(xin[s], 16)
            groups(sp, load)

        @block.gpsimd
        def _(pool):
            groups(pool, lambda g, s, j: root(pool, c, lnstep, rooted, passed, g, ln[2], ln[3]))

        @block.tensor
        def _(pe):
            pe.sem_inc(hidden, 2)
            pe.wait_ge(wready, 1)

            def body(g, s, j):
                pe.wait_ge(xin[s], 32 * j + 32)
                for k in range(UNROLL):
                    q = (s + k) % 2
                    pe.wait_ge(xt_made, g * UNROLL + k + 1)
                    for b in range(2):
                        last = pe.transpose(pst[:, q, b * P:(b + 1) * P], xn[:, s, k, b * P:(b + 1) * P], c.ident[:, :])
                    last.then_inc(turned, 1)
                pe.wait_ge(xt_made, g * UNROLL + UNROLL + 2)
                for m in range(4 * FC):
                    f, half, q = m // 2, m % 2, m % 2
                    pe.wait_ge(gelued, g * (4 * FC) + m + 1)
                    for b in range(2):
                        last = pe.matmul(psh[:, q, 0:NH], w1[:, f // FC, b, (f % FC) * P:(f % FC + 1) * P],
                                         xt[:, b, half * NH:(half + 1) * NH], start=(b == 0), stop=(b == 1))
                    last.then_inc(hidden, 1)
                pe.wait_ge(gelued, g * (4 * FC) + 4 * FC + 2)
                for k in range(UNROLL):
                    q = (s + k) % 2
                    pe.wait_ge(emptied, g * UNROLL + k + 1)
                    for f in range(2 * FC):
                        last = pe.matmul(psy[:, q, 0:D], hid[:, f, k * P:(k + 1) * P], w2[:, f // FC, f % FC, :],
                                         start=(f == 0), stop=(f == 2 * FC - 1))
                    last.then_inc(mixed, 1)
            groups(pe, body)

        @block.scalar
        def _(act):
            act.sem_inc(xt_made, 2)
            act.sem_inc(gelued, 2)
            act.sem_inc(stored[0], 16)
            act.sem_inc(stored[1], 16)
            act.wait_ge(wloaded, 160)

            def body(g, s, j):
                act.wait_ge(hidden, g * (4 * FC) + 2)
                for k in range(UNROLL):
                    act.wait_ge(turned, g * UNROLL + k + 1)
                    nc.scalar.copy(xt[:, :, k * P:(k + 1) * P],
                                   pst[:, (s + k) % 2, 0:2 * P].rearrange("p (b n) -> p b n", b=2)).then_inc(xt_made, 1)
                act.wait_ge(mixed, g * UNROLL + 1)
                for m in range(4 * FC):
                    f, half = m // 2, m % 2
                    act.wait_ge(hidden, g * (4 * FC) + m + 3)
                    nc.scalar.activation(hid[:, f, half * NH:(half + 1) * NH], psh[:, m % 2, 0:NH], ACT.Gelu,
                                         bias=b1s[:, f // FC, f % FC:f % FC + 1]).then_inc(gelued, 1)
                act.wait_ge(out, g + 3)
                act.dma_start(rows(c.x2, g, D), yo[:, s]).then_inc(stored[s], 16)
            groups(act, body)
            act.wait_ge(stored[0], 16 * 5)
            act.wait_ge(stored[1], 16 * 4)

        @block.vector
        def _(dve):
            n = [0]

            def do(ins):
                ins.then_inc(step, 1)
                n[0] += 1
                dve.wait_ge(step, n[0])

            dve.sem_inc(mixed, 1)
            dve.sem_inc(emptied, 2)
            dve.sem_inc(out, 2)
            dve.wait_ge(wloaded, 160)
            for m in range(2):
                do(dve.tensor_scalar(w2[:, m], w2[:, m], c.share[:, m:m + 1], None, ALU.mult))
                do(dve.tensor_scalar(b2s[:, m, :], b2s[:, m, :], c.share[:, m:m + 1], None, ALU.mult))
            do(dve.tensor_tensor(b2s[:, 0, :], b2s[:, 0, :], b2s[:, 1, :], ALU.add))
            dve.sem_inc(wready, 1)
            base = n[0]
            bias = b2s[:, 0:1, :].broadcast_to([P, UNROLL, D])
            wide = lambda t: t[:, :].unsqueeze(1).broadcast_to([P, UNROLL, D])

            def body(g, s, j):
                dve.wait_ge(xin[s], 32 * j + 32)
                at = base + g * (UNROLL + 4)
                for k in range(UNROLL):
                    dve.wait_ge(mixed, g * UNROLL + k + 2)
                    dve.tensor_tensor(y[:, k, :], psy[:, (s + k) % 2, 0:D], xn[:, s, k, :], ALU.add).then_inc(step, 1)
                    dve.wait_ge(step, at + k + 1)
                    dve.sem_inc(emptied, 1)
                dve.tensor_tensor(y[:, :, :], y[:, :, :], bias, ALU.add).then_inc(step, 1)
                dve.wait_ge(step, at + UNROLL + 1)
                dve.wait_ge(stored[s], 16 * j + 16)
                normalise(dve, lnstep, rooted, g, y, yo[:, s], *ln, done=g * LN_STEPS)
                dve.tensor_tensor(yo[:, s], yo[:, s], wide(gam), ALU.mult).then_inc(step, 1)
                dve.wait_ge(step, at + UNROLL + 2)
                dve.tensor_tensor(yo[:, s], yo[:, s], wide(bet), ALU.add).then_inc(step, 1)
                dve.wait_ge(step, at + UNROLL + 3)
                dve.tensor_tensor(yo[:, s], yo[:, s], xr[:, s], ALU.add).then_inc(step, 1)
                dve.wait_ge(step, at + UNROLL + 4)
                dve.sem_inc(out, 1)
            groups(dve, body)


def prepare_conv(nc, c):
    c.phase = "prep"
    sem = lambda name: nc_sem(nc, c, name)
    rooted, lnstep, normed, passed, step, powd = (sem(s) for s in "rooted lnstep normed passed step powd".split())
    xin, stored = [sem("xin0"), sem("xin1")], [sem("stored0"), sem("stored1")]
    with ExitStack() as ctx:
        sb = lambda name, shape, dt: ctx.enter_context(nc.sbuf_tensor(f"prep_{name}", shape, dt))
        x, xn, xs = (sb(n, [P, 2, UNROLL, D], F32) for n in ("x", "xn", "xs"))
        half = sb("half", [P, TILES], F32)
        ln = ln_buffers(sb)
        block = ctx.enter_context(nc.Block())

        @block.sync
        def _(sp):
            def load(g, s, j):
                sp.wait_ge(normed, g + 1)
                sp.dma_start(x[:, s], rows(c.x2, g, D)).then_inc(xin[s], 16)
            groups(sp, load)

        @block.gpsimd
        def _(pool):
            pool.wait_ge(step, 2)
            pool.tensor_tensor(c.dis[:, :], c.deg[:, :], half[:, :], ALU.pow).then_inc(powd, 1)
            groups(pool, lambda g, s, j: root(pool, c, lnstep, rooted, passed, g, ln[2], ln[3]))

        @block.scalar
        def _(act):
            act.sem_inc(stored[0], 32)
            act.sem_inc(stored[1], 32)

            def store(g, s, j):
                act.wait_ge(normed, g + 3)
                act.dma_start(rows(c.xn2, g, D), xn[:, s]).then_inc(stored[s], 16)
                act.dma_start(rows(c.t_x, g, D), xs[:, s]).then_inc(stored[s], 16)
            groups(act, store)
            act.wait_ge(stored[0], 32 * 5)
            act.wait_ge(stored[1], 32 * 4)

        @block.vector
        def _(dve):
            dve.sem_inc(normed, 2)
            dve.tensor_scalar(half[:, :], c.zeros[:, 0:TILES], -0.5, None, ALU.add).then_inc(step, 1)
            dve.tensor_scalar(c.deg[:, :], c.deg[:, :], 1.0, None, ALU.add).then_inc(step, 1)
            dve.wait_ge(powd, 1)
            dve.tensor_tensor(c.dis[:, TILES - 1:TILES], c.dis[:, TILES - 1:TILES], c.valid[:, 0:1], ALU.mult
                              ).then_inc(step, 1)
            dve.wait_ge(step, 3)

            def body(g, s, j):
                dve.wait_ge(xin[s], 16 * j + 16)
                dve.wait_ge(stored[s], 32 * j + 32)
                normalise(dve, lnstep, rooted, g, x[:, s], xn[:, s], *ln, done=g * LN_STEPS)
                dis = c.dis[:, bass.ds(g * UNROLL, UNROLL)].unsqueeze(2).broadcast_to([P, UNROLL, D])
                dve.tensor_tensor(xs[:, s], xn[:, s], dis, ALU.mult).then_inc(step, 1)
                dve.wait_ge(step, 2 * g + 4)
                dve.sem_inc(passed, 1)
                dve.tensor_copy(c.acc[:, bass.ds(g * (UNROLL * D), UNROLL * D)],
                                xs[:, s].rearrange("p k d -> p (k d)")).then_inc(step, 1)
                dve.wait_ge(step, 2 * g + 5)
                dve.sem_inc(normed, 1)
            groups(dve, body)


def aggregate(nc, c, tag, table):
    c.phase = tag
    sem = lambda name: nc_sem(nc, c, name)
    copied, passed, oh_made, scattered, added = (sem(s) for s in "copied passed oh_made scattered added".split())
    gathered = [sem(f"gathered{k}") for k in range(RING // 4)]
    with ExitStack() as ctx:
        few = ctx.enter_context(nc.sbuf_tensor(f"{tag}_few", [P, 4, 4], I32))
        sent = ctx.enter_context(nc.sbuf_tensor(f"{tag}_sent", [P, RING, D], F32))
        oh = ctx.enter_context(nc.sbuf_tensor(f"{tag}_oh", [P, RING, P], F32))
        ps_sum = ctx.enter_context(nc.psum_tensor(f"{tag}_sum", [P, 4, 512], F32))
        block = ctx.enter_context(nc.Block())

        @block.gpsimd
        def _(pool):
            gather_rows(pool, c.idx_d, few, table, sent, gathered, scattered, copied, passed)

        @block.tensor
        def _(pe):
            pe.sem_inc(scattered, RING)

            def scatter(t, k, turn_):
                if k % 4 == 0:
                    pe.wait_ge(oh_made, 4 * turn_ + k // 4 + 1)
                    pe.wait_ge(gathered[k // 4], 64 * turn_ + 64)
                pe.wait_ge(added, t + 1)
                pe.matmul(ps_sum[:, k % 4, 0:D], oh[:, k, :], sent[:, k, :], start=True, stop=True
                          ).then_inc(scattered, 1)
            skewed(pe, [(0, scatter)], ET, RING)

        @block.vector
        def _(dve):
            dve.sem_inc(added, 4)

            def hots(t, k, turn_):
                if k % 4 == 0:
                    dve.wait_ge(scattered, t + 4)
                    one_hots(dve, c, c.loc_d, oh, t, k).then_inc(oh_made, 1)

            def add(t, k, turn_):
                b = dve.value_load(c.buc_d[0:1, bass.ds(t, 1)], min_val=0, max_val=TILES - 1)
                dve.wait_ge(scattered, t + RING + 1)
                dve.wait_ge(added, t + 4)
                here = c.acc[:, bass.ds(b * D, D)]
                dve.tensor_tensor(here, here, ps_sum[:, k % 4, 0:D], ALU.add).then_inc(added, 1)
            skewed(dve, [(0, hots), (3, add)], ET, RING)
            dve.wait_ge(added, ET + 4)


def conv_hidden(nc, c, W1t, g1, b1, W2t):
    c.phase = "conv"
    FC = IC // P
    NH = UNROLL * P // 2
    LAST = N - (GROUPS - 1) * UNROLL * P - NH
    sem = lambda name: nc_sem(nc, c, name)
    (wloaded, scaled, turned, xt_made, hidden, statted, kept, passed, step, rooted, relued, sent, emptied, out) = (
        sem(s) for s in ("wloaded scaled turned xt_made hidden statted kept passed step rooted relued sent emptied "
                         "out").split())
    stored = [sem("stored0"), sem("stored1")]
    with ExitStack() as ctx:
        sb = lambda name, shape, dt: ctx.enter_context(nc.sbuf_tensor(f"conv_{name}", shape, dt))
        ps = lambda name, shape: ctx.enter_context(nc.psum_tensor(f"conv_ps_{name}", shape, F32))
        w1, w2 = sb("w1", [P, 2, IC], F32), sb("w2", [P, FC, D], F32)
        gb = sb("gb", [P, 2, FC], F32)
        y1 = sb("y1", [P, FC, NP], F32)
        st = sb("st", [P, FC, 2 * GROUPS * 6], F32)
        mv = sb("mv", [P, FC, 2], F32)
        coef = sb("coef", [P, 5, FC], F32)
        ag = sb("ag", [P, UNROLL, D], F32)
        hid = sb("hid", [P, FC, UNROLL * P], F32)
        xt = hid[:, 0:2, :]
        pst, psh = ps("t", [P, 2, 512]), ps("h", [P, 4, 512])
        with nc.Block() as block:
            @block.sync
            def _(sp):
                sp.dma_start(w1[:, :, :], W1t.rearrange("(k p) f -> p k f", p=P)).then_inc(wloaded, 16)
                sp.dma_start(w2[:, :, :], W2t.rearrange("(k p) f -> p k f", p=P)).then_inc(wloaded, 16)
                with nc.allow_non_contiguous_dma("norm weights, one element to a partition"):
                    sp.dma_start(gb[:, 0, :], g1.rearrange("(k p) -> p k", p=P)).then_inc(wloaded, 16)
                    sp.dma_start(gb[:, 1, :], b1.rearrange("(k p) -> p k", p=P)).then_inc(wloaded, 16)
                sp.wait_ge(wloaded, 64)

            @block.vector
            def _(dve):
                dve.sem_inc(turned, 14)

                def body(g, s, j):
                    acc = c.acc[:, bass.ds(g * (UNROLL * D), UNROLL * D)].rearrange("p (k d) -> p k d", d=D)
                    dis = c.dis[:, bass.ds(g * UNROLL, UNROLL)].unsqueeze(2).broadcast_to([P, UNROLL, D])
                    dve.wait_ge(turned, g * UNROLL + 14)
                    dve.tensor_tensor(ag[:, :, :], acc, dis, ALU.mult).then_inc(scaled, 1)
                    for m in range(2 * FC):
                        f, half = m // 2, m % 2
                        n = LAST if isinstance(g, int) and half else NH
                        dve.wait_ge(kept, g * (2 * FC) + m + 5)
                        dve.bn_stats(st[:, f, bass.ds((2 * g + half) * 6, 6)],
                                     y1[:, f, bass.ds(g * (UNROLL * P) + half * NH, n)]).then_inc(statted, 1)
                groups(dve, body)

            @block.scalar
            def _(act):
                act.sem_inc(xt_made, 2)
                act.sem_inc(kept, 4)

                def body(g, s, j):
                    act.wait_ge(hidden, g * (2 * FC) + 4)
                    for k in range(UNROLL):
                        act.wait_ge(turned, g * UNROLL + k + 15)
                        nc.scalar.copy(xt[:, :, k * P:(k + 1) * P],
                                       pst[:, (s + k) % 2, 0:2 * P].rearrange("p (b n) -> p b n", b=2)).then_inc(xt_made, 1)
                    for m in range(2 * FC):
                        f, half = m // 2, m % 2
                        act.wait_ge(hidden, g * (2 * FC) + m + 5)
                        nc.scalar.copy(y1[:, f, bass.ds(g * (UNROLL * P) + half * NH, NH)], psh[:, m % 4, 0:NH]
                                       ).then_inc(kept, 1)
                groups(act, body)

            @block.tensor
            def _(pe):
                pe.sem_inc(hidden, 4)
                pe.wait_ge(wloaded, 64)

                def body(g, s, j):
                    pe.wait_ge(scaled, g + 1)
                    for k in range(UNROLL):
                        pe.wait_ge(xt_made, g * UNROLL + k + 1)
                        for b in range(2):
                            last = pe.transpose(pst[:, (s + k) % 2, b * P:(b + 1) * P], ag[:, k, b * P:(b + 1) * P],
                                                c.ident[:, :])
                        last.then_inc(turned, 1)
                    pe.wait_ge(xt_made, g * UNROLL + UNROLL + 2)
                    for m in range(2 * FC):
                        f, half = m // 2, m % 2
                        pe.wait_ge(kept, g * (2 * FC) + m + 1)
                        for b in range(2):
                            last = pe.matmul(psh[:, m % 4, 0:NH], w1[:, b, f * P:(f + 1) * P],
                                             xt[:, b, half * NH:(half + 1) * NH], start=(b == 0), stop=(b == 1))
                        last.then_inc(hidden, 1)
                groups(pe, body)

        psy = ps("y", [P, 2, 512])
        block = ctx.enter_context(nc.Block())

        @block.gpsimd
        def _(pool):
            pool.wait_ge(step, 2)
            pool.tensor_tensor(coef[:, 1, :], coef[:, 0, :], c.neghalf[:, 0:FC], ALU.pow).then_inc(rooted, 1)

        @block.vector
        def _(dve):
            n = [0]

            def do(ins):
                ins.then_inc(step, 1)
                n[0] += 1
                dve.wait_ge(step, n[0])

            dve.sem_inc(emptied, 2)
            for f in range(FC):
                last = dve.bn_aggr(mv[:, f, :], st[:, f, :])
            do(last)
            do(dve.tensor_scalar(coef[:, 0, :], mv[:, :, 1], EPS, None, ALU.add))
            dve.wait_ge(rooted, 1)
            do(dve.tensor_tensor(coef[:, 2, :], coef[:, 1, :], gb[:, 0, :], ALU.mult))
            do(dve.tensor_tensor(coef[:, 3, :], mv[:, :, 0], coef[:, 2, :], ALU.mult))
            do(dve.tensor_tensor(coef[:, 4, :], gb[:, 1, :], coef[:, 3, :], ALU.subtract))
            base = n[0]

            def body(g, s, j):
                for k in range(UNROLL):
                    if k == 0:
                        dve.wait_ge(stored[0], 16 * g + 16)
                    at = base + g * (UNROLL + 1)
                    dve.wait_ge(sent, g * UNROLL + k + 2)
                    dve.tensor_scalar(ag[:, k, :], psy[:, (s + k) % 2, 0:D], c.dis[:, bass.ds(g * UNROLL + k, 1)], None,
                                      ALU.mult).then_inc(step, 1)
                    dve.wait_ge(step, at + k + 1)
                    dve.sem_inc(emptied, 1)
                dve.sem_inc(passed, 1)
                dve.tensor_copy(c.acc[:, bass.ds(g * (UNROLL * D), UNROLL * D)],
                                ag[:, :, :].rearrange("p k d -> p (k d)")).then_inc(step, 1)
                dve.wait_ge(step, base + g * (UNROLL + 1) + UNROLL + 1)
                dve.sem_inc(out, 1)
            groups(dve, body)

        @block.sync
        def _(sp):
            sp.sem_inc(stored[0], 16)

            def store(g, s, j):
                sp.wait_ge(out, g + 1)
                sp.dma_start(rows(c.t_x, g, D), ag[:, :, :]).then_inc(stored[0], 16)
            groups(sp, store)
            sp.wait_ge(stored[0], 16 * 8)

        @block.scalar
        def _(act):
            act.wait_ge(step, 5)

            def body(g, s, j):
                act.wait_ge(sent, g * UNROLL + 1)
                for f in range(FC):
                    last = nc.scalar.activation(hid[:, f, :], y1[:, f, bass.ds(g * (UNROLL * P), UNROLL * P)], ACT.Relu,
                                                bias=coef[:, 4, f:f + 1], scale=coef[:, 2, f:f + 1])
                last.then_inc(relued, 1)
            groups(act, body)

        @block.tensor
        def _(pe):
            pe.sem_inc(sent, 1)

            def body(g, s, j):
                pe.wait_ge(relued, g + 1)
                for k in range(UNROLL):
                    pe.wait_ge(emptied, g * UNROLL + k + 1)
                    for f in range(FC):
                        last = pe.matmul(psy[:, (s + k) % 2, 0:D], hid[:, f, k * P:(k + 1) * P], w2[:, f, :], start=(f == 0),
                                         stop=(f == FC - 1))
                    last.then_inc(sent, 1)
            groups(pe, body)


def close_conv(nc, c, g2, b2, gate_w, gate_b):
    c.phase = "closeconv"
    sem = lambda name: nc_sem(nc, c, name)
    (loaded, scaled, meaned, squared, used, varied, step, rooted, lnstep, passed, normed, turned, xt_made, given,
     taken, done2) = (sem(s) for s in ("loaded scaled meaned squared used varied step rooted lnstep passed normed "
                                       "turned xt_made given taken done2").split())
    xin, stored = [sem("xin0"), sem("xin1")], [sem("stored0"), sem("stored1")]
    with ExitStack() as ctx:
        sb = lambda name, shape, dt: ctx.enter_context(nc.sbuf_tensor(f"closeconv_{name}", shape, dt))
        ps = lambda name, shape: ctx.enter_context(nc.psum_tensor(f"closeconv_ps_{name}", shape, F32))
        gam, bet, mean, rstd, nh = (sb(n, [P, D], F32) for n in ("gam", "bet", "bmean", "brstd", "nh"))
        gw, gb = sb("gw", [P, 2, X1], F32), sb("gb", [P, X1], F32)
        vones = sb("vones", [P, P], F32)
        sq = sb("sq", [P, 2, UNROLL, D], F32)
        ps_m, ps_v = ps("m", [P, 512]), ps("v", [P, 512])
        with nc.Block() as block:
            @block.sync
            def _(sp):
                for t, d in ((gam, g2), (bet, b2), (gb, gate_b)):
                    sp.dma_start(t[:, :], d.rearrange("(a e) -> a e", a=1).broadcast_to([P, d.shape[0]])
                                 ).then_inc(loaded, 16)
                sp.dma_start(gw[:, :, :], gate_w.rearrange("(k p) e -> p k e", p=P)).then_inc(loaded, 16)
                sp.wait_ge(loaded, 64)

            @block.tensor
            def _(pe):
                pe.sem_inc(used, 2)
                pe.wait_ge(step, 2)
                pe.matmul(ps_m[:, 0:D], c.zeros[:, 0:P], c.zeros[:, 0:D], start=True, stop=False)

                def add(g, s, j):
                    pe.wait_ge(scaled, g + 1)
                    for k in range(UNROLL):
                        last = pe.matmul(ps_m[:, 0:D], c.ones[:, :], sq[:, s, k, :], start=False, stop=False)
                    last.then_inc(used, 1)
                groups(pe, add)
                pe.matmul(ps_m[:, 0:D], c.zeros[:, 0:P], c.zeros[:, 0:D], start=False, stop=True).then_inc(meaned, 1)
                pe.matmul(ps_v[:, 0:D], c.zeros[:, 0:P], c.zeros[:, 0:D], start=True, stop=False)

                def add_squares(g, s, j):
                    pe.wait_ge(squared, g + 1)
                    for k in range(UNROLL):
                        real = vones if isinstance(g, int) and k == UNROLL - 1 else c.ones
                        last = pe.matmul(ps_v[:, 0:D], real[:, :], sq[:, s, k, :], start=False, stop=False)
                    last.then_inc(used, 1)
                groups(pe, add_squares)
                pe.matmul(ps_v[:, 0:D], c.zeros[:, 0:P], c.zeros[:, 0:D], start=False, stop=True).then_inc(meaned, 1)

            @block.gpsimd
            def _(pool):
                pool.wait_ge(varied, 1)
                pool.tensor_tensor(rstd[:, :], mean[:, :], nh[:, :], ALU.pow).then_inc(rooted, 1)

            @block.vector
            def _(dve):
                n = [0]

                def do(ins):
                    ins.then_inc(step, 1)
                    n[0] += 1
                    dve.wait_ge(step, n[0])

                do(dve.tensor_scalar(vones[:, :], c.ones[:, :], c.valid[:, 0:1], None, ALU.mult))
                do(dve.tensor_scalar(nh[:, :], c.zeros[:, 0:D], -0.5, None, ALU.add))
                view = lambda g: c.acc[:, bass.ds(g * (UNROLL * D), UNROLL * D)].rearrange("p (k d) -> p k d", d=D)

                def scale(g, s, j):
                    dis = c.dis[:, bass.ds(g * UNROLL, UNROLL)].unsqueeze(2).broadcast_to([P, UNROLL, D])
                    dve.wait_ge(used, g + 1)
                    dve.tensor_tensor(sq[:, s], view(g), dis, ALU.mult).then_inc(scaled, 1)
                    dve.wait_ge(scaled, g + 1)
                    dve.sem_inc(passed, 1)
                    dve.tensor_copy(view(g), sq[:, s]).then_inc(done2, 1)
                groups(dve, scale)
                dve.wait_ge(meaned, 1)
                dve.wait_ge(done2, GROUPS)
                do(dve.tensor_scalar(mean[:, :], ps_m[:, 0:D], 1.0 / N, None, ALU.mult))
                wide = mean[:, :].unsqueeze(1).broadcast_to([P, UNROLL, D])

                def square(g, s, j):
                    dve.wait_ge(used, g + GROUPS + 1)
                    dve.tensor_tensor(view(g), view(g), wide, ALU.subtract).then_inc(done2, 1)
                    dve.wait_ge(done2, g + GROUPS + 1)
                    dve.tensor_tensor(sq[:, s], view(g), view(g), ALU.mult).then_inc(squared, 1)
                groups(dve, square)
                dve.wait_ge(meaned, 2)
                dve.wait_ge(squared, GROUPS)
                dve.tensor_scalar(mean[:, :], ps_v[:, 0:D], 1.0 / N, EPS, ALU.mult, ALU.add).then_inc(varied, 1)
                dve.wait_ge(rooted, 1)
                dve.wait_ge(loaded, 64)
                do(dve.tensor_tensor(gam[:, :], gam[:, :], rstd[:, :], ALU.mult))

        x, xn, xr = (sb(n, [P, 2, UNROLL, D], F32) for n in ("x", "xn", "xr"))
        x3 = sq
        ln = ln_buffers(sb)
        xt = sb("xt", [P, 2, 2, P], F32)
        pst, psg = ps("t", [P, 2, 512]), ps("g", [P, 2, 512])
        block = ctx.enter_context(nc.Block())
        base = 4

        @block.sync
        def _(sp):
            def load(g, s, j):
                sp.wait_ge(normed, g + 1)
                sp.dma_start(xr[:, s], rows(c.x2, g, D)).then_inc(xin[s], 16)
                sp.dma_start(x[:, s], rows(c.xn2, g, D)).then_inc(xin[s], 16)
            groups(sp, load)

        @block.gpsimd
        def _(pool):
            groups(pool, lambda g, s, j: root(pool, c, lnstep, rooted, passed, g + 1, ln[2], ln[3], done=-LN_STEPS))

        @block.vector
        def _(dve):
            dve.sem_inc(normed, 2)
            view = lambda g: c.acc[:, bass.ds(g * (UNROLL * D), UNROLL * D)].rearrange("p (k d) -> p k d", d=D)
            wide = lambda t: t[:, :].unsqueeze(1).broadcast_to([P, UNROLL, D])

            def body(g, s, j):
                at = base + 4 * g

                def do(ins, n):
                    ins.then_inc(step, 1)
                    dve.wait_ge(step, at + n)
                dve.wait_ge(xin[s], 32 * j + 32)
                dve.wait_ge(stored[s], 32 * j + 32)
                dve.wait_ge(turned, g * UNROLL + UNROLL)
                do(dve.tensor_tensor(x3[:, s], view(g), wide(gam), ALU.mult), 1)
                do(dve.tensor_tensor(x3[:, s], x3[:, s], wide(bet), ALU.add), 2)
                do(dve.tensor_tensor(x3[:, s], x3[:, s], x[:, s], ALU.add), 3)
                do(dve.scalar_tensor_tensor(out=x3[:, s].rearrange("p k d -> p (k d)"),
                                            in0=x3[:, s].rearrange("p k d -> p (k d)"), scalar=0.0,
                                            in1=xr[:, s].rearrange("p k d -> p (k d)"), op0=ALU.max, op1=ALU.add), 4)
                normalise(dve, lnstep, rooted, g + 1, x3[:, s], xn[:, s], *ln, done=g * LN_STEPS)
                dve.sem_inc(normed, 1)
                dve.wait_ge(given, g + 1)
                dve.tensor_tensor(c.logit[:, bass.ds(g * (UNROLL * X1), UNROLL * X1)].rearrange("p (k e) -> p k e", e=X1),
                                  psg[:, s, 0:UNROLL * X1].rearrange("p (k e) -> p k e", e=X1),
                                  gb[:, :].unsqueeze(1).broadcast_to([P, UNROLL, X1]), ALU.add).then_inc(taken, 1)
            groups(dve, body)
            dve.wait_ge(taken, GROUPS)

        @block.scalar
        def _(act):
            act.sem_inc(xt_made, 2)
            act.sem_inc(stored[0], 32)
            act.sem_inc(stored[1], 32)

            def body(g, s, j):
                act.wait_ge(normed, g + 3)
                act.dma_start(rows(c.x3, g, D), x3[:, s]).then_inc(stored[s], 16)
                act.dma_start(rows(c.xn3, g, D), xn[:, s]).then_inc(stored[s], 16)
                for k in range(UNROLL):
                    act.wait_ge(turned, g * UNROLL + k + 15)
                    nc.scalar.copy(xt[:, (s + k) % 2], pst[:, (s + k) % 2, 0:2 * P].rearrange("p (b n) -> p b n", b=2)
                                   ).then_inc(xt_made, 1)
            groups(act, body)
            act.wait_ge(stored[0], 32 * 5)
            act.wait_ge(stored[1], 32 * 4)

        @block.tensor
        def _(pe):
            pe.sem_inc(turned, 14)

            def body(g, s, j):
                pe.wait_ge(normed, g + 3)
                for k in range(UNROLL):
                    q = (s + k) % 2
                    pe.wait_ge(xt_made, g * UNROLL + k + 1)
                    for b in range(2):
                        last = pe.transpose(pst[:, q, b * P:(b + 1) * P], xn[:, s, k, b * P:(b + 1) * P], c.ident[:, :])
                    last.then_inc(turned, 1)
                    pe.wait_ge(xt_made, g * UNROLL + k + 3)
                    for b in range(2):
                        last = pe.matmul(psg[:, s, k * X1:(k + 1) * X1], xt[:, q, b, :], gw[:, b, :], start=(b == 0),
                                         stop=(b == 1))
                last.then_inc(given, 1)
            groups(pe, body)


def route(nc, c):
    c.phase = "route"
    sem = lambda name: nc_sem(nc, c, name)
    step, given, peed = (sem(s) for s in "step given peed".split())
    T8 = TILES * X1
    with ExitStack() as ctx:
        sb = lambda name, shape, dt: ctx.enter_context(nc.sbuf_tensor(f"route_{name}", shape, dt))
        p, e, oh, inc, tot, before, tmp = (sb(n, [P, T8], F32) for n in "p e oh inc tot before tmp".split())
        mx, sm, pm, idx, pos, kept, to, node = (sb(n, [P, TILES], F32) for n in "mx sm pm idx pos kept to node".split())
        ps1, ps2 = (ctx.enter_context(nc.psum_tensor(f"route_ps{m}", [P, 512], F32)) for m in range(2))
        block = ctx.enter_context(nc.Block())
        te = lambda t: t[:, :].rearrange("p (t e) -> p t e", e=X1)
        et = lambda t: t[:, :].rearrange("p (e t) -> p e t", e=X1)
        w8 = lambda t: t[:, :].unsqueeze(2).broadcast_to([P, TILES, X1])

        @block.gpsimd
        def _(pool):
            nc.gpsimd.iota(node[:, :], [[P, TILES]], base=0, channel_multiplier=1,
                           allow_small_or_imprecise_dtypes=True).then_inc(peed, 1)

        @block.scalar
        def _(act):
            act.wait_ge(given, 1)
            nc.scalar.activation(e[:, :], p[:, :], ACT.Exp).then_inc(peed, 1)

        @block.tensor
        def _(pe):
            pe.wait_ge(given, 2)
            pe.matmul(ps1[:, 0:T8], c.below[:, :], oh[:, :], start=True, stop=True)
            pe.matmul(ps2[:, 0:T8], c.ones[:, :], oh[:, :], start=True, stop=True).then_inc(peed, 1)

        @block.vector
        def _(dve):
            n = [0]

            def do(ins):
                ins.then_inc(step, 1)
                n[0] += 1
                dve.wait_ge(step, n[0])

            do(dve.tensor_reduce(mx[:, :], te(c.logit), AX.X, ALU.max))
            do(dve.tensor_tensor(te(p), te(c.logit), w8(mx), ALU.subtract))
            dve.sem_inc(given, 1)
            dve.wait_ge(peed, 2)
            do(dve.tensor_reduce(sm[:, :], te(e), AX.X, ALU.add))
            do(dve.reciprocal(sm[:, :], sm[:, :]))
            do(dve.tensor_tensor(te(p), te(e), w8(sm), ALU.mult))
            do(dve.tensor_reduce(pm[:, :], te(p), AX.X, ALU.max))
            do(dve.tensor_tensor(te(oh), te(p), w8(pm), ALU.is_lt))
            eight = c.iota[:, 0:X1].unsqueeze(1).broadcast_to([P, TILES, X1])
            do(dve.tensor_scalar(oh[:, :], oh[:, :], 100.0, None, ALU.mult))
            do(dve.tensor_tensor(te(tmp), te(oh), eight, ALU.add))
            do(dve.tensor_reduce(idx[:, :], te(tmp), AX.X, ALU.min))
            do(dve.tensor_tensor(te(oh), w8(idx), eight, ALU.is_equal))
            do(dve.tensor_scalar(oh[:, T8 - X1:T8], oh[:, T8 - X1:T8], c.valid[:, 0:1], None, ALU.mult))
            dve.sem_inc(given, 1)
            dve.wait_ge(peed, 3)
            do(dve.tensor_copy(et(tot), ps2[:, 0:T8].rearrange("p (t e) -> p e t", e=X1)))
            for x in range(X1):
                last = dve.tensor_tensor_scan(inc[:, x * TILES:(x + 1) * TILES], tot[:, x * TILES:(x + 1) * TILES],
                                              c.zeros[:, 0:TILES], 0.0, ALU.add, ALU.add)
            do(last)
            do(dve.tensor_tensor(before[:, :], inc[:, :], tot[:, :], ALU.subtract))
            do(dve.tensor_tensor(te(tmp), before[:, :].rearrange("p (e t) -> p t e", e=X1), te(ps1[:, 0:T8]), ALU.add))
            do(dve.tensor_tensor(tmp[:, :], tmp[:, :], oh[:, :], ALU.mult))
            do(dve.tensor_reduce(pos[:, :], te(tmp), AX.X, ALU.add))
            do(dve.tensor_scalar(kept[:, :], pos[:, :], float(CAP), None, ALU.is_lt))
            do(dve.tensor_scalar(kept[:, TILES - 1:TILES], kept[:, TILES - 1:TILES], c.valid[:, 0:1], None, ALU.mult))
            do(dve.tensor_tensor(c.gate[:, :], pm[:, :], kept[:, :], ALU.mult))
            do(dve.tensor_scalar(pos[:, :], pos[:, :], float(CAP - 1), None, ALU.min))
            do(dve.tensor_scalar(sm[:, :], idx[:, :], float(CAP), None, ALU.mult))
            do(dve.tensor_tensor(c.take[:, :], pos[:, :], sm[:, :], ALU.add))
            do(dve.tensor_scalar(idx[:, :], idx[:, :], float(SLOTS), None, ALU.mult))
            do(dve.tensor_tensor(pos[:, :], pos[:, :], idx[:, :], ALU.add))
            do(dve.tensor_scalar(node[:, :], node[:, :], float(X1 * SLOTS), None, ALU.add))
            do(dve.tensor_tensor(to[:, :], pos[:, :], node[:, :], ALU.subtract))
            do(dve.tensor_tensor(to[:, :], to[:, :], kept[:, :], ALU.mult))
            do(dve.tensor_tensor(c.put[:, :], to[:, :], node[:, :], ALU.add))


def dispatch(nc, c):
    c.phase = "dispatch"
    sem = lambda name: nc_sem(nc, c, name)
    copied, passed, free = (sem(s) for s in "copied passed free".split())
    xin, sent = [sem("xin0"), sem("xin1")], [sem("sent0"), sem("sent1")]
    with ExitStack() as ctx:
        sb = lambda name, shape, dt: ctx.enter_context(nc.sbuf_tensor(f"dispatch_{name}", shape, dt))
        x = sb("x", [P, 2, UNROLL, D], F32)
        few = sb("few", [P, 2, UNROLL], I32)
        block = ctx.enter_context(nc.Block())

        @block.sync
        def _(sp):
            def load(g, s, j):
                sp.wait_ge(free, g + 1)
                sp.dma_start(x[:, s], rows(c.xn3, g, D)).then_inc(xin[s], 16)
            groups(sp, load)

        @block.gpsimd
        def _(pool):
            pool.sem_inc(free, 2)

            def send(g, s, j):
                pool.wait_ge(xin[s], 16 * j + 16)
                pool.sem_inc(passed, 1)
                pool.tensor_copy(few[:, s, :], c.put[:, bass.ds(g * UNROLL, UNROLL)]).then_inc(copied, 1)
                pool.wait_ge(copied, g + 1)
                pool.sem_inc(passed, 1)
                for k in range(UNROLL):
                    pool.indirect_dma_start(out=c.slots_in[:, :], in_=x[:, s, k, :], in_offset=None,
                                            out_offset=bass.IndirectOffsetOnAxis(ap=few[:, s, k:k + 1], axis=0)
                                            ).then_inc(sent[s], 16)
                pool.wait_ge(sent[s], 16 * UNROLL * j + 16 * UNROLL)
                pool.sem_inc(free, 1)
            groups(pool, send)


def experts1(nc, c, w1, b1, w2, b2):
    c.phase = "experts1"
    FC, TC = F1 // P, SLOTS // P
    HALVES = ((0, 489), (489, CAP))
    LASTM = CAP - (TC - 1) * P
    sem = lambda name: nc_sem(nc, c, name)
    (turned, xt_made, hidden, relued, mixed, emptied, wfree, yfree, passed) = (
        sem(s) for s in "turned xt_made hidden relued mixed emptied wfree yfree passed".split())
    loaded, stored = [sem("loaded0"), sem("loaded1")], [sem("stored0"), sem("stored1")]
    with ExitStack() as ctx:
        sb = lambda name, shape, dt: ctx.enter_context(nc.sbuf_tensor(f"experts1_{name}", shape, dt))
        ps = lambda name, shape: ctx.enter_context(nc.psum_tensor(f"experts1_ps_{name}", shape, F32))
        x = sb("x", [P, 2, TC, D], F32)
        w1s, w2s = sb("w1", [P, 2, 2, F1], F32), sb("w2", [P, 2, FC, D], F32)
        b1s, b2s = sb("b1", [P, 2, FC], F32), sb("b2", [P, 2, D], F32)
        xt = sb("xt", [P, 2, SLOTS], F32)
        hid = sb("hid", [P, FC, SLOTS], F32)
        y = sb("y", [P, 2, TC, D], F32)
        pst, psh, psy = ps("t", [P, 2, 512]), ps("h", [P, 2, 512]), ps("y", [P, 2, 512])
        block = ctx.enter_context(nc.Block())

        def experts(eng, body):
            with eng.Fori(0, X1 // 2) as i:
                body(2 * i, 0, i)
                body(2 * i + 1, 1, i)

        @block.sync
        def _(sp):
            def load(e, s, j):
                sp.wait_ge(wfree, e + 1)
                one = bass.ds(e, 1)
                sp.dma_start(x[:, s], c.slots_in[bass.ds(e * SLOTS, SLOTS), :].rearrange("(k p) d -> p k d", p=P)
                             ).then_inc(loaded[s], 16)
                sp.dma_start(w1s[:, s], w1[one].rearrange("a (k p) f -> p (a k) f", p=P)).then_inc(loaded[s], 16)
                sp.dma_start(w2s[:, s], w2[one].rearrange("a (k p) f -> p (a k) f", p=P)).then_inc(loaded[s], 16)
                with nc.allow_non_contiguous_dma("a bias, one element to a partition"):
                    sp.dma_start(b1s[:, s, :], b1[one].rearrange("a (k p) -> p (a k)", p=P)).then_inc(loaded[s], 16)
                sp.dma_start(b2s[:, s, :], b2[one].broadcast_to([P, D])).then_inc(loaded[s], 16)
            experts(sp, load)

        @block.tensor
        def _(pe):
            pe.sem_inc(hidden, 2)
            pe.sem_inc(mixed, 1)

            def body(e, s, j):
                pe.wait_ge(loaded[s], 80 * j + 80)
                for k in range(TC):
                    pe.wait_ge(xt_made, e * TC + k + 1)
                    for b in range(2):
                        last = pe.transpose(pst[:, k % 2, b * P:(b + 1) * P], x[:, s, k, b * P:(b + 1) * P],
                                            c.ident[:, :])
                    last.then_inc(turned, 1)
                pe.wait_ge(xt_made, e * TC + TC + 2)
                for m in range(2 * FC):
                    f, (lo, hi) = m // 2, HALVES[m % 2]
                    pe.wait_ge(relued, e * (2 * FC) + m + 1)
                    for b in range(2):
                        last = pe.matmul(psh[:, m % 2, 0:hi - lo], w1s[:, s, b, f * P:(f + 1) * P], xt[:, b, lo:hi],
                                         start=(b == 0), stop=(b == 1))
                    last.then_inc(hidden, 1)
                pe.wait_ge(relued, e * (2 * FC) + 2 * FC + 2)
                for k in range(TC):
                    n = LASTM if k == TC - 1 else P
                    pe.wait_ge(emptied, e * TC + k + 1)
                    for f in range(FC):
                        last = pe.matmul(psy[0:n, k % 2, 0:D], hid[:, f, k * P:k * P + n], w2s[:, s, f, :],
                                         start=(f == 0), stop=(f == FC - 1))
                    last.then_inc(mixed, 1)
            experts(pe, body)

        @block.scalar
        def _(act):
            act.sem_inc(xt_made, 2)
            act.sem_inc(relued, 2)

            def body(e, s, j):
                act.wait_ge(loaded[s], 80 * j + 80)
                act.wait_ge(hidden, e * (2 * FC) + 2)
                for k in range(TC):
                    act.wait_ge(turned, e * TC + k + 1)
                    nc.scalar.copy(xt[:, :, k * P:(k + 1) * P],
                                   pst[:, k % 2, 0:2 * P].rearrange("p (b n) -> p b n", b=2)).then_inc(xt_made, 1)
                act.wait_ge(mixed, e * TC + 1)
                for m in range(2 * FC):
                    f, (lo, hi) = m // 2, HALVES[m % 2]
                    act.wait_ge(hidden, e * (2 * FC) + m + 3)
                    nc.scalar.activation(hid[:, f, lo:hi], psh[:, m % 2, 0:hi - lo], ACT.Relu,
                                         bias=b1s[:, s, f:f + 1]).then_inc(relued, 1)
            experts(act, body)

        @block.vector
        def _(dve):
            dve.sem_inc(emptied, 2)
            dve.sem_inc(wfree, 2)

            def body(e, s, j):
                dve.wait_ge(loaded[s], 80 * j + 80)
                dve.wait_ge(yfree, e + 1)
                for k in range(TC):
                    n = LASTM if k == TC - 1 else P
                    dve.wait_ge(mixed, e * TC + k + 2)
                    last = dve.tensor_tensor(y[0:n, s, k, :], psy[0:n, k % 2, 0:D], b2s[0:n, s, :], ALU.add)
                    last.then_inc(emptied, 1)
                dve.wait_ge(emptied, e * TC + TC + 2)
                dve.sem_inc(wfree, 1)
            experts(dve, body)

        @block.gpsimd
        def _(pool):
            pool.sem_inc(yfree, 2)

            def store(e, s, j):
                pool.wait_ge(wfree, e + 3)
                pool.sem_inc(passed, 1)
                pool.dma_start(c.slots_out[bass.ds(e * CAP, (TC - 1) * P), :].rearrange("(k p) d -> p k d", p=P),
                               y[:, s, 0:TC - 1, :]).then_inc(stored[s], 16)
                pool.dma_start(c.slots_out[bass.ds(e * CAP + (TC - 1) * P, LASTM), :], y[0:LASTM, s, TC - 1, :]
                               ).then_inc(stored[s], 16)
                pool.wait_ge(stored[s], 32 * j + 32)
                pool.sem_inc(yfree, 1)
            experts(pool, store)


def combine(nc, c, out):
    c.phase = "combine"
    BIG = 3.4028234663852886e38
    sem = lambda name: nc_sem(nc, c, name)
    copied, passed, summed, step = (sem(s) for s in "copied passed summed step".split())
    xin, got, stored = ([sem(f"{n}0"), sem(f"{n}1")] for n in ("xin", "got", "stored"))
    with ExitStack() as ctx:
        sb = lambda name, shape, dt: ctx.enter_context(nc.sbuf_tensor(f"combine_{name}", shape, dt))
        x, y, z, o = (sb(n, [P, 2, UNROLL * D], F32) for n in "xyzo")
        fill = sb("fill", [P, 3, UNROLL * D], F32)
        mask = sb("mask", [P, 2, 3, UNROLL * D], I32)
        few = sb("few", [P, 2, UNROLL], I32)
        block = ctx.enter_context(nc.Block())
        tiles = lambda t, s: t[:, s, :].rearrange("p (k d) -> p k d", d=D)

        @block.sync
        def _(sp):
            def load(g, s, j):
                sp.wait_ge(summed, g + 1)
                sp.dma_start(tiles(x, s), rows(c.x3, g, D)).then_inc(xin[s], 16)
            groups(sp, load)

        @block.gpsimd
        def _(pool):
            def fetch(g, s, j):
                pool.wait_ge(summed, g + 1)
                pool.sem_inc(passed, 1)
                pool.tensor_copy(few[:, s, :], c.take[:, bass.ds(g * UNROLL, UNROLL)]).then_inc(copied, 1)
                pool.wait_ge(copied, g + 1)
                pool.sem_inc(passed, 1)
                for k in range(UNROLL):
                    pool.indirect_dma_start(out=y[:, s, k * D:(k + 1) * D], out_offset=None, in_=c.slots_out[:, :],
                                            in_offset=bass.IndirectOffsetOnAxis(ap=few[:, s, k:k + 1], axis=0)
                                            ).then_inc(got[s], 16)
            groups(pool, fetch)

        @block.vector
        def _(dve):
            dve.sem_inc(summed, 2)
            dve.memset(fill[:, 0, :], 0.0).then_inc(step, 1)
            dve.memset(fill[:, 1, :], 1e4).then_inc(step, 1)
            dve.memset(fill[:, 2, :], -1e4).then_inc(step, 1)
            dve.wait_ge(step, 3)

            def body(g, s, j):
                def do(ins, n):
                    ins.then_inc(step, 1)
                    dve.wait_ge(step, 8 * g + 3 + n)
                gate = c.gate[:, bass.ds(g * UNROLL, UNROLL)].unsqueeze(2).broadcast_to([P, UNROLL, D])
                dve.wait_ge(got[s], 16 * UNROLL * j + 16 * UNROLL)
                dve.wait_ge(xin[s], 16 * j + 16)
                dve.wait_ge(stored[s], 16 * j + 16)
                do(dve.tensor_tensor(tiles(z, s), tiles(y, s), gate, ALU.mult), 1)
                do(dve.tensor_tensor(mask[:, s, 0, :], z[:, s], z[:, s], ALU.not_equal), 2)
                do(dve.tensor_scalar(mask[:, s, 1, :], z[:, s], BIG, None, ALU.is_gt), 3)
                do(dve.tensor_scalar(mask[:, s, 2, :], z[:, s], -BIG, None, ALU.is_lt), 4)
                for m in range(3):
                    dve.sem_inc(passed, 1)
                    dve.copy_predicated(z[:, s], mask[:, s, m, :], fill[:, m, :]).then_inc(step, 1)
                    dve.wait_ge(step, 8 * g + 8 + m)
                do(dve.tensor_tensor(o[:, s], z[:, s], x[:, s], ALU.add), 8)
                dve.sem_inc(summed, 1)
            groups(dve, body)

        @block.scalar
        def _(act):
            act.sem_inc(stored[0], 16)
            act.sem_inc(stored[1], 16)

            def store(g, s, j):
                act.wait_ge(summed, g + 3)
                if isinstance(g, int):
                    at = g * UNROLL * P
                    full = (N - at) // P
                    act.dma_start(out[at:at + full * P, :].rearrange("(k p) d -> p k d", p=P), tiles(o, s)[:, 0:full]
                                  ).then_inc(stored[s], 16)
                    act.dma_start(out[at + full * P:N, :], tiles(o, s)[0:(N - at) % P, full, :]
                                  ).then_inc(stored[s], 16)
                else:
                    act.dma_start(rows(out, g, D), tiles(o, s)).then_inc(stored[s], 16)
            groups(act, store)
            act.wait_ge(stored[0], 16 * 6)
            act.wait_ge(stored[1], 16 * 4)



def build(nc, a, out):
    c = Ctx()
    with ExitStack() as ctx:
        c.ctx = ctx
        c.phase, c.sems = "setup", []
        dram = lambda name, shape, dt=F32: nc.dram_tensor(name, shape, dt, kind="Internal").ap()
        sb = lambda name, shape, dt: ctx.enter_context(nc.sbuf_tensor(name, shape, dt))
        c.x0, c.x1, c.xn1, c.x2, c.xn2, c.x3, c.xn3, c.t_x = (
            dram(name, [NP, D]) for name in ("x0", "x1", "xn1", "x2", "xn2", "x3", "xn3", "t_x"))
        c.t_h, c.t_hr = dram("t_h", [NP, D + 4]), dram("t_hr", [NP, 4])
        c.slots_in = dram("slots_in", [X1 * SLOTS + NP, D])
        c.slots_dst = dram("slots_dst", [P * ET, 2], I32)
        c.slots_out = dram("slots_out", [X1 * CAP, D])
        setup(nc, c, ctx, a["x"])
        c.idx_d, c.loc_d, c.buc_d = sb("idx_d", [P, ET + 4], I32), sb("loc_d", [P, ET], F32), sb("buc_d", [1, ET], I32)
        c.deg, c.dis = sb("deg", [P, TILES], F32), sb("dis", [P, TILES], F32)
        c.colsum, c.share, c.chosen = sb("colsum", [P, 2], F32), sb("share", [P, 2], F32), sb("chosen", [1, 2], I32)
        c.logit = sb("logit", [P, TILES * X1], F32)
        c.put, c.take, c.gate = sb("put", [P, TILES], I32), sb("take", [P, TILES], I32), sb("gate", [P, TILES], F32)
        with ExitStack() as att:
            sa = lambda name, shape, dt: att.enter_context(nc.sbuf_tensor(name, shape, dt))
            c.idx_s, c.loc_s, c.buc_s = sa("idx_s", [P, ET + 4], I32), sa("loc_s", [P, ET], F32), sa("buc_s", [1, ET], I32)
            sort_edges(nc, c, a["src"], a["dst"])
            c.hlm = sa("hlm", [P, TILES * 8], F32)
            c.acc = sa("acc_heads", [P, TILES * (D + 4)], F32)
            project_heads(nc, c, a["L0_gnn_W"], a["L0_gnn_a_l"], a["L0_gnn_a_r"])
            neighbour_max(nc, c)
            attend(nc, c)
            close_attention(nc, c)
        recycle(nc, c)
        choose_experts(nc, c, a["L0_ffn_Wr"], a["L0_ffn_br"])
        experts0(nc, c, a["L0_ffn_W1"], a["L0_ffn_b1"], a["L0_ffn_W2"], a["L0_ffn_b2"], a["L0_ffn_gamma"],
                 a["L0_ffn_beta"])
        with ExitStack() as conv:
            c.acc = conv.enter_context(nc.sbuf_tensor("acc_conv", [P, TILES * D], F32))
            prepare_conv(nc, c)
            aggregate(nc, c, "conv1", c.t_x)
            conv_hidden(nc, c, a["L1_gnn_W1"], a["L1_gnn_g1"], a["L1_gnn_b1"], a["L1_gnn_W2"])
            aggregate(nc, c, "conv2", c.t_x)
            recycle(nc, c)
            close_conv(nc, c, a["L1_gnn_g2"], a["L1_gnn_b2"], a["L1_ffn_gate_w"], a["L1_ffn_gate_b"])
        route(nc, c)
        dispatch(nc, c)
        experts1(nc, c, a["L1_ffn_w1"], a["L1_ffn_b1"], a["L1_ffn_w2"], a["L1_ffn_b2"])
        combine(nc, c, out)


_INS = ['x', 'src', 'dst', 'L0_gnn_W', 'L0_gnn_a_l', 'L0_gnn_a_r', 'L0_ffn_Wr', 'L0_ffn_br', 'L0_ffn_W1',
        'L0_ffn_b1', 'L0_ffn_W2', 'L0_ffn_b2', 'L0_ffn_gamma', 'L0_ffn_beta', 'L1_gnn_W1', 'L1_gnn_g1', 'L1_gnn_b1',
        'L1_gnn_W2', 'L1_gnn_g2', 'L1_gnn_b2', 'L1_ffn_gate_w', 'L1_ffn_gate_b', 'L1_ffn_w1', 'L1_ffn_b1',
        'L1_ffn_w2', 'L1_ffn_b2']
_TURNED = ('L1_gnn_W1', 'L1_gnn_W2')
_OUTS = [((N, D), 'float32')]


def kernel(**inputs):
    import numpy as _np
    import concourse.bacc as _bacc
    from concourse import mybir as _mybir
    from concourse.bass_utils import run_bass_kernel_spmd as _run

    nc = _bacc.Bacc("TRN2", target_bir_lowering=False, num_devices=1)
    arrays, args = {}, {}
    for name in _INS:
        a = _np.asarray(inputs[name])
        a = _np.ascontiguousarray(a.T if name in _TURNED else a)
        arrays[f"in_{name}_dram"] = a
        args[name] = nc.dram_tensor(f"in_{name}_dram", a.shape, _mybir.dt.from_np(a.dtype), kind="ExternalInput").ap()
    outs = []
    for i, (shape, dtype) in enumerate(_OUTS):
        dt = _mybir.dt.from_np(_np.dtype(dtype))
        outs.append(nc.dram_tensor(f"out_{i}_dram", shape, dt, kind="ExternalOutput").ap())
    build(nc, args, outs[0])
    r = _run(nc, [arrays], core_ids=[0])
    got = tuple(r.results[0][f"out_{i}_dram"] for i in range(len(_OUTS)))
    return got[0]
```

```python
from contextlib import ExitStack

import concourse.bass as bass
from concourse import mybir

ALU = mybir.AluOpType
ACT = mybir.ActivationFunctionType
AX = mybir.AxisListType
F32 = mybir.dt.float32
F16 = mybir.dt.float16
BF16 = mybir.dt.bfloat16
I32 = mybir.dt.int32

P = 128
N = 6250
D = 256
TILES = 49
NP = TILES * P
PADS = NP - N
UNROLL = 7
GROUPS = TILES // UNROLL
E = 100000
EP, EC = 125, 800
ET = 880
PAIR_BITS = 8
PAIR = 1 << PAIR_BITS
PAIRS = ET // 2
HALF = ET // 2
QUAD = 4
QUADS = 4
RING = QUADS * QUAD
DONE = 16 * QUAD
HEADS, HD = 4, 64
ZROW = NP - 1
LOW = -3.0e38
FAR = -1.0e30
F0, X0 = 512, 8
F1, X1 = 1024, 8
CAP0 = 977.0
CAP = 977
IC = 512
SLOTS = 1024
EPS = 1e-5
assert E == EP * EC and (E + TILES * (PAIR - 1)) // PAIR <= PAIRS and ET % RING == 0


class Ctx:
    pass


def groups(eng, body):
    with eng.Fori(0, GROUPS // 2) as i:
        body(2 * i, 0, i)
        body(2 * i + 1, 1, i)
    body(GROUPS - 1, 0, GROUPS // 2)


def rows(dram, g, width):
    return dram[bass.ds(g * (UNROLL * P), UNROLL * P), 0:width].rearrange("(k p) d -> p k d", p=P)


def setup(nc, c, ctx):
    sb = lambda name, shape, dt: ctx.enter_context(nc.sbuf_tensor(name, shape, dt))
    c.iota = sb("iota", [P, ET], F32)
    c.iota16 = sb("iota16", [P, ET], F16)
    c.pidx = sb("pidx", [P, 1], F32)
    c.ident = sb("ident", [P, P], F32)
    c.ones = sb("ones", [P, P], F32)
    c.below = sb("below", [P, P], F32)
    c.upto = sb("upto", [P, P], F32)
    c.zeros = sb("zeros", [P, EC], F32)
    c.zeros16 = sb("zeros16", [P, HALF], F16)
    c.neghalf = sb("neghalf", [P, UNROLL], F32)
    c.valid = sb("valid", [P, 1], F32)
    made = nc_sem(nc, c, "consts_made")
    with nc.Block() as block:
        @block.gpsimd
        def _(pool):
            nc.gpsimd.iota(c.iota[:, :], [[1, ET]], base=0, channel_multiplier=0,
                           allow_small_or_imprecise_dtypes=True).then_inc(made, 1)
            nc.gpsimd.iota(c.iota16[:, :], [[1, ET]], base=0, channel_multiplier=0,
                           allow_small_or_imprecise_dtypes=True).then_inc(made, 1)
            nc.gpsimd.iota(c.pidx[:, :], [[1, 1]], base=0, channel_multiplier=1,
                           allow_small_or_imprecise_dtypes=True).then_inc(made, 1)
            nc.gpsimd.memset(c.neghalf[:, :], -0.5).then_inc(made, 1)
            nc.gpsimd.memset(c.ones[:, :], 1.0).then_inc(made, 1)
            nc.gpsimd.memset(c.zeros[:, :], 0.0).then_inc(made, 1)
            nc.gpsimd.memset(c.zeros16[:, :], 0.0).then_inc(made, 1)

        @block.vector
        def _(dve):
            dve.wait_ge(made, 7)
            dve.tensor_scalar(c.ident[:, :], c.iota[:, 0:P], c.pidx[:, 0:1], None, ALU.is_equal)
            dve.tensor_scalar(c.valid[:, :], c.pidx[:, :], float(P - PADS), None, ALU.is_lt)
            dve.tensor_scalar(c.below[:, :], c.iota[:, 0:P], c.pidx[:, 0:1], None, ALU.is_gt)
            dve.tensor_scalar(c.upto[:, :], c.iota[:, 0:P], c.pidx[:, 0:1], None, ALU.is_ge)


def nc_sem(nc, c, name):
    c.sems.append(nc.alloc_semaphore(name=f"{c.phase}_{name}"))
    return c.sems[-1]


def recycle(nc, c):
    nc.clear_and_free_semaphores(c.sems)
    nc.all_engine_barrier()
    c.sems = []


def skewed(eng, stages, total, u):
    for t in range(u):
        for lag, body in stages:
            if t >= lag:
                body(t - lag, (t - lag) % u, (t - lag) // u)
    with eng.Fori(1, total // u) as i:
        for k in range(u):
            for lag, body in stages:
                body(i * u + (k - lag), (k - lag) % u, i - 1 if k < lag else i)
    for t in range(total, total + max(lag for lag, _ in stages)):
        for lag, body in stages:
            if t - lag < total:
                body(t - lag, (t - lag) % u, (t - lag) // u)


def sort_edges(nc, c, x, src, dst):
    c.phase = "sort"
    sem = lambda name: nc_sem(nc, c, name)
    place_ready, onehot, paid, spread, placed, unpacked = (
        sem(s) for s in "place_ready onehot paid spread placed unpacked".split())
    cleared, emptied_table, positioned, copied, passed, returned = (
        sem(s) for s in "cleared emptied_table positioned copied passed returned".split())
    filled = sem("filled")
    sent = [sem(f"sent{s}") for s in range(4)]
    loaded = {"dst": sem("loaded_dst"), "src": sem("loaded_src")}
    split, counted, summed, based, ended, table, masked, scanned, picked, usedhit, pos_whole = (
        {t: sem(f"{s}_{t}") for t in ("dst", "src")}
        for s in ("split counted summed based ended table masked scanned picked usedhit "
                  "pos_whole").split())
    U = 4
    B = 10
    HC = EC // 2
    with ExitStack() as ctx:
        sb = lambda name, shape, dt: ctx.enter_context(nc.sbuf_tensor(f"sort_{name}", shape, dt))
        ps = lambda name, shape: ctx.enter_context(nc.psum_tensor(f"sort_{name}", shape, F32))
        keys = {t: sb(f"key_{t}", [EP, EC], I32) for t in ("src", "dst")}
        others = {t: sb(f"oth_{t}", [EP, EC], I32) for t in ("src", "dst")}
        tmp_i = sb("tmp_i", [EP, EC], I32)
        pay1, pay2 = sb("pay1", [EP, EC], F32), sb("pay2", [EP, EC], F32)
        hi16, mask = sb("hi16", [EP, EC], F16), sb("mask", [EP, 2, EC], F16)
        cum, hit = sb("cum", [EP, 2, EC], F32), sb("hit", [EP, 2, EC], F32)
        plo, ptile = sb("plo", [EP, EC], F32), sb("ptile", [EP, EC], F32)
        dst_lo, dst_hi = sb("dst_lo", [EP, EC], F32), sb("dst_hi", [EP, EC], F32)
        tot = sb("tot", [EP, TILES], F32)
        small_i = sb("small_i", [P, 2, TILES], I32)
        nt, inc, off = (sb(n, [P, TILES], F32) for n in ("nt", "inc", "off"))
        col_i, col_f, endc = sb("col_i", [TILES, 2], I32), sb("col_f", [TILES, 1], F32), sb("endc", [TILES, 1], F32)
        ge = sb("ge", [TILES, PAIRS], F32)
        whose, ends = sb("whose", [P, PAIRS], F32), sb("ends", [P, PAIRS], F32)
        lo1 = sb("lo1", [EP, U, P], F16)
        l12 = sb("l12", [EP, U, 2, P], F16)
        hot = sb("hot", [EP, U, ET], F16)
        dlo, dhi = sb("dlo", [EP, U, P], F16), sb("dhi", [EP, U, TILES], F16)
        u1, u2, u3 = (sb(n, [P, ET], I32) for n in ("u1", "u2", "u3"))
        trio = sb("trio", [EP, 3, EC], I32)
        few = sb("few", [EP, 4, B, 3], I32)
        back = sb("back", [P, ET, 2], I32)
        accs = [ps("acc1", [P, 2, 512]), ps("acc2", [P, 2, 512])]
        psd, pss = ps("psd", [P, 512]), ps("pss", [P, 512])
        ps_pos = ps("pos", [P, 2, 512])
        block = ctx.enter_context(nc.Block())
        halves = lambda t: t.rearrange("p (a b) -> p a b", a=2)

        @block.sync
        def _(sp):
            for t, (key, other) in (("dst", (dst, src)), ("src", (src, dst))):
                sp.dma_start(keys[t][:, :], key.rearrange("(p c) -> p c", p=EP)).then_inc(loaded[t], 16)
                sp.dma_start(others[t][:, :], other.rearrange("(p c) -> p c", p=EP)).then_inc(loaded[t], 16)
            sp.dma_start(c.x0[0:N, :], x[:, :]).then_inc(filled, 16)
            sp.dma_start(c.x0[N:NP, :], c.zeros[0:PADS, 0:D]).then_inc(filled, 16)
            sp.dma_start(c.slots_in[0:X1 * SLOTS, :].rearrange("(p r) d -> p r d", p=P),
                         c.zeros[:, 0:D].unsqueeze(1).broadcast_to([P, X1 * SLOTS // P, D])).then_inc(filled, 16)
            sp.wait_ge(cleared, 1)
            sp.dma_start(c.slots_dst[:, :].rearrange("(p t) w -> p t w", p=P), back[:, :, :]
                         ).then_inc(emptied_table, 16)
            sp.wait_ge(filled, 48)
            sp.wait_ge(returned, 1)
            sp.dma_start(back[:, :, :], c.slots_dst[:, :].rearrange("(p t) w -> p t w", p=P)).then_inc(returned, 16)

        @block.gpsimd
        def _(pool):
            pool.memset(back[:, :, :], 0).then_inc(cleared, 1)
            pool.wait_ge(emptied_table, 16)
            pool.wait_ge(positioned, 3)

            def batch(i, s):
                pool.sem_inc(passed, 1)
                pool.tensor_copy(few[:, s, :, :].rearrange("p b w -> p w b"),
                                 trio[:, :, bass.ds((4 * i + s) * B, B)]).then_inc(copied, 1)
                pool.wait_ge(copied, 4 * i + s + 1)
                pool.sem_inc(passed, 1)
                for k in range(B):
                    pool.indirect_dma_start(out=c.slots_dst[:, :], in_=few[:, s, k, 1:3], in_offset=None,
                                            out_offset=bass.IndirectOffsetOnAxis(ap=few[:, s, k, 0:1], axis=0)
                                            ).then_inc(sent[s], 16)
            for s in range(4):
                batch(0, s)
            with pool.Fori(1, EC // (4 * B)) as i:
                for s in range(4):
                    pool.wait_ge(sent[s], i * (16 * B))
                    batch(i, s)
            for s in range(4):
                pool.wait_ge(sent[s], 16 * B * (EC // (4 * B)))
            pool.sem_inc(returned, 1)

        def dve_positions(dve, t, bucket_of):
            n = [0]

            def step(ins):
                ins.then_inc(split[t], 1)
                n[0] += 1
                dve.wait_ge(split[t], n[0])

            key, oth = keys[t], others[t]
            dve.wait_ge(loaded[t], 32)
            step(dve.tensor_scalar(tmp_i[:, :], key[:, :], 7, None, ALU.arith_shift_right))
            step(dve.tensor_copy(hi16[:, :], tmp_i[:, :]))
            if t == "dst":
                step(dve.tensor_copy(dst_hi[:, :], tmp_i[:, :]))
            step(dve.tensor_scalar(key[:, :], key[:, :], 127, None, ALU.bitwise_and))
            step(dve.tensor_scalar(oth[:, :], oth[:, :], -1.0, float(ZROW), ALU.mult, ALU.add))
            if t == "dst":
                step(dve.tensor_copy(dst_lo[:, :], key[:, :]))
                step(dve.tensor_copy(trio[:, 1, :], oth[:, :]))
                dve.tensor_scalar(trio[:, 2, :], key[:, :], 1.0, None, ALU.add).then_inc(positioned, 1)
            else:
                step(dve.tensor_copy(plo[:, :], key[:, :]))
                step(dve.tensor_scalar(tmp_i[:, :], oth[:, :], 7, None, ALU.bitwise_and))
                step(dve.tensor_scalar(oth[:, :], oth[:, :], 3, None, ALU.arith_shift_right))
                step(dve.tensor_copy(pay2[:, :], oth[:, :]))
                step(dve.tensor_scalar(cum[:, 0, :], plo[:, :], 8.0, 8.0, ALU.mult, ALU.add))
                step(dve.tensor_tensor(pay1[:, :], cum[:, 0, :], tmp_i[:, :], ALU.add))
            dve.sem_inc(counted[t], 2)

            def count(b, q):
                dve.wait_ge(counted[t], b + 1)
                dve.tensor_scalar(mask[:, q, :], hi16[:, :], c.iota[0:EP, bass.ds(b, 1)], 0.0, ALU.is_equal, ALU.add,
                                  accum_out=tot[:, bass.ds(b, 1)]).then_inc(counted[t], 1)
            with dve.Fori(0, TILES // 2) as i:
                count(2 * i, 0)
                count(2 * i + 1, 1)
            count(TILES - 1, 0)
            dve.wait_ge(counted[t], TILES + 2)
            dve.wait_ge(summed[t], 1)
            step(dve.tensor_scalar(small_i[:, 0, :], pss[:, 64:64 + TILES], float(PAIR - 1), None, ALU.add))
            step(dve.tensor_scalar(small_i[:, 1, :], small_i[:, 0, :], PAIR_BITS, None, ALU.arith_shift_right))
            step(dve.tensor_copy(nt[:, :], small_i[:, 1, :]))
            step(dve.tensor_tensor_scan(inc[:, :], nt[:, :], c.zeros[:, 0:TILES], 0.0, ALU.add, ALU.add))
            if t == "src":
                step(dve.tensor_scalar(off[:, :], inc[:, :], 2.0, -1.0, ALU.mult, ALU.add))
                step(dve.tensor_scalar(c.last_s[:, :], off[0:1, :], 0.0, None, ALU.max))
            step(dve.tensor_tensor(inc[:, :], inc[:, :], nt[:, :], ALU.subtract))
            step(dve.tensor_scalar(inc[:, :], inc[:, :], float(PAIR), -1.0, ALU.mult, ALU.add))
            step(dve.tensor_tensor(off[0:EP, :], inc[0:EP, :], pss[0:EP, 0:TILES], ALU.add))
            step(dve.tensor_scalar(col_i[:, 0:1], pss[0:TILES, 128:129], float(PAIR - 1), None, ALU.add))
            step(dve.tensor_scalar(col_i[:, 1:2], col_i[:, 0:1], PAIR_BITS, None, ALU.arith_shift_right))
            dve.tensor_copy(col_f[:, :], col_i[:, 1:2]).then_inc(based[t], 1)
            dve.wait_ge(ended[t], 1)
            step(dve.tensor_copy(endc[:, :], pss[0:TILES, 192:193]))
            dve.tensor_scalar(ge[:, :], c.iota[0:TILES, 0:PAIRS], endc[:, 0:1], None, ALU.is_ge).then_inc(based[t], 1)
            dve.wait_ge(table[t], 1)
            step(dve.tensor_copy(bucket_of[0:1, :], accs[0][0:1, 0, 0:PAIRS]))
            if t == "src":
                step(dve.tensor_copy(whose[:, :], accs[0][:, 0, 0:PAIRS]))
                step(dve.memset(c.reset_s[:, :, :], 0.0))
                step(dve.tensor_tensor(ends[:, 1:PAIRS], whose[:, 1:PAIRS], whose[:, 0:PAIRS - 1], ALU.not_equal))
                step(dve.tensor_scalar(c.reset_s[:, 1:PAIRS, 0], ends[:, 1:PAIRS], LOW, None, ALU.mult))

            def mark(b, q):
                dve.tensor_scalar(mask[:, q, :], hi16[:, :], c.iota[0:EP, bass.ds(b, 1)], None,
                                  ALU.is_equal).then_inc(masked[t], 1)

            def bucket(b, q):
                dve.wait_ge(masked[t], b + 1)
                dve.tensor_tensor_scan(cum[:, q, :], mask[:, q, :], c.zeros[0:EP, :], off[0:EP, bass.ds(b, 1)],
                                       ALU.add, ALU.add).then_inc(scanned[t], 1)
                dve.wait_ge(picked[t], b + 1)
                mark(b + 1, 1 - q)
                dve.wait_ge(scanned[t], b + 1)
                dve.wait_ge(usedhit[t], b + 1)
                dve.tensor_tensor(hit[:, q, :], mask[:, q, :], cum[:, q, :], ALU.mult).then_inc(picked[t], 1)
            dve.sem_inc(picked[t], 1)
            mark(0, 0)
            with dve.Fori(0, TILES // 2) as i:
                bucket(2 * i, 0)
                bucket(2 * i + 1, 1)
            bucket(TILES - 1, 0)
            dve.wait_ge(pos_whole[t], 1)
            step(dve.tensor_copy(halves(tmp_i[:, :]), ps_pos[0:EP, :, 0:HC]))
            step(dve.tensor_scalar(key[:, :], tmp_i[:, :], 127, None, ALU.bitwise_and))
            step(dve.tensor_copy(plo[:, :], key[:, :]))
            step(dve.tensor_scalar(key[:, :], tmp_i[:, :], 7, None, ALU.arith_shift_right))
            step(dve.tensor_copy(ptile[:, :], key[:, :]))
            if t == "dst":
                step(dve.tensor_scalar(cum[:, 0, :], plo[:, :], float(ET), None, ALU.mult))
                step(dve.tensor_tensor(trio[:, 0, :], cum[:, 0, :], ptile[:, :], ALU.add))
                dve.sem_inc(positioned, 2)

        @block.vector
        def _(dve):
            dve_positions(dve, "dst", c.buc_d)
            dve_positions(dve, "src", c.buc_s)

            def factors(t, k, turn):
                dve.wait_ge(spread, t + 1)
                dve.tensor_scalar(lo1[:, k, :], c.iota16[0:EP, 0:P], plo[:, bass.ds(t, 1)], None, ALU.is_equal
                                  ).then_inc(place_ready, 1)
                dve.tensor_scalar(hot[:, k, :], c.iota16[0:EP, :], ptile[:, bass.ds(t, 1)], None, ALU.is_equal)
                dve.tensor_scalar(dlo[:, k, :], c.iota16[0:EP, 0:P], dst_lo[:, bass.ds(t, 1)], None, ALU.is_equal)
                dve.tensor_scalar(dhi[:, k, :], c.iota16[0:EP, 0:TILES], dst_hi[:, bass.ds(t, 1)], None,
                                  ALU.is_equal).then_inc(onehot, 1)
            skewed(dve, [(0, factors)], EC, U)

            n = [0]

            def step(ins):
                ins.then_inc(unpacked, 1)
                n[0] += 1
                dve.wait_ge(unpacked, n[0])
            dve.wait_ge(placed, 1)
            step(dve.tensor_copy(halves(u1[:, :]), accs[0][:, :, 0:HALF]))
            step(dve.tensor_scalar(u2[:, :], u1[:, :], 3, None, ALU.arith_shift_right))
            step(dve.tensor_scalar(c.loc_s[:, :], u2[:, :], -1.0, None, ALU.add))
            step(dve.tensor_scalar(u2[:, :], u1[:, :], 7, None, ALU.bitwise_and))
            step(dve.tensor_scalar(halves(u3[:, :]), accs[1][:, :, 0:HALF], -8.0, float(ZROW), ALU.mult, ALU.add))
            step(dve.tensor_tensor(c.idx_s[:, 0:ET], u3[:, :], u2[:, :], ALU.subtract))
            step(dve.tensor_copy(c.deg[:, :], psd[:, 0:TILES]))
            dve.wait_ge(returned, 17)
            step(dve.tensor_scalar(c.idx_d[:, 0:ET], back[:, :, 0], -1.0, float(ZROW), ALU.mult, ALU.add))
            step(dve.tensor_scalar(c.loc_d[:, :], back[:, :, 1], -1.0, None, ALU.add))
            step(dve.tensor_scalar(c.idx_d[:, ET:ET + RING], u2[:, 0:RING], 0.0, None, ALU.mult))
            step(dve.tensor_scalar(c.idx_s[:, ET:ET + RING], u2[:, 0:RING], 0.0, None, ALU.mult))

        @block.scalar
        def _(act):
            def pay(t, k, turn):
                act.wait_ge(place_ready, t + 1)
                act.wait_ge(spread, t + 1)
                nc.scalar.activation(l12[:, k, 0, :], lo1[:, k, :], ACT.Copy, scale=pay1[:, bass.ds(t, 1)])
                nc.scalar.activation(l12[:, k, 1, :], lo1[:, k, :], ACT.Copy, scale=pay2[:, bass.ds(t, 1)]
                                     ).then_inc(paid, 1)
            skewed(act, [(0, pay)], EC, U)

        def pe_positions(pe, t):
            pe.sem_inc(usedhit[t], 2)
            pe.wait_ge(counted[t], TILES + 2)
            pe.matmul(pss[0:EP, 0:TILES], c.below[0:EP, 0:EP], tot[:, :], start=True, stop=True)
            pe.matmul(pss[:, 64:64 + TILES], c.ones[0:EP, :], tot[:, :], start=True, stop=True)
            pe.matmul(pss[0:TILES, 128:129], tot[:, :], c.ones[0:EP, 0:1], start=True, stop=True
                      ).then_inc(summed[t], 1)
            pe.wait_ge(based[t], 1)
            pe.matmul(pss[0:TILES, 192:193], c.upto[0:TILES, 0:TILES], col_f[:, :], start=True,
                      stop=True).then_inc(ended[t], 1)
            pe.wait_ge(based[t], 2)
            pe.matmul(accs[0][:, 0, 0:PAIRS], c.ones[0:TILES - 1, :], ge[0:TILES - 1, :], start=True, stop=True
                      ).then_inc(table[t], 1)
            for a in range(2):
                pe.matmul(ps_pos[0:EP, a, 0:HC], c.zeros[0:EP, 0:EP], c.zeros[0:EP, 0:HC], start=True, stop=False)

            def add(b, q):
                pe.wait_ge(picked[t], b + 2)
                for a in range(2):
                    last = pe.matmul(ps_pos[0:EP, a, 0:HC], c.ident[0:EP, 0:EP], hit[:, q, a * HC:(a + 1) * HC],
                                     start=False, stop=False)
                last.then_inc(usedhit[t], 1)
            with pe.Fori(0, TILES // 2) as i:
                add(2 * i, 0)
                add(2 * i + 1, 1)
            add(TILES - 1, 0)
            for a in range(2):
                last = pe.matmul(ps_pos[0:EP, a, 0:HC], c.zeros[0:EP, 0:EP], c.zeros[0:EP, 0:HC], start=False,
                                 stop=True)
            last.then_inc(pos_whole[t], 1)

        @block.tensor
        def _(pe):
            pe_positions(pe, "dst")
            pe_positions(pe, "src")
            pe.sem_inc(spread, U)
            pe.wait_ge(onehot, 1)
            for acc in accs:
                for a in range(2):
                    pe.matmul(acc[:, a, 0:HALF], c.zeros16[:, 0:P], c.zeros16[:, :], start=True, stop=False)
            pe.matmul(psd[:, 0:TILES], c.zeros16[:, 0:P], c.zeros16[:, 0:TILES], start=True, stop=False)

            def place(t, k, turn):
                pe.wait_ge(onehot, t + 1)
                pe.wait_ge(paid, t + 1)
                for m, acc in enumerate(accs):
                    for a in range(2):
                        pe.matmul(acc[:, a, 0:HALF], l12[:, k, m, :], hot[:, k, a * HALF:(a + 1) * HALF],
                                  start=False, stop=False)
                pe.matmul(psd[:, 0:TILES], dlo[:, k, :], dhi[:, k, :], start=False, stop=False
                          ).then_inc(spread, 1)
            skewed(pe, [(0, place)], EC, U)
            for acc in accs:
                for a in range(2):
                    pe.matmul(acc[:, a, 0:HALF], c.zeros16[:, 0:P], c.zeros16[:, :], start=False, stop=True)
            pe.matmul(psd[:, 0:TILES], c.zeros16[:, 0:P], c.zeros16[:, 0:TILES], start=False,
                      stop=True).then_inc(placed, 1)


def normalise(dve, sem, rooted, g, x, out, st, mean, rstd, var, done=0):
    tmp = var
    n = [0]

    def step(ins):
        ins.then_inc(sem, 1)
        n[0] += 1
        dve.wait_ge(sem, done + n[0])

    for k in range(UNROLL):
        last = dve.bn_stats(st[:, k, :], x[:, k, :])
    step(last)
    step(dve.tensor_tensor(mean[:, :], st[:, :, 1], st[:, :, 4], ALU.add))
    step(dve.tensor_tensor(tmp[:, :], st[:, :, 1], st[:, :, 4], ALU.subtract))
    step(dve.tensor_tensor(tmp[:, :], tmp[:, :], tmp[:, :], ALU.mult))
    step(dve.tensor_scalar(mean[:, :], mean[:, :], 0.5, None, ALU.mult))
    step(dve.tensor_scalar(tmp[:, :], tmp[:, :], D / 4.0, None, ALU.mult))
    step(dve.tensor_tensor(tmp[:, :], tmp[:, :], st[:, :, 2], ALU.add))
    step(dve.tensor_tensor(tmp[:, :], tmp[:, :], st[:, :, 5], ALU.add))
    step(dve.tensor_scalar(tmp[:, :], tmp[:, :], 1.0 / D, EPS, ALU.mult, ALU.add))
    dve.wait_ge(rooted, g + 1)
    for k in range(UNROLL):
        last = dve.tensor_scalar(out[:, k, :], x[:, k, :], mean[:, k:k + 1], rstd[:, k:k + 1], ALU.subtract,
                                 ALU.mult)
    step(last)
    assert n[0] == LN_STEPS


LN_STEPS = 10


def root(pool, c, sem, rooted, passed, g, rstd, var, done=0):
    pool.wait_ge(sem, done + g * LN_STEPS + LN_STEPS - 1)
    pool.sem_inc(passed, 1)
    pool.tensor_tensor(rstd[:, :], var[:, :], c.neghalf[:, :], ALU.pow).then_inc(rooted, 1)


def ln_buffers(sb):
    return (sb("st", [P, UNROLL, 6], F32), sb("mean", [P, UNROLL], F32), sb("rstd", [P, UNROLL], F32),
            sb("tmp", [P, UNROLL], F32))


def project_heads(nc, c, W, a_l, a_r):
    c.phase = "heads"
    sem = lambda name: nc_sem(nc, c, name)
    wloaded, rooted, lnstep, normed, turned, xt_made, projected, evac, passed = (
        sem(s) for s in "wloaded rooted lnstep normed turned xt_made projected evac passed".split())
    xin, stored = [sem("xin0"), sem("xin1")], [sem("stored0"), sem("stored1")]
    with ExitStack() as ctx:
        sb = lambda name, shape, dt: ctx.enter_context(nc.sbuf_tensor(f"heads_{name}", shape, dt))
        ps = lambda name, shape: ctx.enter_context(nc.psum_tensor(f"heads_ps_{name}", shape, F32))
        w = sb("w", [P, 2, D + 8], F32)
        al = sb("al", [P, 2, D], F32)
        prod = sb("prod", [P, D], F32)
        x, xn = sb("x", [P, 2, UNROLL, D], F32), sb("xn", [P, 2, UNROLL, D], F32)
        ln = ln_buffers(sb)
        xt = sb("xt", [P, 2, 2, P], F32)
        ht = sb("ht", [P, 2, UNROLL, D + 4], F32)
        pst, psh = ps("pst", [P, 2, 512]), ps("psh", [P, 2, 512])
        block = ctx.enter_context(nc.Block())

        @block.sync
        def _(sp):
            sp.dma_start(w[:, :, 0:D], W.rearrange("(k p) d -> p k d", p=P)).then_inc(wloaded, 16)
            for j, a in enumerate((a_l, a_r)):
                sp.dma_start(al[:, j, :], a.rearrange("a h d -> a (h d)").broadcast_to([P, D])).then_inc(wloaded, 16)

            def load(g, s, j):
                sp.wait_ge(normed, g + 1)
                sp.dma_start(x[:, s, :, :], rows(c.x0, g, D)).then_inc(xin[s], 16)
            groups(sp, load)

        @block.gpsimd
        def _(pool):
            groups(pool, lambda g, s, j: root(pool, c, lnstep, rooted, passed, g, ln[2], ln[3], done=8))

        @block.vector
        def _(dve):
            n = [0]

            def step(ins):
                ins.then_inc(lnstep, 1)
                n[0] += 1
                dve.wait_ge(lnstep, n[0])
            dve.sem_inc(normed, 2)
            dve.wait_ge(wloaded, 48)
            for k in range(2):
                for j in range(2):
                    step(dve.tensor_tensor(prod[:, :], w[:, k, 0:D], al[:, j, :], ALU.mult))
                    at = D + 4 * (1 - j)
                    step(dve.tensor_reduce(w[:, k, at:at + 4], prod[:, :].rearrange("p (h d) -> p h d", h=HEADS),
                                           AX.X, ALU.add))
            base = n[0]

            def body(g, s, j):
                dve.wait_ge(xin[s], 16 * j + 16)
                dve.wait_ge(turned, g * UNROLL + UNROLL)
                normalise(dve, lnstep, rooted, g, x[:, s], xn[:, s], *ln, done=base + g * LN_STEPS)
                dve.sem_inc(normed, 1)
            groups(dve, body)

        @block.scalar
        def _(act):
            act.sem_inc(xt_made, 2)
            act.sem_inc(evac, 2)
            act.sem_inc(stored[0], 32)
            act.sem_inc(stored[1], 32)

            def body(g, s, j):
                act.wait_ge(stored[s], 32 * j + 32)
                for k in range(UNROLL + 1):
                    if k < UNROLL:
                        t, q = g * UNROLL + k, (s + k) % 2
                        act.wait_ge(turned, t + 15)
                        act.wait_ge(projected, t + 1)
                        nc.scalar.copy(xt[:, q, :, :], pst[:, q, 0:2 * P]).then_inc(xt_made, 1)
                    if k > 0:
                        t, q = g * UNROLL + k - 1, (s + k - 1) % 2
                        act.wait_ge(projected, t + 3)
                        nc.scalar.copy(ht[:, s, k - 1, :], psh[:, q, 0:D + 4])
                        nc.scalar.copy(c.hlm[:, bass.ds(t * 8, 4)], psh[:, q, D + 4:D + 8]).then_inc(evac, 1)
                act.wait_ge(evac, g * UNROLL + UNROLL + 2)
                act.dma_start(rows(c.t_h, g, D + 4), ht[:, s, :, :]).then_inc(stored[s], 16)
                act.dma_start(rows(c.t_hr, g, 4), ht[:, s, :, D:D + 4]).then_inc(stored[s], 16)
            groups(act, body)
            act.wait_ge(stored[0], 32 * 5)
            act.wait_ge(stored[1], 32 * 4)

        @block.tensor
        def _(pe):
            pe.sem_inc(turned, 14)
            pe.sem_inc(projected, 2)
            pe.wait_ge(lnstep, 8)

            def body(g, s, j):
                pe.wait_ge(normed, g + 3)
                for k in range(UNROLL + 1):
                    if k < UNROLL:
                        t, q = g * UNROLL + k, (s + k) % 2
                        pe.wait_ge(xt_made, t + 1)
                        for b in range(2):
                            last = pe.transpose(pst[:, q, b * P:(b + 1) * P], xn[:, s, k, b * P:(b + 1) * P],
                                                c.ident[:, :])
                        last.then_inc(turned, 1)
                    if k > 0:
                        t, q = g * UNROLL + k - 1, (s + k - 1) % 2
                        pe.wait_ge(xt_made, t + 3)
                        pe.wait_ge(evac, t + 1)
                        for b in range(2):
                            last = pe.matmul(psh[:, q, 0:D + 8], xt[:, q, b, :], w[:, b, :], start=(b == 0),
                                             stop=(b == 1))
                        last.then_inc(projected, 1)
            groups(pe, body)


def gather_rows(pool, few, table, ring, gathered, freed, copied, passed):
    with pool.Fori(0, ET // RING) as i:
        for h in range(QUADS):
            pool.wait_ge(copied, QUADS * i + h + 1)
            pool.wait_ge(freed, (QUADS * i + h) * QUAD + QUAD)
            pool.sem_inc(passed, 1)
            for k in range(QUAD):
                pool.indirect_dma_start(out=ring[:, QUAD * h + k, :], out_offset=None, in_=table[:, :],
                                        in_offset=bass.IndirectOffsetOnAxis(ap=few[:, h, k:k + 1], axis=0)
                                        ).then_inc(gathered[h], 16)


def first_indices(nc, idx, few, copied):
    for k in range(QUADS):
        nc.scalar.copy(few[:, k, :], idx[:, QUAD * k:QUAD * k + QUAD]).then_inc(copied, 1)


def next_indices(nc, act, idx, few, gathered, copied, q, k, turn_):
    act.wait_ge(gathered[k], DONE * turn_ + DONE)
    nc.scalar.copy(few[:, k, :], idx[:, bass.ds(q * QUAD + RING, QUAD)]).then_inc(copied, 1)


def one_hots(dve, c, local, oh, q, k, compare):
    return dve.tensor_tensor(oh[:, QUAD * k:QUAD * k + QUAD, :], c.iota[:, 0:P].unsqueeze(1).broadcast_to([P, QUAD, P]),
                             local[:, bass.ds(q * QUAD, QUAD)].unsqueeze(2).broadcast_to([P, QUAD, P]), compare)


def neighbour_max(nc, c):
    c.phase = "nmax"
    sem = lambda name: nc_sem(nc, c, name)
    copied, passed, no_made, diag_act, diag_dve, summed, reduced, cleared, scanned, picked = (
        sem(s) for s in "copied passed no_made diag_act diag_dve summed reduced cleared scanned picked".split())
    gathered = [sem(f"gathered{k}") for k in range(QUADS)]
    with ExitStack() as ctx:
        sb = lambda name, shape, dt: ctx.enter_context(nc.sbuf_tensor(f"nmax_{name}", shape, dt))
        few = sb("few", [P, QUADS, QUAD], I32)
        hr = sb("hr", [P, RING, HEADS], F32)
        no = sb("no", [P, RING, P], BF16)
        diag = sb("diag", [P, 2, QUAD, HEADS, P], F32)
        far = sb("far", [P, HEADS, P], BF16)
        tmax = sb("tmax", [P, ET, HEADS], F32)
        runmax = sb("runmax", [P, HEADS, ET], F32)
        best = sb("best", [P, TILES, HEADS], F32)
        tmp = sb("tmp", [P, TILES, HEADS], F32)
        ps_all = ctx.enter_context(nc.psum_tensor("nmax_ps_all", [P, 2 * QUAD, 512], F32))
        block = ctx.enter_context(nc.Block())

        @block.gpsimd
        def _(pool):
            gather_rows(pool, few, c.t_hr, hr, gathered, summed, copied, passed)

        @block.tensor
        def _(pe):
            pe.sem_inc(summed, RING)
            pe.wait_ge(cleared, 1)

            def every_node(q, k, turn_):
                pe.wait_ge(no_made, q + 1)
                pe.wait_ge(diag_dve, q + 1)
                pe.wait_ge(diag_act, q + 1)
                for m in range(QUAD):
                    bank = QUAD * (k % 2) + m
                    pe.wait_ge(reduced, q * QUAD + m + 1)
                    pe.matmul(ps_all[:, bank, :], c.ones[:, :], diag[:, k % 2, m].rearrange("p h e -> p (h e)"),
                              start=True, stop=False)
                    pe.matmul(ps_all[:, bank, :], no[:, QUAD * k + m, :], far[:, :, :].rearrange("p h e -> p (h e)"),
                              start=False, stop=True).then_inc(summed, 1)
            skewed(pe, [(0, every_node)], ET // QUAD, QUADS)

        @block.scalar
        def _(act):
            first_indices(nc, c.idx_s, few, copied)

            def diagonal(q, k, turn_):
                next_indices(nc, act, c.idx_s, few, gathered, copied, q, k, turn_)
                act.wait_ge(summed, q * QUAD + RING - QUAD)
                for m in range(QUAD):
                    for h in range(3):
                        last = nc.scalar.activation(diag[:, k % 2, m, h, :], c.ident[:, :], ACT.Copy,
                                                    scale=hr[:, QUAD * k + m, h:h + 1])
                last.then_inc(diag_act, 1)
            skewed(act, [(0, diagonal)], ET // QUAD, QUADS)

        @block.vector
        def _(dve):
            dve.tensor_scalar(far[:, :, :], c.ident[:, :].unsqueeze(1).broadcast_to([P, HEADS, P]), FAR, None, ALU.mult
                              ).then_inc(cleared, 1)
            dve.sem_inc(reduced, 2 * QUAD)

            def hots(q, k, turn_):
                dve.wait_ge(summed, q * QUAD + QUAD)
                one_hots(dve, c, c.loc_s, no, q, k, ALU.not_equal).then_inc(no_made, 1)

            def diagonal(q, k, turn_):
                dve.wait_ge(gathered[k], DONE * turn_ + DONE)
                dve.wait_ge(summed, q * QUAD + RING - QUAD)
                dve.tensor_tensor(diag[:, k % 2, :, 3, :], c.ident[:, :].unsqueeze(1).broadcast_to([P, QUAD, P]),
                                  hr[:, QUAD * k:QUAD * k + QUAD, 3:4].broadcast_to([P, QUAD, P]), ALU.mult
                                  ).then_inc(diag_dve, 1)

            def reduce(q, k, turn_):
                for m in range(QUAD):
                    dve.wait_ge(summed, q * QUAD + m + RING + 1)
                    dve.tensor_reduce(tmax[:, bass.ds(q * QUAD + m, 1), :],
                                      ps_all[:, QUAD * (k % 2) + m, :].rearrange("p (a h e) -> p a h e", a=1, h=HEADS),
                                      AX.X, ALU.max).then_inc(reduced, 1)
            skewed(dve, [(0, hots), (0, diagonal), (1, reduce)], ET // QUAD, QUADS)
            dve.wait_ge(reduced, ET + 2 * QUAD)
            for h in range(HEADS):
                dve.tensor_tensor_scan(runmax[:, h, :], c.reset_s[:, :, :].rearrange("p j m -> p (j m)"), tmax[:, :, h], LOW, ALU.add, ALU.max
                                       ).then_inc(scanned, 1)
            dve.wait_ge(scanned, HEADS)
            with dve.Fori(0, TILES) as b:
                t = dve.value_load(c.last_s[0:1, bass.ds(b, 1)], min_val=0, max_val=ET - 1)
                dve.tensor_scalar(best[:, bass.ds(b, 1), :], runmax[:, :, bass.ds(t, 1)].rearrange("p h a -> p a h"),
                                  0.0, None, ALU.add).then_inc(picked, 1)
            dve.wait_ge(picked, TILES)
            hl = c.hlm[:, :].rearrange("p (i e) -> p i e", e=8)
            dve.tensor_tensor(tmp[:, :, :], hl[:, :, 0:4], best[:, :, :], ALU.add).then_inc(cleared, 1)
            dve.wait_ge(cleared, 2)
            dve.scalar_tensor_tensor(out=hl[:, :, 4:8], in0=tmp[:, :, :], scalar=0.2, in1=tmp[:, :, :], op0=ALU.mult,
                                     op1=ALU.max).then_inc(cleared, 1)
            dve.wait_ge(cleared, 3)


def attend(nc, c):
    c.phase = "attend"
    W = D + 4
    sem = lambda name: nc_sem(nc, c, name)
    (copied, passed, oh_made, oh_turned, oht_made, looked, scored, exped, weighed_act, weighed_dve, scattered, added,
     step, cleared) = (sem(s) for s in ("copied passed oh_made oh_turned oht_made looked scored exped weighed_act "
                                        "weighed_dve scattered added step cleared").split())
    gathered = [sem(f"gathered{k}") for k in range(QUADS)]
    with ExitStack() as ctx:
        sb = lambda name, shape, dt: ctx.enter_context(nc.sbuf_tensor(f"attend_{name}", shape, dt))
        ps = lambda name, shape: ctx.enter_context(nc.psum_tensor(f"attend_ps_{name}", shape, F32))
        few = sb("few", [P, QUADS, QUAD], I32)
        rows_h = sb("rows", [P, RING, W], F32)
        oh = sb("oh", [P, RING, P], F32)
        oht = sb("oht", [P, 2, QUAD * P], F32)
        sc = sb("sc", [P, 2, 3, QUAD, HEADS], F32)
        wr = sb("wr", [P, 2, QUAD, W], F32)
        ps_oh, ps_look, ps_sum = ps("oh", [P, 2, 512]), ps("look", [P, 2, 512]), ps("sum", [P, QUAD, 512])
        block = ctx.enter_context(nc.Block())
        seen = lambda k: ps_look[:, k % 2, 0:QUAD * 8].rearrange("p (m e) -> p m e", e=8)

        @block.gpsimd
        def _(pool):
            gather_rows(pool, few, c.t_h, rows_h, gathered, scattered, copied, passed)

        @block.tensor
        def _(pe):
            pe.sem_inc(looked, 2 * QUAD)
            pe.sem_inc(scattered, RING)

            def turn(q, k, turn_):
                pe.wait_ge(oh_made, q + 1)
                pe.wait_ge(oht_made, q + 1)
                for m in range(QUAD):
                    last = pe.transpose(ps_oh[:, k % 2, m * P:(m + 1) * P], oh[:, QUAD * k + m, :], c.ident[:, :])
                last.then_inc(oh_turned, 1)

            def look(q, k, turn_):
                pe.wait_ge(oht_made, q + 3)
                pe.wait_ge(scored, q + 1)
                look_pair(q, k, 0)

            def look_pair(q, k, j):
                b = pe.value_load(c.buc_s[0:1, bass.ds(q * 2 + j, 1)], min_val=0, max_val=TILES - 1)
                for m in (2 * j, 2 * j + 1):
                    pe.matmul(ps_look[:, k % 2, m * 8:m * 8 + 8], oht[:, k % 2, m * P:(m + 1) * P],
                              c.hlm[:, bass.ds(b * 8, 8)], start=True, stop=True).then_inc(looked, 1)

            def scatter(q, k, turn_):
                pe.wait_ge(weighed_act, q + 1)
                pe.wait_ge(weighed_dve, q + 1)
                scatter_pair(q, k, 0)

            def scatter_pair(q, k, j):
                pe.wait_ge(added, q * 2 + j + 1)
                for m in (2 * j, 2 * j + 1):
                    pe.matmul(ps_sum[:, 2 * (k % 2) + j, 0:W], oh[:, QUAD * k + m, :], wr[:, k % 2, m, :],
                              start=(m % 2 == 0), stop=(m % 2 == 1)).then_inc(scattered, 1)
            look_rest = lambda q, k, turn_: look_pair(q, k, 1)
            scatter_rest = lambda q, k, turn_: scatter_pair(q, k, 1)
            skewed(pe, [(3, scatter), (1, look), (3, scatter_rest), (1, look_rest), (0, turn)], ET // QUAD, QUADS)

        @block.scalar
        def _(act):
            act.sem_inc(oht_made, 2)
            act.sem_inc(exped, 2)
            first_indices(nc, c.idx_s, few, copied)
            indices = lambda q, k, turn_: next_indices(nc, act, c.idx_s, few, gathered, copied, q, k, turn_)

            def turned(q, k, turn_):
                act.wait_ge(oh_turned, q + 1)
                act.wait_ge(looked, q * QUAD + QUAD)
                nc.scalar.copy(oht[:, k % 2, :], ps_oh[:, k % 2, :]).then_inc(oht_made, 1)

            def exponentials(q, k, turn_):
                act.wait_ge(scored, q + 3)
                act.wait_ge(scattered, q * QUAD + RING - QUAD)
                nc.scalar.activation(wr[:, k % 2, :, D:W], sc[:, k % 2, 2, :, :], ACT.Exp).then_inc(exped, 1)

            def weigh(q, k, turn_):
                act.wait_ge(exped, q + 3)
                for m in range(QUAD):
                    for h in range(2):
                        last = nc.scalar.activation(wr[:, k % 2, m, h * HD:(h + 1) * HD],
                                                    rows_h[:, QUAD * k + m, h * HD:(h + 1) * HD], ACT.Copy,
                                                    scale=wr[:, k % 2, m, D + h:D + h + 1])
                last.then_inc(weighed_act, 1)
            skewed(act, [(2, exponentials), (2, weigh), (0, turned), (1, indices)], ET // QUAD, QUADS)

        @block.vector
        def _(dve):
            dve.memset(c.acc[:, 0:TILES * W], 0.0).then_inc(cleared, 1)
            dve.sem_inc(scored, 2)
            dve.sem_inc(added, 4)
            dve.wait_ge(cleared, 1)

            def hots(q, k, turn_):
                dve.wait_ge(scattered, q * QUAD + QUAD)
                one_hots(dve, c, c.loc_s, oh, q, k, ALU.is_equal).then_inc(oh_made, 1)

            def score(q, k, turn_):
                dve.wait_ge(looked, q * QUAD + 3 * QUAD)
                dve.wait_ge(gathered[k], DONE * turn_ + DONE)
                dve.wait_ge(exped, q + 1)
                dve.tensor_tensor(sc[:, k % 2, 0, :, :], seen(k)[:, :, 0:4], rows_h[:, QUAD * k:QUAD * k + QUAD, D:W],
                                  ALU.add).then_inc(step, 1)

            def leaky(q, k, turn_):
                dve.wait_ge(step, 2 * q + 1)
                dve.scalar_tensor_tensor(out=sc[:, k % 2, 1, :, :], in0=sc[:, k % 2, 0, :, :], scalar=0.2,
                                         in1=sc[:, k % 2, 0, :, :], op0=ALU.mult, op1=ALU.max).then_inc(step, 1)

            def stabilise(q, k, turn_):
                dve.wait_ge(step, 2 * q + 2)
                dve.tensor_tensor(sc[:, k % 2, 2, :, :], sc[:, k % 2, 1, :, :], seen(k)[:, :, 4:8], ALU.subtract
                                  ).then_inc(scored, 1)

            def weigh(q, k, turn_):
                dve.wait_ge(exped, q + 3)
                for h in range(2, HEADS):
                    last = dve.tensor_tensor(wr[:, k % 2, :, h * HD:(h + 1) * HD],
                                             rows_h[:, QUAD * k:QUAD * k + QUAD, h * HD:(h + 1) * HD],
                                             wr[:, k % 2, :, D + h:D + h + 1].broadcast_to([P, QUAD, HD]), ALU.mult)
                last.then_inc(weighed_dve, 1)

            def add(q, k, turn_):
                for j in range(2):
                    pair = q * 2 + j
                    b = dve.value_load(c.buc_s[0:1, bass.ds(pair, 1)], min_val=0, max_val=TILES - 1)
                    dve.wait_ge(scattered, pair * 2 + RING + 2)
                    dve.wait_ge(added, pair + 4)
                    here = c.acc[:, bass.ds(b * W, W)]
                    dve.tensor_tensor(here, here, ps_sum[:, 2 * (k % 2) + j, 0:W], ALU.add).then_inc(added, 1)
            skewed(dve, [(0, hots), (2, weigh), (3, add), (1, score), (1, leaky), (1, stabilise)], ET // QUAD, QUADS)
            dve.wait_ge(added, PAIRS + 4)


def close_attention(nc, c):
    c.phase = "close"
    W = D + 4
    sem = lambda name: nc_sem(nc, c, name)
    rooted, lnstep, summed, normed, used, passed, counted, allsummed = (
        sem(s) for s in "rooted lnstep summed normed used passed counted allsummed".split())
    xin, stored = [sem("xin0"), sem("xin1")], [sem("stored0"), sem("stored1")]
    with ExitStack() as ctx:
        sb = lambda name, shape, dt: ctx.enter_context(nc.sbuf_tensor(f"close_{name}", shape, dt))
        x, x1, xn = (sb(n, [P, 2, UNROLL, D], F32) for n in ("x", "x1", "xn"))
        den = sb("den", [P, UNROLL, HEADS], F32)
        ln = ln_buffers(sb)
        pcol = ctx.enter_context(nc.psum_tensor("close_pcol", [P, 2, 512], F32))
        block = ctx.enter_context(nc.Block())

        @block.sync
        def _(sp):
            def load(g, s, j):
                sp.wait_ge(summed, g + 1)
                sp.dma_start(x[:, s, :, :], rows(c.x0, g, D)).then_inc(xin[s], 16)
            groups(sp, load)

        @block.gpsimd
        def _(pool):
            groups(pool, lambda g, s, j: root(pool, c, lnstep, rooted, passed, g, ln[2], ln[3]))

        @block.vector
        def _(dve):
            dve.sem_inc(summed, 2)

            def body(g, s, j):
                acc = c.acc[:, bass.ds(g * (UNROLL * W), UNROLL * W)].rearrange("p (k w) -> p k w", w=W)
                att = acc[:, :, 0:D].rearrange("p k (h d) -> p k h d", h=HEADS)
                dve.tensor_scalar(den[:, :, :], acc[:, :, D:W], 1e-30, None, ALU.max).then_inc(counted, 1)
                dve.wait_ge(counted, 3 * g + 1)
                dve.reciprocal(den[:, :, :], den[:, :, :]).then_inc(counted, 1)
                dve.wait_ge(counted, 3 * g + 2)
                dve.tensor_tensor(att, att, den[:, :, :].unsqueeze(3).broadcast_to([P, UNROLL, HEADS, HD]), ALU.mult
                                  ).then_inc(counted, 1)
                dve.wait_ge(xin[s], 16 * j + 16)
                dve.wait_ge(stored[s], 32 * j + 32)
                dve.wait_ge(counted, 3 * g + 3)
                dve.tensor_tensor(x1[:, s], acc[:, :, 0:D], x[:, s], ALU.add).then_inc(summed, 1)
                dve.wait_ge(summed, g + 3)
                dve.wait_ge(used, g + 1)
                normalise(dve, lnstep, rooted, g, x1[:, s], xn[:, s], *ln, done=g * LN_STEPS)
                dve.sem_inc(normed, 1)
            groups(dve, body)
            dve.wait_ge(allsummed, 1)
            dve.tensor_copy(c.colsum[:, :], pcol[:, :, 0]).then_inc(counted, 1)
            dve.wait_ge(counted, 3 * GROUPS + 1)

        @block.scalar
        def _(act):
            act.sem_inc(stored[0], 32)
            act.sem_inc(stored[1], 32)

            def store(g, s, j):
                act.wait_ge(normed, g + 1)
                act.dma_start(rows(c.x1, g, D), x1[:, s]).then_inc(stored[s], 16)
                act.dma_start(rows(c.xn1, g, D), xn[:, s]).then_inc(stored[s], 16)
            groups(act, store)
            act.wait_ge(stored[0], 32 * 5)
            act.wait_ge(stored[1], 32 * 4)

        @block.tensor
        def _(pe):
            pe.sem_inc(used, 2)
            for b in range(2):
                pe.matmul(pcol[:, b, 0:1], c.zeros[:, 0:P], c.ones[:, 0:1], start=True, stop=False)

            def body(g, s, j):
                pe.wait_ge(normed, g + 1)
                for k in range(UNROLL):
                    for b in range(2):
                        last = pe.matmul(pcol[:, b, 0:1], xn[:, s, k, b * P:(b + 1) * P], c.ones[:, 0:1],
                                         start=False, stop=False)
                last.then_inc(used, 1)
            groups(pe, body)
            for b in range(2):
                last = pe.matmul(pcol[:, b, 0:1], c.zeros[:, 0:P], c.ones[:, 0:1], start=False, stop=True)
            last.then_inc(allsummed, 1)


def choose_experts(nc, c, Wr, br):
    c.phase = "choose"
    sem = lambda name: nc_sem(nc, c, name)
    loaded, step, given, expd = (sem(s) for s in "loaded step given expd".split())
    with ExitStack() as ctx:
        sb = lambda name, shape, dt: ctx.enter_context(nc.sbuf_tensor(f"choose_{name}", shape, dt))
        wr, brow = sb("wr", [P, 2, X0], F32), sb("brow", [P, X0], F32)
        mean = sb("mean", [P, 2, P], F32)
        v, e, w, eq, cand = (sb(n, [P, X0], F32) for n in ("v", "e", "w", "eq", "cand"))
        one, two = sb("one", [P, 8], F32), sb("two", [P, 8], F32)
        plog = ctx.enter_context(nc.psum_tensor("choose_plog", [P, 512], F32))
        block = ctx.enter_context(nc.Block())

        @block.sync
        def _(sp):
            sp.dma_start(wr[:, :, :], Wr.rearrange("(k p) e -> p k e", p=P)).then_inc(loaded, 16)
            sp.dma_start(brow[:, :], br.rearrange("(a e) -> a e", a=1).broadcast_to([P, X0])).then_inc(loaded, 16)

        @block.tensor
        def _(pe):
            pe.wait_ge(loaded, 32)
            pe.wait_ge(step, 2)
            for b in range(2):
                last = pe.matmul(plog[:, 0:X0], mean[:, b, :], wr[:, b, :], start=(b == 0), stop=(b == 1))
            last.then_inc(given, 1)

        @block.scalar
        def _(act):
            act.wait_ge(expd, 1)
            nc.scalar.activation(e[:, :], v[:, :], ACT.Exp).then_inc(given, 1)
            act.wait_ge(expd, 2)
            nc.scalar.activation(e[:, :], v[:, :], ACT.Exp).then_inc(given, 1)
            act.wait_ge(expd, 3)
            nc.scalar.activation(two[:, 2:3], two[:, 0:1], ACT.Exp).then_inc(given, 1)

        @block.vector
        def _(dve):
            n = [0]

            def do(ins):
                ins.then_inc(step, 1)
                n[0] += 1
                dve.wait_ge(step, n[0])

            def softmax(nth):
                do(dve.tensor_reduce(one[:, 0:1], v[:, :], AX.X, ALU.max))
                do(dve.tensor_scalar(v[:, :], v[:, :], one[:, 0:1], None, ALU.subtract))
                dve.sem_inc(expd, 1)
                dve.wait_ge(given, nth + 1)
                do(dve.tensor_reduce(one[:, 1:2], e[:, :], AX.X, ALU.add))
                do(dve.reciprocal(one[:, 1:2], one[:, 1:2]))
                do(dve.tensor_scalar(w[:, :], e[:, :], one[:, 1:2], None, ALU.mult))

            for b in range(2):
                do(dve.tensor_scalar(mean[:, b, :], c.ones[:, :], c.colsum[:, b:b + 1], 1.0 / N, ALU.mult, ALU.mult))
            dve.wait_ge(given, 1)
            do(dve.tensor_tensor(v[:, :], plog[:, 0:X0], brow[:, :], ALU.add))
            softmax(1)
            do(dve.tensor_scalar(v[:, :], w[:, :], float(N), CAP0, ALU.mult, ALU.max))
            do(dve.reciprocal(v[:, :], v[:, :]))
            do(dve.tensor_scalar(v[:, :], v[:, :], CAP0, None, ALU.mult))
            do(dve.tensor_tensor(v[:, :], v[:, :], w[:, :], ALU.mult))
            softmax(2)
            for m in range(2):
                do(dve.tensor_reduce(one[:, 2 + m:3 + m], w[:, :], AX.X, ALU.max))
                do(dve.tensor_scalar(eq[:, :], w[:, :], one[:, 2 + m:3 + m], 100.0, ALU.not_equal, ALU.mult))
                do(dve.tensor_tensor(cand[:, :], eq[:, :], c.iota[:, 0:X0], ALU.add))
                do(dve.tensor_reduce(one[:, 4 + m:5 + m], cand[:, :], AX.X, ALU.min))
                do(dve.tensor_scalar(eq[:, :], c.iota[:, 0:X0], one[:, 4 + m:5 + m], 4.0, ALU.is_equal, ALU.mult))
                do(dve.tensor_tensor(w[:, :], w[:, :], eq[:, :], ALU.subtract))
            do(dve.tensor_copy(c.chosen[0:1, :], one[0:1, 4:6]))
            do(dve.tensor_tensor(two[:, 0:1], one[:, 3:4], one[:, 2:3], ALU.subtract))
            dve.sem_inc(expd, 1)
            dve.wait_ge(given, 4)
            do(dve.tensor_scalar(two[:, 3:4], two[:, 2:3], 1.0, None, ALU.add))
            do(dve.reciprocal(c.share[:, 0:1], two[:, 3:4]))
            do(dve.tensor_tensor(c.share[:, 1:2], c.share[:, 0:1], two[:, 2:3], ALU.mult))


def experts0(nc, c, W1, b1, W2, b2, gamma, beta):
    c.phase = "experts0"
    FC = F0 // P
    NH = UNROLL * P // 2
    sem = lambda name: nc_sem(nc, c, name)
    (wloaded, wready, rooted, lnstep, turned, xt_made, hidden, gelued, mixed, emptied, passed, step, out) = (
        sem(s) for s in ("wloaded wready rooted lnstep turned xt_made hidden gelued mixed emptied passed step "
                         "out").split())
    xin, stored = [sem("xin0"), sem("xin1")], [sem("stored0"), sem("stored1")]
    with ExitStack() as ctx:
        sb = lambda name, shape, dt: ctx.enter_context(nc.sbuf_tensor(f"experts0_{name}", shape, dt))
        ps = lambda name, shape: ctx.enter_context(nc.psum_tensor(f"experts0_ps_{name}", shape, F32))
        w1 = sb("w1", [P, 2, 2, F0], F32)
        w2 = sb("w2", [P, 2, FC, D], F32)
        b1s = sb("b1", [P, 2, FC], F32)
        b2s = sb("b2", [P, 2, D], F32)
        gam, bet = sb("gam", [P, D], F32), sb("bet", [P, D], F32)
        xn, xr = sb("xn", [P, 2, UNROLL, D], F32), sb("xr", [P, 2, UNROLL, D], F32)
        xt = sb("xt", [P, 2, UNROLL * P], F32)
        hid = sb("hid", [P, 2 * FC, UNROLL * P], F32)
        y = sb("y", [P, UNROLL, D], F32)
        yo = sb("yo", [P, 2, UNROLL, D], F32)
        ln = ln_buffers(sb)
        pst, psh, psy = ps("t", [P, 2, 512]), ps("h", [P, 2, 512]), ps("y", [P, 2, 512])
        block = ctx.enter_context(nc.Block())

        @block.sync
        def _(sp):
            for m in range(2):
                e = sp.value_load(c.chosen[0:1, m:m + 1], min_val=0, max_val=X0 - 1)
                sp.dma_start(w1[:, m], W1[bass.ds(e, 1)].rearrange("a (k p) f -> p (a k) f", p=P)).then_inc(wloaded, 16)
                sp.dma_start(w2[:, m], W2[bass.ds(e, 1)].rearrange("a (k p) f -> p (a k) f", p=P)).then_inc(wloaded, 16)
                with nc.allow_non_contiguous_dma("a bias, one element to a partition"):
                    sp.dma_start(b1s[:, m, :], b1[bass.ds(e, 1)].rearrange("a (k p) -> p (a k)", p=P)
                                 ).then_inc(wloaded, 16)
                sp.dma_start(b2s[:, m, :], b2[bass.ds(e, 1)].broadcast_to([P, D])).then_inc(wloaded, 16)
            for t, d in ((gam, gamma), (bet, beta)):
                sp.dma_start(t[:, :], d.rearrange("(a e) -> a e", a=1).broadcast_to([P, D])).then_inc(wloaded, 16)

            def load(g, s):
                sp.dma_start(xn[:, s], rows(c.xn1, g, D)).then_inc(xin[s], 16)
                sp.dma_start(xr[:, s], rows(c.x1, g, D)).then_inc(xin[s], 16)

            def store(g, s):
                sp.wait_ge(out, g + 1)
                sp.dma_start(rows(c.x2, g, D), yo[:, s]).then_inc(stored[s], 16)
            load(0, 0)
            load(1, 1)
            sp.sem_inc(stored[0], 16)
            sp.sem_inc(stored[1], 16)
            with sp.Fori(0, (GROUPS - 3) // 2) as i:
                for s in range(2):
                    store(2 * i + s, s)
                    load(2 * i + s + 2, s)
            store(GROUPS - 3, 0)
            load(GROUPS - 1, 0)
            store(GROUPS - 2, 1)
            store(GROUPS - 1, 0)
            sp.wait_ge(stored[0], 16 * 5)
            sp.wait_ge(stored[1], 16 * 4)

        @block.gpsimd
        def _(pool):
            groups(pool, lambda g, s, j: root(pool, c, lnstep, rooted, passed, g, ln[2], ln[3]))

        @block.tensor
        def _(pe):
            pe.sem_inc(hidden, 2)
            pe.wait_ge(wready, 1)

            def body(g, s, j):
                pe.wait_ge(xin[s], 32 * j + 32)
                for k in range(UNROLL):
                    q = (s + k) % 2
                    pe.wait_ge(xt_made, g * UNROLL + k + 1)
                    for b in range(2):
                        last = pe.transpose(pst[:, q, b * P:(b + 1) * P], xn[:, s, k, b * P:(b + 1) * P], c.ident[:, :])
                    last.then_inc(turned, 1)
                pe.wait_ge(xt_made, g * UNROLL + UNROLL + 2)
                for m in range(4 * FC):
                    f, half, q = m // 2, m % 2, m % 2
                    pe.wait_ge(gelued, g * (4 * FC) + m + 1)
                    for b in range(2):
                        last = pe.matmul(psh[:, q, 0:NH], w1[:, f // FC, b, (f % FC) * P:(f % FC + 1) * P],
                                         xt[:, b, half * NH:(half + 1) * NH], start=(b == 0), stop=(b == 1))
                    last.then_inc(hidden, 1)
                pe.wait_ge(gelued, g * (4 * FC) + 4 * FC + 2)
                for k in range(UNROLL):
                    q = (s + k) % 2
                    pe.wait_ge(emptied, g * UNROLL + k + 1)
                    for f in range(2 * FC):
                        last = pe.matmul(psy[:, q, 0:D], hid[:, f, k * P:(k + 1) * P], w2[:, f // FC, f % FC, :],
                                         start=(f == 0), stop=(f == 2 * FC - 1))
                    last.then_inc(mixed, 1)
            groups(pe, body)

        @block.scalar
        def _(act):
            act.sem_inc(xt_made, 2)
            act.sem_inc(gelued, 2)
            act.wait_ge(wloaded, 160)

            def body(g, s, j):
                act.wait_ge(hidden, g * (4 * FC) + 2)
                for k in range(UNROLL):
                    act.wait_ge(turned, g * UNROLL + k + 1)
                    nc.scalar.copy(xt[:, :, k * P:(k + 1) * P],
                                   pst[:, (s + k) % 2, 0:2 * P].rearrange("p (b n) -> p b n", b=2)).then_inc(xt_made, 1)
                act.wait_ge(mixed, g * UNROLL + 1)
                for m in range(4 * FC):
                    f, half = m // 2, m % 2
                    act.wait_ge(hidden, g * (4 * FC) + m + 3)
                    nc.scalar.activation(hid[:, f, half * NH:(half + 1) * NH], psh[:, m % 2, 0:NH], ACT.Gelu,
                                         bias=b1s[:, f // FC, f % FC:f % FC + 1]).then_inc(gelued, 1)
            groups(act, body)

        @block.vector
        def _(dve):
            n = [0]

            def do(ins):
                ins.then_inc(step, 1)
                n[0] += 1
                dve.wait_ge(step, n[0])

            dve.sem_inc(mixed, 1)
            dve.sem_inc(emptied, 2)
            dve.wait_ge(wloaded, 160)
            for m in range(2):
                do(dve.tensor_scalar(w2[:, m], w2[:, m], c.share[:, m:m + 1], None, ALU.mult))
                do(dve.tensor_scalar(b2s[:, m, :], b2s[:, m, :], c.share[:, m:m + 1], None, ALU.mult))
            do(dve.tensor_tensor(b2s[:, 0, :], b2s[:, 0, :], b2s[:, 1, :], ALU.add))
            dve.sem_inc(wready, 1)
            base = n[0]
            bias = b2s[:, 0:1, :].broadcast_to([P, UNROLL, D])
            wide = lambda t: t[:, :].unsqueeze(1).broadcast_to([P, UNROLL, D])

            def body(g, s, j):
                dve.wait_ge(xin[s], 32 * j + 32)
                at = base + g * (UNROLL + 4)
                for k in range(UNROLL):
                    dve.wait_ge(mixed, g * UNROLL + k + 2)
                    dve.tensor_tensor(y[:, k, :], psy[:, (s + k) % 2, 0:D], xn[:, s, k, :], ALU.add).then_inc(step, 1)
                    dve.wait_ge(step, at + k + 1)
                    dve.sem_inc(emptied, 1)
                dve.tensor_tensor(y[:, :, :], y[:, :, :], bias, ALU.add).then_inc(step, 1)
                dve.wait_ge(step, at + UNROLL + 1)
                dve.wait_ge(stored[s], 16 * j + 16)
                normalise(dve, lnstep, rooted, g, y, yo[:, s], *ln, done=g * LN_STEPS)
                dve.tensor_tensor(yo[:, s], yo[:, s], wide(gam), ALU.mult).then_inc(step, 1)
                dve.wait_ge(step, at + UNROLL + 2)
                dve.tensor_tensor(yo[:, s], yo[:, s], wide(bet), ALU.add).then_inc(step, 1)
                dve.wait_ge(step, at + UNROLL + 3)
                dve.tensor_tensor(yo[:, s], yo[:, s], xr[:, s], ALU.add).then_inc(step, 1)
                dve.wait_ge(step, at + UNROLL + 4)
                dve.sem_inc(out, 1)
            groups(dve, body)


def prepare_conv(nc, c):
    c.phase = "prep"
    sem = lambda name: nc_sem(nc, c, name)
    rooted, lnstep, normed, passed, step, powd = (sem(s) for s in "rooted lnstep normed passed step powd".split())
    xin, stored = [sem("xin0"), sem("xin1")], [sem("stored0"), sem("stored1")]
    with ExitStack() as ctx:
        sb = lambda name, shape, dt: ctx.enter_context(nc.sbuf_tensor(f"prep_{name}", shape, dt))
        x, xn, xs = (sb(n, [P, 2, UNROLL, D], F32) for n in ("x", "xn", "xs"))
        half = sb("half", [P, TILES], F32)
        ln = ln_buffers(sb)
        block = ctx.enter_context(nc.Block())

        @block.sync
        def _(sp):
            def load(g, s, j):
                sp.wait_ge(normed, g + 1)
                sp.dma_start(x[:, s], rows(c.x2, g, D)).then_inc(xin[s], 16)
            groups(sp, load)

        @block.gpsimd
        def _(pool):
            pool.wait_ge(step, 2)
            pool.tensor_tensor(c.dis[:, :], c.deg[:, :], half[:, :], ALU.pow).then_inc(powd, 1)
            groups(pool, lambda g, s, j: root(pool, c, lnstep, rooted, passed, g, ln[2], ln[3]))

        @block.scalar
        def _(act):
            act.sem_inc(stored[0], 32)
            act.sem_inc(stored[1], 32)

            def store(g, s, j):
                act.wait_ge(normed, g + 3)
                act.dma_start(rows(c.xn2, g, D), xn[:, s]).then_inc(stored[s], 16)
                act.dma_start(rows(c.t_x, g, D), xs[:, s]).then_inc(stored[s], 16)
            groups(act, store)
            act.wait_ge(stored[0], 32 * 5)
            act.wait_ge(stored[1], 32 * 4)

        @block.vector
        def _(dve):
            dve.sem_inc(normed, 2)
            dve.tensor_scalar(half[:, :], c.zeros[:, 0:TILES], -0.5, None, ALU.add).then_inc(step, 1)
            dve.tensor_scalar(c.deg[:, :], c.deg[:, :], 1.0, None, ALU.add).then_inc(step, 1)
            dve.wait_ge(powd, 1)
            dve.tensor_tensor(c.dis[:, TILES - 1:TILES], c.dis[:, TILES - 1:TILES], c.valid[:, 0:1], ALU.mult
                              ).then_inc(step, 1)
            dve.wait_ge(step, 3)

            def body(g, s, j):
                dve.wait_ge(xin[s], 16 * j + 16)
                dve.wait_ge(stored[s], 32 * j + 32)
                normalise(dve, lnstep, rooted, g, x[:, s], xn[:, s], *ln, done=g * LN_STEPS)
                dis = c.dis[:, bass.ds(g * UNROLL, UNROLL)].unsqueeze(2).broadcast_to([P, UNROLL, D])
                dve.tensor_tensor(xs[:, s], xn[:, s], dis, ALU.mult).then_inc(step, 1)
                dve.wait_ge(step, 2 * g + 4)
                dve.sem_inc(passed, 1)
                dve.tensor_copy(c.acc[:, bass.ds(g * (UNROLL * D), UNROLL * D)],
                                xs[:, s].rearrange("p k d -> p (k d)")).then_inc(step, 1)
                dve.wait_ge(step, 2 * g + 5)
                dve.sem_inc(normed, 1)
            groups(dve, body)


def aggregate(nc, c, tag, table):
    c.phase = tag
    sem = lambda name: nc_sem(nc, c, name)
    copied, passed, oh_made, scattered, added = (sem(s) for s in "copied passed oh_made scattered added".split())
    gathered = [sem(f"gathered{k}") for k in range(QUADS)]
    with ExitStack() as ctx:
        few = ctx.enter_context(nc.sbuf_tensor(f"{tag}_few", [P, QUADS, QUAD], I32))
        sent = ctx.enter_context(nc.sbuf_tensor(f"{tag}_sent", [P, RING, D], F32))
        oh = ctx.enter_context(nc.sbuf_tensor(f"{tag}_oh", [P, RING, P], F32))
        ps_sum = ctx.enter_context(nc.psum_tensor(f"{tag}_sum", [P, 2 * QUAD, 512], F32))
        block = ctx.enter_context(nc.Block())

        @block.gpsimd
        def _(pool):
            gather_rows(pool, few, table, sent, gathered, scattered, copied, passed)

        @block.scalar
        def _(act):
            first_indices(nc, c.idx_d, few, copied)
            indices = lambda q, k, turn_: next_indices(nc, act, c.idx_d, few, gathered, copied, q, k, turn_)
            skewed(act, [(0, indices)], ET // QUAD, QUADS)

        @block.tensor
        def _(pe):
            pe.sem_inc(scattered, RING)

            def scatter(q, k, turn_):
                pe.wait_ge(oh_made, q + 1)
                pe.wait_ge(gathered[k], DONE * turn_ + DONE)
                for j in range(2):
                    pe.wait_ge(added, q * 2 + j + 1)
                    for m in (2 * j, 2 * j + 1):
                        pe.matmul(ps_sum[:, 2 * k + j, 0:D], oh[:, QUAD * k + m, :], sent[:, QUAD * k + m, :],
                                  start=(m % 2 == 0), stop=(m % 2 == 1)).then_inc(scattered, 1)
            skewed(pe, [(0, scatter)], ET // QUAD, QUADS)

        @block.vector
        def _(dve):
            dve.sem_inc(added, 8)

            def hots(q, k, turn_):
                dve.wait_ge(scattered, q * QUAD + QUAD)
                one_hots(dve, c, c.loc_d, oh, q, k, ALU.is_equal).then_inc(oh_made, 1)

            def add(q, k, turn_):
                for j in range(2):
                    pair = q * 2 + j
                    b = dve.value_load(c.buc_d[0:1, bass.ds(pair, 1)], min_val=0, max_val=TILES - 1)
                    dve.wait_ge(scattered, pair * 2 + RING + 2)
                    dve.wait_ge(added, pair + 8)
                    here = c.acc[:, bass.ds(b * D, D)]
                    dve.tensor_tensor(here, here, ps_sum[:, 2 * k + j, 0:D], ALU.add).then_inc(added, 1)
            skewed(dve, [(0, hots), (2, add)], ET // QUAD, QUADS)
            dve.wait_ge(added, PAIRS + 8)


def conv_hidden(nc, c, W1t, g1, b1, W2t):
    c.phase = "conv"
    FC = IC // P
    NH = UNROLL * P // 2
    PARTS = (0, 4), (4, UNROLL)
    LAST = N - (GROUPS - 1) * UNROLL * P - NH
    sem = lambda name: nc_sem(nc, c, name)
    (wloaded, scaled, turned, xt_made, hidden, statted, kept, passed, step, rooted, relued, sent, emptied, out) = (
        sem(s) for s in ("wloaded scaled turned xt_made hidden statted kept passed step rooted relued sent emptied "
                         "out").split())
    stored = [sem("stored0"), sem("stored1")]
    with ExitStack() as ctx:
        sb = lambda name, shape, dt: ctx.enter_context(nc.sbuf_tensor(f"conv_{name}", shape, dt))
        ps = lambda name, shape: ctx.enter_context(nc.psum_tensor(f"conv_ps_{name}", shape, F32))
        w1, w2 = sb("w1", [P, 2, IC], F32), sb("w2", [P, FC, D], F32)
        gb = sb("gb", [P, 2, FC], F32)
        y1 = sb("y1", [P, FC, NP], F32)
        st = sb("st", [P, FC, 2 * GROUPS * 6], F32)
        mv = sb("mv", [P, FC, 2], F32)
        coef = sb("coef", [P, 5, FC], F32)
        ag = sb("ag", [P, UNROLL, D], F32)
        hid = sb("hid", [P, FC, UNROLL * P], F32)
        xt = hid[:, 0:2, :]
        pst, psh = ps("t", [P, 2, 512]), ps("h", [P, 4, 512])
        with nc.Block() as block:
            @block.sync
            def _(sp):
                sp.dma_start(w1[:, :, :], W1t.rearrange("(k p) f -> p k f", p=P)).then_inc(wloaded, 16)
                sp.dma_start(w2[:, :, :], W2t.rearrange("(k p) f -> p k f", p=P)).then_inc(wloaded, 16)
                with nc.allow_non_contiguous_dma("norm weights, one element to a partition"):
                    sp.dma_start(gb[:, 0, :], g1.rearrange("(k p) -> p k", p=P)).then_inc(wloaded, 16)
                    sp.dma_start(gb[:, 1, :], b1.rearrange("(k p) -> p k", p=P)).then_inc(wloaded, 16)
                sp.wait_ge(wloaded, 64)

            @block.vector
            def _(dve):
                dve.sem_inc(turned, 14)

                def body(g, s, j):
                    acc = c.acc[:, bass.ds(g * (UNROLL * D), UNROLL * D)].rearrange("p (k d) -> p k d", d=D)
                    dis = c.dis[:, bass.ds(g * UNROLL, UNROLL)].unsqueeze(2).broadcast_to([P, UNROLL, D])
                    dve.wait_ge(turned, g * UNROLL + 14)
                    dve.tensor_tensor(ag[:, :, :], acc, dis, ALU.mult).then_inc(scaled, 1)
                    for m in range(2 * FC):
                        f, half = m // 2, m % 2
                        n = LAST if isinstance(g, int) and half else NH
                        dve.wait_ge(kept, g * (2 * FC) + m + 5)
                        dve.bn_stats(st[:, f, bass.ds((2 * g + half) * 6, 6)],
                                     y1[:, f, bass.ds(g * (UNROLL * P) + half * NH, n)]).then_inc(statted, 1)
                groups(dve, body)

            @block.scalar
            def _(act):
                act.sem_inc(xt_made, 2)
                act.sem_inc(kept, 4)

                def body(g, s, j):
                    act.wait_ge(hidden, g * (2 * FC) + 4)
                    for k in range(UNROLL):
                        act.wait_ge(turned, g * UNROLL + k + 15)
                        nc.scalar.copy(xt[:, :, k * P:(k + 1) * P],
                                       pst[:, (s + k) % 2, 0:2 * P].rearrange("p (b n) -> p b n", b=2)).then_inc(xt_made, 1)
                    for m in range(2 * FC):
                        f, half = m // 2, m % 2
                        act.wait_ge(hidden, g * (2 * FC) + m + 5)
                        nc.scalar.copy(y1[:, f, bass.ds(g * (UNROLL * P) + half * NH, NH)], psh[:, m % 4, 0:NH]
                                       ).then_inc(kept, 1)
                groups(act, body)

            @block.tensor
            def _(pe):
                pe.sem_inc(hidden, 4)
                pe.wait_ge(wloaded, 64)

                def body(g, s, j):
                    pe.wait_ge(scaled, g + 1)
                    for k in range(UNROLL):
                        pe.wait_ge(xt_made, g * UNROLL + k + 1)
                        for b in range(2):
                            last = pe.transpose(pst[:, (s + k) % 2, b * P:(b + 1) * P], ag[:, k, b * P:(b + 1) * P],
                                                c.ident[:, :])
                        last.then_inc(turned, 1)
                    pe.wait_ge(xt_made, g * UNROLL + UNROLL + 2)
                    for m in range(2 * FC):
                        f, half = m // 2, m % 2
                        pe.wait_ge(kept, g * (2 * FC) + m + 1)
                        for b in range(2):
                            last = pe.matmul(psh[:, m % 4, 0:NH], w1[:, b, f * P:(f + 1) * P],
                                             xt[:, b, half * NH:(half + 1) * NH], start=(b == 0), stop=(b == 1))
                        last.then_inc(hidden, 1)
                groups(pe, body)

        psy = ps("y", [P, 2, 512])
        block = ctx.enter_context(nc.Block())

        @block.gpsimd
        def _(pool):
            pool.wait_ge(step, 2)
            pool.tensor_tensor(coef[:, 1, :], coef[:, 0, :], c.neghalf[:, 0:FC], ALU.pow).then_inc(rooted, 1)

        @block.vector
        def _(dve):
            n = [0]

            def do(ins):
                ins.then_inc(step, 1)
                n[0] += 1
                dve.wait_ge(step, n[0])

            dve.sem_inc(emptied, 2)
            for f in range(FC):
                last = dve.bn_aggr(mv[:, f, :], st[:, f, :])
            do(last)
            do(dve.tensor_scalar(coef[:, 0, :], mv[:, :, 1], EPS, None, ALU.add))
            dve.wait_ge(rooted, 1)
            do(dve.tensor_tensor(coef[:, 2, :], coef[:, 1, :], gb[:, 0, :], ALU.mult))
            do(dve.tensor_tensor(coef[:, 3, :], mv[:, :, 0], coef[:, 2, :], ALU.mult))
            do(dve.tensor_tensor(coef[:, 4, :], gb[:, 1, :], coef[:, 3, :], ALU.subtract))
            base = n[0]

            def body(g, s, j):
                for k in range(UNROLL):
                    if k == 0:
                        dve.wait_ge(stored[0], 16 * g + 16)
                    at = base + g * (UNROLL + 1)
                    dve.wait_ge(sent, g * UNROLL + k + UNROLL + 1)
                    dve.tensor_scalar(ag[:, k, :], psy[:, (s + k) % 2, 0:D], c.dis[:, bass.ds(g * UNROLL + k, 1)], None,
                                      ALU.mult).then_inc(step, 1)
                    dve.wait_ge(step, at + k + 1)
                    dve.sem_inc(emptied, 1)
                dve.sem_inc(passed, 1)
                dve.tensor_copy(c.acc[:, bass.ds(g * (UNROLL * D), UNROLL * D)],
                                ag[:, :, :].rearrange("p k d -> p (k d)")).then_inc(step, 1)
                dve.wait_ge(step, base + g * (UNROLL + 1) + UNROLL + 1)
                dve.sem_inc(out, 1)
            groups(dve, body)

        @block.sync
        def _(sp):
            sp.sem_inc(stored[0], 16)

            def store(g, s, j):
                sp.wait_ge(out, g + 1)
                sp.dma_start(rows(c.t_x, g, D), ag[:, :, :]).then_inc(stored[0], 16)
            groups(sp, store)
            sp.wait_ge(stored[0], 16 * 8)

        @block.scalar
        def _(act):
            act.wait_ge(step, 5)

            def body(g, s, j):
                for lo, hi in PARTS:
                    act.wait_ge(sent, g * UNROLL + hi)
                    for f in range(FC):
                        last = nc.scalar.activation(hid[:, f, lo * P:hi * P],
                                                    y1[:, f, bass.ds((g * UNROLL + lo) * P, (hi - lo) * P)], ACT.Relu,
                                                    bias=coef[:, 4, f:f + 1], scale=coef[:, 2, f:f + 1])
                    last.then_inc(relued, 1)
            groups(act, body)

        @block.tensor
        def _(pe):
            pe.sem_inc(sent, UNROLL)

            def body(g, s, j):
                for k in range(UNROLL):
                    for n, (lo, hi) in enumerate(PARTS):
                        if k == lo:
                            pe.wait_ge(relued, len(PARTS) * g + n + 1)
                    pe.wait_ge(emptied, g * UNROLL + k + 1)
                    for f in range(FC):
                        last = pe.matmul(psy[:, (s + k) % 2, 0:D], hid[:, f, k * P:(k + 1) * P], w2[:, f, :], start=(f == 0),
                                         stop=(f == FC - 1))
                    last.then_inc(sent, 1)
            groups(pe, body)


def close_conv(nc, c, g2, b2, gate_w, gate_b):
    c.phase = "closeconv"
    sem = lambda name: nc_sem(nc, c, name)
    (loaded, scaled, meaned, squared, used, varied, step, rooted, lnstep, passed, normed, turned, xt_made, given,
     taken, done2) = (sem(s) for s in ("loaded scaled meaned squared used varied step rooted lnstep passed normed "
                                       "turned xt_made given taken done2").split())
    xin, stored = [sem("xin0"), sem("xin1")], [sem("stored0"), sem("stored1")]
    with ExitStack() as ctx:
        sb = lambda name, shape, dt: ctx.enter_context(nc.sbuf_tensor(f"closeconv_{name}", shape, dt))
        ps = lambda name, shape: ctx.enter_context(nc.psum_tensor(f"closeconv_ps_{name}", shape, F32))
        gam, bet, mean, rstd = (sb(n, [P, D], F32) for n in ("gam", "bet", "bmean", "brstd"))
        vcol = sb("vcol", [P, 4], F32)
        gw, gb = sb("gw", [P, 2, X1], F32), sb("gb", [P, X1], F32)
        vones = sb("vones", [P, P], F32)
        sq = sb("sq", [P, 2, UNROLL, D], F32)
        ps_m, ps_v = ps("m", [P, 512]), ps("v", [P, 512])
        with nc.Block() as block:
            @block.sync
            def _(sp):
                for t, d in ((gam, g2), (bet, b2), (gb, gate_b)):
                    sp.dma_start(t[:, :], d.rearrange("(a e) -> a e", a=1).broadcast_to([P, d.shape[0]])
                                 ).then_inc(loaded, 16)
                sp.dma_start(gw[:, :, :], gate_w.rearrange("(k p) e -> p k e", p=P)).then_inc(loaded, 16)
                sp.wait_ge(loaded, 64)

            @block.tensor
            def _(pe):
                pe.sem_inc(used, 2)
                pe.wait_ge(step, 1)
                pe.matmul(ps_m[:, 0:D], c.zeros[:, 0:P], c.zeros[:, 0:D], start=True, stop=False)

                def add(g, s, j):
                    pe.wait_ge(scaled, g + 1)
                    for k in range(UNROLL):
                        pe.matmul(ps_m[:, 0:D], c.ones[:, :], c.acc[:, bass.ds((g * UNROLL + k) * D, D)], start=False,
                                  stop=False)
                groups(pe, add)
                pe.matmul(ps_m[:, 0:D], c.zeros[:, 0:P], c.zeros[:, 0:D], start=False, stop=True).then_inc(meaned, 1)
                pe.matmul(ps_v[:, 0:D], c.zeros[:, 0:P], c.zeros[:, 0:D], start=True, stop=False)

                def add_squares(g, s, j):
                    pe.wait_ge(squared, g + 1)
                    for k in range(UNROLL):
                        real = vones if isinstance(g, int) and k == UNROLL - 1 else c.ones
                        last = pe.matmul(ps_v[:, 0:D], real[:, :], sq[:, s, k, :], start=False, stop=False)
                    last.then_inc(used, 1)
                groups(pe, add_squares)
                pe.matmul(ps_v[:, 0:D], c.zeros[:, 0:P], c.zeros[:, 0:D], start=False, stop=True).then_inc(meaned, 1)
                pe.wait_ge(varied, 2)
                pe.matmul(ps_m[:, 0:D], c.ones[:, :], rstd[:, :], start=True, stop=True).then_inc(meaned, 1)

            @block.gpsimd
            def _(pool):
                pool.wait_ge(varied, 1)
                pool.tensor_tensor(vcol[:, 2:4], vcol[:, 0:2], c.neghalf[:, 0:2], ALU.pow).then_inc(rooted, 1)

            @block.vector
            def _(dve):
                n = [0]

                def do(ins):
                    ins.then_inc(step, 1)
                    n[0] += 1
                    dve.wait_ge(step, n[0])

                do(dve.tensor_scalar(vones[:, :], c.ones[:, :], c.valid[:, 0:1], None, ALU.mult))
                view = lambda g: c.acc[:, bass.ds(g * (UNROLL * D), UNROLL * D)].rearrange("p (k d) -> p k d", d=D)

                def scale(g, s, j):
                    dis = c.dis[:, bass.ds(g * UNROLL, UNROLL)].unsqueeze(2).broadcast_to([P, UNROLL, D])
                    dve.tensor_tensor(view(g), view(g), dis, ALU.mult).then_inc(scaled, 1)
                groups(dve, scale)
                dve.wait_ge(meaned, 1)
                dve.wait_ge(scaled, GROUPS)
                do(dve.tensor_scalar(mean[:, :], ps_m[:, 0:D], 1.0 / N, None, ALU.mult))
                wide = mean[:, :].unsqueeze(1).broadcast_to([P, UNROLL, D])

                def square(g, s, j):
                    dve.wait_ge(used, g + 1)
                    dve.tensor_tensor(view(g), view(g), wide, ALU.subtract).then_inc(done2, 1)
                    dve.wait_ge(done2, g + 1)
                    dve.tensor_tensor(sq[:, s], view(g), view(g), ALU.mult).then_inc(squared, 1)
                groups(dve, square)
                dve.wait_ge(meaned, 2)
                dve.wait_ge(squared, GROUPS)
                do(dve.tensor_scalar(mean[:, :], ps_v[:, 0:D], 1.0 / N, EPS, ALU.mult, ALU.add))
                halved = lambda t: t[:, :].rearrange("p (b f) -> p b f", b=2)
                twice = c.ident[:, :].unsqueeze(1).broadcast_to([P, 2, P])
                do(dve.tensor_tensor(halved(rstd), halved(mean), twice, ALU.mult))
                dve.tensor_reduce(vcol[:, 0:2], halved(rstd), AX.X, ALU.add).then_inc(varied, 1)
                dve.wait_ge(rooted, 1)
                dve.tensor_tensor(halved(rstd), vcol[:, 2:4].unsqueeze(2).broadcast_to([P, 2, P]), twice, ALU.mult
                                  ).then_inc(varied, 1)
                dve.wait_ge(meaned, 3)
                dve.wait_ge(loaded, 64)
                do(dve.tensor_tensor(gam[:, :], gam[:, :], ps_m[:, 0:D], ALU.mult))

        x, xn, xr = (sb(n, [P, 2, UNROLL, D], F32) for n in ("x", "xn", "xr"))
        x3 = sq
        ln = ln_buffers(sb)
        xt = sb("xt", [P, 2, 2, P], F32)
        pst, psg = ps("t", [P, 2, 512]), ps("g", [P, 2, 512])
        block = ctx.enter_context(nc.Block())
        base = 5

        @block.sync
        def _(sp):
            def load(g, s, j):
                sp.wait_ge(normed, g + 1)
                sp.dma_start(xr[:, s], rows(c.x2, g, D)).then_inc(xin[s], 16)
                sp.dma_start(x[:, s], rows(c.xn2, g, D)).then_inc(xin[s], 16)
            groups(sp, load)

        @block.gpsimd
        def _(pool):
            groups(pool, lambda g, s, j: root(pool, c, lnstep, rooted, passed, g + 1, ln[2], ln[3], done=-LN_STEPS))

        @block.vector
        def _(dve):
            dve.sem_inc(normed, 2)
            view = lambda g: c.acc[:, bass.ds(g * (UNROLL * D), UNROLL * D)].rearrange("p (k d) -> p k d", d=D)
            wide = lambda t: t[:, :].unsqueeze(1).broadcast_to([P, UNROLL, D])

            def body(g, s, j):
                at = base + 4 * g

                def do(ins, n):
                    ins.then_inc(step, 1)
                    dve.wait_ge(step, at + n)
                dve.wait_ge(xin[s], 32 * j + 32)
                dve.wait_ge(stored[s], 32 * j + 32)
                dve.wait_ge(turned, g * UNROLL + UNROLL)
                do(dve.tensor_tensor(x3[:, s], view(g), wide(gam), ALU.mult), 1)
                do(dve.tensor_tensor(x3[:, s], x3[:, s], wide(bet), ALU.add), 2)
                do(dve.tensor_tensor(x3[:, s], x3[:, s], x[:, s], ALU.add), 3)
                do(dve.scalar_tensor_tensor(out=x3[:, s].rearrange("p k d -> p (k d)"),
                                            in0=x3[:, s].rearrange("p k d -> p (k d)"), scalar=0.0,
                                            in1=xr[:, s].rearrange("p k d -> p (k d)"), op0=ALU.max, op1=ALU.add), 4)
                normalise(dve, lnstep, rooted, g + 1, x3[:, s], xn[:, s], *ln, done=g * LN_STEPS)
                dve.sem_inc(normed, 1)
                dve.wait_ge(given, g + 1)
                dve.tensor_tensor(c.logit[:, bass.ds(g * (UNROLL * X1), UNROLL * X1)].rearrange("p (k e) -> p k e", e=X1),
                                  psg[:, s, 0:UNROLL * X1].rearrange("p (k e) -> p k e", e=X1),
                                  gb[:, :].unsqueeze(1).broadcast_to([P, UNROLL, X1]), ALU.add).then_inc(taken, 1)
            groups(dve, body)
            dve.wait_ge(taken, GROUPS)

        @block.scalar
        def _(act):
            act.sem_inc(xt_made, 2)
            act.sem_inc(stored[0], 32)
            act.sem_inc(stored[1], 32)

            def body(g, s, j):
                act.wait_ge(normed, g + 3)
                act.dma_start(rows(c.x3, g, D), x3[:, s]).then_inc(stored[s], 16)
                act.dma_start(rows(c.xn3, g, D), xn[:, s]).then_inc(stored[s], 16)
                for k in range(UNROLL):
                    act.wait_ge(turned, g * UNROLL + k + 15)
                    nc.scalar.copy(xt[:, (s + k) % 2], pst[:, (s + k) % 2, 0:2 * P].rearrange("p (b n) -> p b n", b=2)
                                   ).then_inc(xt_made, 1)
            groups(act, body)
            act.wait_ge(stored[0], 32 * 5)
            act.wait_ge(stored[1], 32 * 4)

        @block.tensor
        def _(pe):
            pe.sem_inc(turned, 14)

            def body(g, s, j):
                pe.wait_ge(normed, g + 3)
                for k in range(UNROLL + 1):
                    if k < UNROLL:
                        q = (s + k) % 2
                        pe.wait_ge(xt_made, g * UNROLL + k + 1)
                        for b in range(2):
                            last = pe.transpose(pst[:, q, b * P:(b + 1) * P], xn[:, s, k, b * P:(b + 1) * P],
                                                c.ident[:, :])
                        last.then_inc(turned, 1)
                    if k > 0:
                        q = (s + k - 1) % 2
                        pe.wait_ge(xt_made, g * UNROLL + k + 2)
                        for b in range(2):
                            last = pe.matmul(psg[:, s, (k - 1) * X1:k * X1], xt[:, q, b, :], gw[:, b, :],
                                             start=(b == 0), stop=(b == 1))
                last.then_inc(given, 1)
            groups(pe, body)


def route(nc, c):
    c.phase = "route"
    sem = lambda name: nc_sem(nc, c, name)
    step, given, peed = (sem(s) for s in "step given peed".split())
    T8 = TILES * X1
    with ExitStack() as ctx:
        sb = lambda name, shape, dt: ctx.enter_context(nc.sbuf_tensor(f"route_{name}", shape, dt))
        p, e, oh, inc, tot, before, tmp = (sb(n, [P, T8], F32) for n in "p e oh inc tot before tmp".split())
        mx, sm, pm, idx, pos, kept, to, node = (sb(n, [P, TILES], F32) for n in "mx sm pm idx pos kept to node".split())
        ps1, ps2 = (ctx.enter_context(nc.psum_tensor(f"route_ps{m}", [P, 512], F32)) for m in range(2))
        block = ctx.enter_context(nc.Block())
        te = lambda t: t[:, :].rearrange("p (t e) -> p t e", e=X1)
        et = lambda t: t[:, :].rearrange("p (e t) -> p e t", e=X1)
        w8 = lambda t: t[:, :].unsqueeze(2).broadcast_to([P, TILES, X1])

        @block.gpsimd
        def _(pool):
            nc.gpsimd.iota(node[:, :], [[P, TILES]], base=0, channel_multiplier=1,
                           allow_small_or_imprecise_dtypes=True).then_inc(peed, 1)

        @block.scalar
        def _(act):
            act.wait_ge(given, 1)
            nc.scalar.activation(e[:, :], p[:, :], ACT.Exp).then_inc(peed, 1)

        @block.tensor
        def _(pe):
            pe.wait_ge(given, 2)
            pe.matmul(ps1[:, 0:T8], c.below[:, :], oh[:, :], start=True, stop=True)
            pe.matmul(ps2[:, 0:T8], c.ones[:, :], oh[:, :], start=True, stop=True).then_inc(peed, 1)

        @block.vector
        def _(dve):
            n = [0]

            def do(ins):
                ins.then_inc(step, 1)
                n[0] += 1
                dve.wait_ge(step, n[0])

            do(dve.tensor_reduce(mx[:, :], te(c.logit), AX.X, ALU.max))
            do(dve.tensor_tensor(te(p), te(c.logit), w8(mx), ALU.subtract))
            dve.sem_inc(given, 1)
            dve.wait_ge(peed, 2)
            do(dve.tensor_reduce(sm[:, :], te(e), AX.X, ALU.add))
            do(dve.reciprocal(sm[:, :], sm[:, :]))
            do(dve.tensor_tensor(te(p), te(e), w8(sm), ALU.mult))
            do(dve.tensor_reduce(pm[:, :], te(p), AX.X, ALU.max))
            do(dve.tensor_tensor(te(oh), te(p), w8(pm), ALU.is_lt))
            eight = c.iota[:, 0:X1].unsqueeze(1).broadcast_to([P, TILES, X1])
            do(dve.tensor_scalar(oh[:, :], oh[:, :], 100.0, None, ALU.mult))
            do(dve.tensor_tensor(te(tmp), te(oh), eight, ALU.add))
            do(dve.tensor_reduce(idx[:, :], te(tmp), AX.X, ALU.min))
            do(dve.tensor_tensor(te(oh), w8(idx), eight, ALU.is_equal))
            do(dve.tensor_scalar(oh[:, T8 - X1:T8], oh[:, T8 - X1:T8], c.valid[:, 0:1], None, ALU.mult))
            dve.sem_inc(given, 1)
            dve.wait_ge(peed, 3)
            do(dve.tensor_copy(et(tot), ps2[:, 0:T8].rearrange("p (t e) -> p e t", e=X1)))
            for x in range(X1):
                last = dve.tensor_tensor_scan(inc[:, x * TILES:(x + 1) * TILES], tot[:, x * TILES:(x + 1) * TILES],
                                              c.zeros[:, 0:TILES], 0.0, ALU.add, ALU.add)
            do(last)
            do(dve.tensor_tensor(before[:, :], inc[:, :], tot[:, :], ALU.subtract))
            do(dve.tensor_tensor(te(tmp), before[:, :].rearrange("p (e t) -> p t e", e=X1), te(ps1[:, 0:T8]), ALU.add))
            do(dve.tensor_tensor(tmp[:, :], tmp[:, :], oh[:, :], ALU.mult))
            do(dve.tensor_reduce(pos[:, :], te(tmp), AX.X, ALU.add))
            do(dve.tensor_scalar(kept[:, :], pos[:, :], float(CAP), None, ALU.is_lt))
            do(dve.tensor_scalar(kept[:, TILES - 1:TILES], kept[:, TILES - 1:TILES], c.valid[:, 0:1], None, ALU.mult))
            do(dve.tensor_tensor(c.gate[:, :], pm[:, :], kept[:, :], ALU.mult))
            do(dve.tensor_scalar(pos[:, :], pos[:, :], float(CAP - 1), None, ALU.min))
            do(dve.tensor_scalar(sm[:, :], idx[:, :], float(CAP), None, ALU.mult))
            do(dve.tensor_tensor(c.take[:, :], pos[:, :], sm[:, :], ALU.add))
            do(dve.tensor_scalar(idx[:, :], idx[:, :], float(SLOTS), None, ALU.mult))
            do(dve.tensor_tensor(pos[:, :], pos[:, :], idx[:, :], ALU.add))
            do(dve.tensor_scalar(node[:, :], node[:, :], float(X1 * SLOTS), None, ALU.add))
            do(dve.tensor_tensor(to[:, :], pos[:, :], node[:, :], ALU.subtract))
            do(dve.tensor_tensor(to[:, :], to[:, :], kept[:, :], ALU.mult))
            do(dve.tensor_tensor(c.put[:, :], to[:, :], node[:, :], ALU.add))


def dispatch(nc, c):
    c.phase = "dispatch"
    sem = lambda name: nc_sem(nc, c, name)
    copied, passed, free = (sem(s) for s in "copied passed free".split())
    xin, sent = [sem("xin0"), sem("xin1")], [sem("sent0"), sem("sent1")]
    with ExitStack() as ctx:
        sb = lambda name, shape, dt: ctx.enter_context(nc.sbuf_tensor(f"dispatch_{name}", shape, dt))
        x = sb("x", [P, 2, UNROLL, D], F32)
        few = sb("few", [P, 2, UNROLL], I32)
        block = ctx.enter_context(nc.Block())

        @block.sync
        def _(sp):
            def load(g, s, j):
                sp.wait_ge(free, g + 1)
                sp.dma_start(x[:, s], rows(c.xn3, g, D)).then_inc(xin[s], 16)
            groups(sp, load)

        @block.gpsimd
        def _(pool):
            pool.sem_inc(free, 2)

            def send(g, s, turn, before):
                pool.wait_ge(xin[s], 16 * turn + 16)
                pool.sem_inc(passed, 1)
                pool.tensor_copy(few[:, s, :], c.put[:, bass.ds(g * UNROLL, UNROLL)]).then_inc(copied, 1)
                pool.wait_ge(copied, g + 1)
                pool.sem_inc(passed, 1)
                for k in range(UNROLL):
                    pool.indirect_dma_start(out=c.slots_in[:, :], in_=x[:, s, k, :], in_offset=None,
                                            out_offset=bass.IndirectOffsetOnAxis(ap=few[:, s, k:k + 1], axis=0)
                                            ).then_inc(sent[s], 16)
                if before is not None:
                    pool.wait_ge(sent[1 - s], 16 * UNROLL * before + 16 * UNROLL)
                    pool.sem_inc(free, 1)
            send(0, 0, 0, None)
            with pool.Fori(0, GROUPS // 2) as i:
                send(2 * i + 1, 1, i, i)
                send(2 * i + 2, 0, i + 1, i)
            pool.wait_ge(sent[0], 16 * UNROLL * 4)
            pool.wait_ge(sent[1], 16 * UNROLL * 3)


def experts1(nc, c, w1, b1, w2, b2):
    c.phase = "experts1"
    FC, TC = F1 // P, SLOTS // P
    HALVES = ((0, 489), (489, CAP))
    LASTM = CAP - (TC - 1) * P
    sem = lambda name: nc_sem(nc, c, name)
    (turned, xt_made, hidden, relued, mixed, emptied, wfree, yfree, passed) = (
        sem(s) for s in "turned xt_made hidden relued mixed emptied wfree yfree passed".split())
    loaded, stored = [sem("loaded0"), sem("loaded1")], [sem("stored0"), sem("stored1")]
    with ExitStack() as ctx:
        sb = lambda name, shape, dt: ctx.enter_context(nc.sbuf_tensor(f"experts1_{name}", shape, dt))
        ps = lambda name, shape: ctx.enter_context(nc.psum_tensor(f"experts1_ps_{name}", shape, F32))
        x = sb("x", [P, 2, TC, D], F32)
        w1s, w2s = sb("w1", [P, 2, 2, F1], F32), sb("w2", [P, 2, FC, D], F32)
        b1s, b2s = sb("b1", [P, 2, FC], F32), sb("b2", [P, 2, D], F32)
        xt = sb("xt", [P, 2, SLOTS], F32)
        hid = sb("hid", [P, FC, SLOTS], F32)
        y = sb("y", [P, 2, TC, D], F32)
        pst, psh, psy = ps("t", [P, 2, 512]), ps("h", [P, 2, 512]), ps("y", [P, 2, 512])
        block = ctx.enter_context(nc.Block())

        def experts(eng, body):
            with eng.Fori(0, X1 // 2) as i:
                body(2 * i, 0, i)
                body(2 * i + 1, 1, i)

        @block.sync
        def _(sp):
            def load(e, s, j):
                sp.wait_ge(wfree, e + 1)
                one = bass.ds(e, 1)
                sp.dma_start(x[:, s], c.slots_in[bass.ds(e * SLOTS, SLOTS), :].rearrange("(k p) d -> p k d", p=P)
                             ).then_inc(loaded[s], 16)
                sp.dma_start(w1s[:, s], w1[one].rearrange("a (k p) f -> p (a k) f", p=P)).then_inc(loaded[s], 16)
                sp.dma_start(w2s[:, s], w2[one].rearrange("a (k p) f -> p (a k) f", p=P)).then_inc(loaded[s], 16)
                with nc.allow_non_contiguous_dma("a bias, one element to a partition"):
                    sp.dma_start(b1s[:, s, :], b1[one].rearrange("a (k p) -> p (a k)", p=P)).then_inc(loaded[s], 16)
                sp.dma_start(b2s[:, s, :], b2[one].broadcast_to([P, D])).then_inc(loaded[s], 16)
            experts(sp, load)

        @block.tensor
        def _(pe):
            pe.sem_inc(hidden, 2)
            pe.sem_inc(mixed, 1)

            def body(e, s, j):
                pe.wait_ge(loaded[s], 80 * j + 80)
                for k in range(TC):
                    pe.wait_ge(xt_made, e * TC + k + 1)
                    for b in range(2):
                        last = pe.transpose(pst[:, k % 2, b * P:(b + 1) * P], x[:, s, k, b * P:(b + 1) * P],
                                            c.ident[:, :])
                    last.then_inc(turned, 1)
                pe.wait_ge(xt_made, e * TC + TC + 2)
                for m in range(2 * FC):
                    f, (lo, hi) = m // 2, HALVES[m % 2]
                    pe.wait_ge(relued, e * (2 * FC) + m + 1)
                    for b in range(2):
                        last = pe.matmul(psh[:, m % 2, 0:hi - lo], w1s[:, s, b, f * P:(f + 1) * P], xt[:, b, lo:hi],
                                         start=(b == 0), stop=(b == 1))
                    last.then_inc(hidden, 1)
                pe.wait_ge(relued, e * (2 * FC) + 2 * FC + 2)
                for k in range(TC):
                    n = LASTM if k == TC - 1 else P
                    pe.wait_ge(emptied, e * TC + k + 1)
                    for f in range(FC):
                        last = pe.matmul(psy[0:n, k % 2, 0:D], hid[:, f, k * P:k * P + n], w2s[:, s, f, :],
                                         start=(f == 0), stop=(f == FC - 1))
                    last.then_inc(mixed, 1)
            experts(pe, body)

        @block.scalar
        def _(act):
            act.sem_inc(xt_made, 2)
            act.sem_inc(relued, 2)

            def body(e, s, j):
                act.wait_ge(loaded[s], 80 * j + 80)
                act.wait_ge(hidden, e * (2 * FC) + 2)
                for k in range(TC):
                    act.wait_ge(turned, e * TC + k + 1)
                    nc.scalar.copy(xt[:, :, k * P:(k + 1) * P],
                                   pst[:, k % 2, 0:2 * P].rearrange("p (b n) -> p b n", b=2)).then_inc(xt_made, 1)
                act.wait_ge(mixed, e * TC + 1)
                for m in range(2 * FC):
                    f, (lo, hi) = m // 2, HALVES[m % 2]
                    act.wait_ge(hidden, e * (2 * FC) + m + 3)
                    nc.scalar.activation(hid[:, f, lo:hi], psh[:, m % 2, 0:hi - lo], ACT.Relu,
                                         bias=b1s[:, s, f:f + 1]).then_inc(relued, 1)
            experts(act, body)

        @block.vector
        def _(dve):
            dve.sem_inc(emptied, 2)
            dve.sem_inc(wfree, 2)

            def body(e, s, j):
                dve.wait_ge(loaded[s], 80 * j + 80)
                dve.wait_ge(yfree, e + 1)
                for k in range(TC):
                    n = LASTM if k == TC - 1 else P
                    dve.wait_ge(mixed, e * TC + k + 2)
                    last = dve.tensor_tensor(y[0:n, s, k, :], psy[0:n, k % 2, 0:D], b2s[0:n, s, :], ALU.add)
                    last.then_inc(emptied, 1)
                dve.wait_ge(emptied, e * TC + TC + 2)
                dve.sem_inc(wfree, 1)
            experts(dve, body)

        @block.gpsimd
        def _(pool):
            pool.sem_inc(yfree, 2)

            def store(e, s, j):
                pool.wait_ge(wfree, e + 3)
                pool.sem_inc(passed, 1)
                pool.dma_start(c.slots_out[bass.ds(e * CAP, (TC - 1) * P), :].rearrange("(k p) d -> p k d", p=P),
                               y[:, s, 0:TC - 1, :]).then_inc(stored[s], 16)
                pool.dma_start(c.slots_out[bass.ds(e * CAP + (TC - 1) * P, LASTM), :], y[0:LASTM, s, TC - 1, :]
                               ).then_inc(stored[s], 16)
                pool.wait_ge(stored[s], 32 * j + 32)
                pool.sem_inc(yfree, 1)
            experts(pool, store)


def combine(nc, c, out):
    c.phase = "combine"
    BIG = 3.4028234663852886e38
    sem = lambda name: nc_sem(nc, c, name)
    copied, passed, summed, step, gated = (sem(s) for s in "copied passed summed step gated".split())
    xin, got, stored = ([sem(f"{n}0"), sem(f"{n}1")] for n in ("xin", "got", "stored"))
    with ExitStack() as ctx:
        sb = lambda name, shape, dt: ctx.enter_context(nc.sbuf_tensor(f"combine_{name}", shape, dt))
        x, y, z, o = (sb(n, [P, 2, UNROLL * D], F32) for n in "xyzo")
        fill = sb("fill", [P, 3, UNROLL * D], F32)
        mask = sb("mask", [P, 2, 3, UNROLL * D], I32)
        few = sb("few", [P, 2, UNROLL], I32)
        block = ctx.enter_context(nc.Block())
        tiles = lambda t, s: t[:, s, :].rearrange("p (k d) -> p k d", d=D)

        @block.sync
        def _(sp):
            def load(g, s, j):
                sp.wait_ge(summed, g + 1)
                sp.dma_start(tiles(x, s), rows(c.x3, g, D)).then_inc(xin[s], 16)
            groups(sp, load)

        @block.gpsimd
        def _(pool):
            def fetch(g, s, j):
                pool.wait_ge(summed, g + 1)
                pool.sem_inc(passed, 1)
                pool.tensor_copy(few[:, s, :], c.take[:, bass.ds(g * UNROLL, UNROLL)]).then_inc(copied, 1)
                pool.wait_ge(copied, g + 1)
                pool.sem_inc(passed, 1)
                for k in range(UNROLL):
                    pool.indirect_dma_start(out=y[:, s, k * D:(k + 1) * D], out_offset=None, in_=c.slots_out[:, :],
                                            in_offset=bass.IndirectOffsetOnAxis(ap=few[:, s, k:k + 1], axis=0)
                                            ).then_inc(got[s], 16)
            groups(pool, fetch)

        @block.vector
        def _(dve):
            dve.sem_inc(summed, 2)
            dve.memset(fill[:, 0, :], 0.0).then_inc(step, 1)
            dve.memset(fill[:, 1, :], 1e4).then_inc(step, 1)
            dve.memset(fill[:, 2, :], -1e4).then_inc(step, 1)
            dve.wait_ge(step, 3)

            def body(g, s, j):
                def do(ins, n):
                    ins.then_inc(step, 1)
                    dve.wait_ge(step, 7 * g + 3 + n)
                dve.wait_ge(gated, g + 1)
                dve.wait_ge(xin[s], 16 * j + 16)
                dve.wait_ge(stored[s], 16 * j + 16)
                do(dve.tensor_tensor(mask[:, s, 0, :], z[:, s], z[:, s], ALU.not_equal), 1)
                do(dve.tensor_scalar(mask[:, s, 1, :], z[:, s], BIG, None, ALU.is_gt), 2)
                do(dve.tensor_scalar(mask[:, s, 2, :], z[:, s], -BIG, None, ALU.is_lt), 3)
                for m in range(3):
                    dve.sem_inc(passed, 1)
                    dve.copy_predicated(z[:, s], mask[:, s, m, :], fill[:, m, :]).then_inc(step, 1)
                    dve.wait_ge(step, 7 * g + 7 + m)
                do(dve.tensor_tensor(o[:, s], z[:, s], x[:, s], ALU.add), 7)
                dve.sem_inc(summed, 1)
            groups(dve, body)

        @block.scalar
        def _(act):
            act.sem_inc(stored[0], 16)
            act.sem_inc(stored[1], 16)

            def weigh(g, s, j):
                act.wait_ge(got[s], 16 * UNROLL * j + 16 * UNROLL)
                act.wait_ge(summed, g + 1)
                for k in range(UNROLL):
                    last = nc.scalar.activation(tiles(z, s)[:, k], tiles(y, s)[:, k], ACT.Copy,
                                                scale=c.gate[:, bass.ds(g * UNROLL + k, 1)])
                last.then_inc(gated, 1)

            def store(g, s):
                act.wait_ge(summed, g + 3)
                if isinstance(g, int):
                    at = g * UNROLL * P
                    full = (N - at) // P
                    act.dma_start(out[at:at + full * P, :].rearrange("(k p) d -> p k d", p=P), tiles(o, s)[:, 0:full]
                                  ).then_inc(stored[s], 16)
                    act.dma_start(out[at + full * P:N, :], tiles(o, s)[0:(N - at) % P, full, :]
                                  ).then_inc(stored[s], 16)
                else:
                    act.dma_start(rows(out, g, D), tiles(o, s)).then_inc(stored[s], 16)
            weigh(0, 0, 0)
            with act.Fori(0, GROUPS // 2) as i:
                weigh(2 * i + 1, 1, i)
                store(2 * i, 0)
                weigh(2 * i + 2, 0, i + 1)
                store(2 * i + 1, 1)
            store(GROUPS - 1, 0)
            act.wait_ge(stored[0], 16 * 6)
            act.wait_ge(stored[1], 16 * 4)



def build(nc, a, out):
    c = Ctx()
    with ExitStack() as ctx:
        c.ctx = ctx
        c.phase, c.sems = "setup", []
        dram = lambda name, shape, dt=F32: nc.dram_tensor(name, shape, dt, kind="Internal").ap()
        sb = lambda name, shape, dt: ctx.enter_context(nc.sbuf_tensor(name, shape, dt))
        c.x0, c.x1, c.xn1, c.x2, c.xn2, c.x3, c.xn3, c.t_x = (
            dram(name, [NP, D]) for name in ("x0", "x1", "xn1", "x2", "xn2", "x3", "xn3", "t_x"))
        c.t_h, c.t_hr = dram("t_h", [NP, D + 4]), dram("t_hr", [NP, 4])
        c.slots_in = dram("slots_in", [X1 * SLOTS + NP, D])
        c.slots_dst = dram("slots_dst", [P * ET, 2], I32)
        c.slots_out = dram("slots_out", [X1 * CAP, D])
        setup(nc, c, ctx)
        c.idx_d, c.loc_d, c.buc_d = sb("idx_d", [P, ET + RING], I32), sb("loc_d", [P, ET], F32), sb("buc_d", [1, PAIRS], I32)
        c.deg, c.dis = sb("deg", [P, TILES], F32), sb("dis", [P, TILES], F32)
        c.colsum, c.share, c.chosen = sb("colsum", [P, 2], F32), sb("share", [P, 2], F32), sb("chosen", [1, 2], I32)
        c.logit = sb("logit", [P, TILES * X1], F32)
        c.put, c.take, c.gate = sb("put", [P, TILES], I32), sb("take", [P, TILES], I32), sb("gate", [P, TILES], F32)
        with ExitStack() as att:
            sa = lambda name, shape, dt: att.enter_context(nc.sbuf_tensor(name, shape, dt))
            c.idx_s, c.loc_s, c.buc_s = sa("idx_s", [P, ET + RING], I32), sa("loc_s", [P, ET], F32), sa("buc_s", [1, PAIRS], I32)
            c.reset_s, c.last_s = sa("reset_s", [P, PAIRS, 2], F32), sa("last_s", [1, TILES], I32)
            sort_edges(nc, c, a["x"], a["src"], a["dst"])
            c.hlm = sa("hlm", [P, TILES * 8], F32)
            c.acc = sa("acc_heads", [P, TILES * (D + 4)], F32)
            project_heads(nc, c, a["L0_gnn_W"], a["L0_gnn_a_l"], a["L0_gnn_a_r"])
            neighbour_max(nc, c)
            attend(nc, c)
            close_attention(nc, c)
        recycle(nc, c)
        choose_experts(nc, c, a["L0_ffn_Wr"], a["L0_ffn_br"])
        experts0(nc, c, a["L0_ffn_W1"], a["L0_ffn_b1"], a["L0_ffn_W2"], a["L0_ffn_b2"], a["L0_ffn_gamma"],
                 a["L0_ffn_beta"])
        with ExitStack() as conv:
            c.acc = conv.enter_context(nc.sbuf_tensor("acc_conv", [P, TILES * D], F32))
            prepare_conv(nc, c)
            aggregate(nc, c, "conv1", c.t_x)
            conv_hidden(nc, c, a["L1_gnn_W1"], a["L1_gnn_g1"], a["L1_gnn_b1"], a["L1_gnn_W2"])
            aggregate(nc, c, "conv2", c.t_x)
            recycle(nc, c)
            close_conv(nc, c, a["L1_gnn_g2"], a["L1_gnn_b2"], a["L1_ffn_gate_w"], a["L1_ffn_gate_b"])
        route(nc, c)
        dispatch(nc, c)
        experts1(nc, c, a["L1_ffn_w1"], a["L1_ffn_b1"], a["L1_ffn_w2"], a["L1_ffn_b2"])
        combine(nc, c, out)


_INS = ['x', 'src', 'dst', 'L0_gnn_W', 'L0_gnn_a_l', 'L0_gnn_a_r', 'L0_ffn_Wr', 'L0_ffn_br', 'L0_ffn_W1',
        'L0_ffn_b1', 'L0_ffn_W2', 'L0_ffn_b2', 'L0_ffn_gamma', 'L0_ffn_beta', 'L1_gnn_W1', 'L1_gnn_g1', 'L1_gnn_b1',
        'L1_gnn_W2', 'L1_gnn_g2', 'L1_gnn_b2', 'L1_ffn_gate_w', 'L1_ffn_gate_b', 'L1_ffn_w1', 'L1_ffn_b1',
        'L1_ffn_w2', 'L1_ffn_b2']
_TURNED = ('L1_gnn_W1', 'L1_gnn_W2')
_OUTS = [((N, D), 'float32')]


def kernel(**inputs):
    import numpy as _np
    import concourse.bacc as _bacc
    from concourse import mybir as _mybir
    from concourse.bass_utils import run_bass_kernel_spmd as _run

    nc = _bacc.Bacc("TRN2", target_bir_lowering=False, num_devices=1)
    arrays, args = {}, {}
    for name in _INS:
        a = _np.asarray(inputs[name])
        a = _np.ascontiguousarray(a.T if name in _TURNED else a)
        arrays[f"in_{name}_dram"] = a
        args[name] = nc.dram_tensor(f"in_{name}_dram", a.shape, _mybir.dt.from_np(a.dtype), kind="ExternalInput").ap()
    outs = []
    for i, (shape, dtype) in enumerate(_OUTS):
        dt = _mybir.dt.from_np(_np.dtype(dtype))
        outs.append(nc.dram_tensor(f"out_{i}_dram", shape, dt, kind="ExternalOutput").ap())
    build(nc, args, outs[0])
    r = _run(nc, [arrays], core_ids=[0])
    got = tuple(r.results[0][f"out_{i}_dram"] for i in range(len(_OUTS)))
    return got[0]
```
